# Optimizing a Trainium2 kernel written in Bass

```python
import numpy as np
import jax
import jax.numpy as jnp

def _softmax(x, axis=-1):
    return jax.nn.softmax(x, axis=axis)

def _gelu(x):
    return jax.nn.gelu(x, approximate=True)

def _silu(x):
    return jax.nn.silu(x)

def _sigmoid(x):
    return jax.nn.sigmoid(x)

def _layernorm(x, axis=-1, eps=1e-05):
    m = jnp.mean(x, axis=axis, keepdims=True)
    v = jnp.var(x, axis=axis, keepdims=True)
    return (x - m) / jnp.sqrt(v + eps)

def _scatter_add(tgt, idx, src, axis=0):
    return tgt.at[idx].add(src)

def _segment_sum(src, seg, n):
    return jax.ops.segment_sum(src, seg, n)
kernel_name = 'mk_perceiver_d2_seqx_r8_1641aa'

def setup_inputs(seed: int=0):
    np.random.seed(seed)
    _w = jnp.asarray

    def _rec_inputs():
        import jax
        import jax.numpy as jnp
        _rk = jax.random.key(seed)
        x = -0.000125 + 0.9999 * jax.random.normal(jax.random.fold_in(_rk, 1), (16, 32, 128), jnp.float32)
        _lenS = 32 - jax.random.randint(jax.random.fold_in(_rk, 7), (16,), 0, max(1, 32 // 4) + 1, jnp.int32)
        _lenS2 = 512 - jax.random.randint(jax.random.fold_in(_rk, 8), (16,), 0, max(1, 512 // 4) + 1, jnp.int32)
        _ctx_768P = jax.random.normal(jax.random.fold_in(_rk, 11), (16, 16, 96), jnp.float32)
        _ctx_768c = jax.random.dirichlet(jax.random.fold_in(_rk, 511), 0.3 * jnp.ones((16,), jnp.float32), (16, 512))
        _ctx_768t = jnp.einsum('bsk,bkd->bsd', _ctx_768c, _ctx_768P)
        _ctx_768t = _ctx_768t * jax.lax.rsqrt(jnp.mean(jnp.square(_ctx_768t)) + 1e-12) * 0.953939
        ctx_768 = -7.36909e-05 + 0.999899 * (_ctx_768t + 0.3 * jax.random.normal(jax.random.fold_in(_rk, 611), (16, 512, 96), jnp.float32))
        return (x, ctx_768)
    x, ctx_768 = _rec_inputs()

    def _L0_xattn_setup():
        import jax, jax.numpy as jnp
        import numpy as np
        import math
        E = 128
        EV = 128
        FFN = 512
        DINO = 96
        B, S, P = (64, 64, 32)

        def bitnet_linear(x, W, b):
            w_scale = jnp.maximum(jnp.mean(jnp.abs(W)), 1e-05)
            qW = jnp.sign(W) * (jnp.abs(W) > 0.5 * w_scale).astype(W.dtype)
            i_scale = jnp.maximum(jnp.max(jnp.abs(x)), 1e-08) / 127.0
            qx = jnp.clip(jnp.round(x / i_scale), -128.0, 127.0)
            out = jnp.einsum('...i,oi->...o', qx, qW) * (w_scale * i_scale)
            return out + b
        key = jax.random.key(seed)
        ks = iter(jax.random.split(key, 32))

        def lin_w(fin, fout):
            return jax.random.normal(next(ks), (fout, fin), jnp.float32) * math.sqrt(2.0 / fin)
        return {'text_embeddings': jax.random.normal(next(ks), (B, S, E), jnp.float32), 'dinov2_features': jax.random.normal(next(ks), (B, P, DINO), jnp.float32), 'W_d2v': lin_w(DINO, EV), 'b_d2v': jnp.zeros((EV,), jnp.float32), 'W_img': lin_w(EV, E), 'b_img': jnp.zeros((E,), jnp.float32), 'W_txt': lin_w(E, E), 'b_txt': jnp.zeros((E,), jnp.float32), 'W_att0': lin_w(E, E // 2), 'b_att0': jnp.zeros((E // 2,), jnp.float32), 'W_att1': lin_w(E, E // 2), 'b_att1': jnp.zeros((E // 2,), jnp.float32), 'W_f1': lin_w(2 * E, FFN), 'b_f1': jnp.zeros((FFN,), jnp.float32), 'W_f2': lin_w(FFN, E), 'b_f2': jnp.zeros((E,), jnp.float32)}
    _L0_xattn_all = _L0_xattn_setup()
    _L0_xattn_in = {k: v for k, v in _L0_xattn_all.items() if k in ('W_d2v', 'b_d2v', 'W_img', 'b_img', 'W_txt', 'b_txt', 'W_att0', 'b_att0', 'W_att1', 'b_att1', 'W_f1', 'b_f1', 'W_f2', 'b_f2')}
    del _L0_xattn_all

    def _L0_attn_setup():
        import jax, jax.numpy as jnp
        import numpy as np
        D_MODEL = 128
        N_HEADS = 16
        N_GROUPS = 4
        D_K = D_MODEL // N_HEADS
        HEADS_PER_GROUP = N_HEADS // N_GROUPS

        def rope(x):
            s, d = (x.shape[1], x.shape[2])
            theta = 1.0 / 10000.0 ** (jnp.arange(d // 2, dtype=jnp.float32) / (d // 2))
            ang = jnp.arange(s, dtype=jnp.float32)[:, None] * theta[None, :]
            cos, sin = (jnp.cos(ang), jnp.sin(ang))
            xe, xo = (x[..., 0::2], x[..., 1::2])
            return jnp.concatenate([xe * cos - xo * sin, xe * sin + xo * cos], axis=-1)
        key = jax.random.key(seed)
        k1, k2, k3, k4, k5 = jax.random.split(key, 5)
        b, s = (1, 256)
        scale = 0.02
        X = jax.random.normal(k1, (b, s, D_MODEL), dtype=jnp.float32)
        W_q = jax.random.normal(k2, (D_MODEL, D_MODEL), dtype=jnp.float32) * scale
        W_k = jax.random.normal(k3, (N_GROUPS * D_K, D_MODEL), dtype=jnp.float32) * scale
        W_v = jax.random.normal(k4, (N_GROUPS * D_K, D_MODEL), dtype=jnp.float32) * scale
        W_o = jax.random.normal(k5, (D_MODEL, D_MODEL), dtype=jnp.float32) * scale
        return {'X': X, 'W_q': W_q, 'W_k': W_k, 'W_v': W_v, 'W_o': W_o}
    _L0_attn_all = _L0_attn_setup()
    _L0_attn_in = {k: v for k, v in _L0_attn_all.items() if k in ('W_q', 'W_k', 'W_v', 'W_o')}
    del _L0_attn_all

    def _L0_ffn_setup():
        import jax, jax.numpy as jnp
        import numpy as np
        B, S, H, F, E = (8, 256, 128, 512, 8)
        INIT_LAMBDA = 0.2
        key = jax.random.key(seed)
        ks = jax.random.split(key, 12)
        std = 0.02
        return {'hidden_states': jax.random.normal(ks[0], (B, S, H), jnp.float32), 'gate_w1': jax.random.normal(ks[1], (H, H), jnp.float32) * 0.01, 'gate_b1': jnp.zeros((H,), jnp.float32), 'gate_w2': jax.random.normal(ks[2], (E, H), jnp.float32) * 0.01, 'gate_b2': jnp.full((E,), INIT_LAMBDA, jnp.float32), 'W1': jax.random.normal(ks[3], (F, H), jnp.float32) * std, 'b1': jax.random.normal(ks[4], (F,), jnp.float32) * std, 'W2': jax.random.normal(ks[5], (H, F), jnp.float32) * std, 'b2': jax.random.normal(ks[6], (H,), jnp.float32) * std, 'TW1': jax.random.normal(ks[7], (E, F, H), jnp.float32) * std, 'Tb1': jax.random.normal(ks[8], (E, F), jnp.float32) * std, 'TW2': jax.random.normal(ks[9], (E, H, F), jnp.float32) * std, 'Tb2': jax.random.normal(ks[10], (E, H), jnp.float32) * std}
    _L0_ffn_all = _L0_ffn_setup()
    _L0_ffn_in = {k: v for k, v in _L0_ffn_all.items() if k in ('gate_w1', 'gate_b1', 'gate_w2', 'gate_b2', 'W1', 'b1', 'W2', 'b2', 'TW1', 'Tb1', 'TW2', 'Tb2')}
    del _L0_ffn_all

    def _L1_xattn_setup():
        import jax, jax.numpy as jnp
        import numpy as np
        NUM_HEADS = 16
        CLAMP = 10000.0
        key = jax.random.key(seed)
        ks = jax.random.split(key, 8)
        B, Nq, Nkv, Cq, Ckv = (4, 256, 256, 128, 96)
        s_q = 1.0 / np.sqrt(Cq)
        s_kv = 1.0 / np.sqrt(Ckv)
        return {'query': jax.random.normal(ks[0], (B, Nq, Cq), jnp.float32), 'key_value': jax.random.normal(ks[1], (B, Nkv, Ckv), jnp.float32), 'Wq': jax.random.normal(ks[2], (Cq, Cq), jnp.float32) * s_q, 'bq': jnp.zeros((Cq,), jnp.float32), 'Wk': jax.random.normal(ks[3], (Ckv, Cq), jnp.float32) * s_kv, 'bk': jnp.zeros((Cq,), jnp.float32), 'Wv': jax.random.normal(ks[4], (Ckv, Cq), jnp.float32) * s_kv, 'bv': jnp.zeros((Cq,), jnp.float32), 'Wo': jax.random.normal(ks[5], (Cq, Cq), jnp.float32) * s_q, 'bo': jnp.zeros((Cq,), jnp.float32)}
    _L1_xattn_all = _L1_xattn_setup()
    _L1_xattn_in = {k: v for k, v in _L1_xattn_all.items() if k in ('Wq', 'bq', 'Wk', 'bk', 'Wv', 'bv', 'Wo', 'bo')}
    del _L1_xattn_all

    def _L1_attn_setup():
        import jax, jax.numpy as jnp
        import numpy as np
        B, S, D = (4, 256, 128)
        H = 16
        HS = D // H
        SCALE = HS ** 0.5
        key = jax.random.key(seed)
        ks = jax.random.split(key, 9)
        std = 1.0 / np.sqrt(D)

        def lin(kw, kb, fan_in, fan_out):
            w = jax.random.uniform(kw, (fan_in, fan_out), minval=-std, maxval=std, dtype=jnp.float32)
            b = jax.random.uniform(kb, (fan_out,), minval=-std, maxval=std, dtype=jnp.float32)
            return (w, b)
        Wq, bq = lin(ks[0], ks[1], D, D)
        Wk, bk = lin(ks[2], ks[3], D, D)
        Wv, bv = lin(ks[4], ks[5], D, D)
        Wm, bm = lin(ks[6], ks[7], D, D)
        x = jax.random.normal(ks[8], (B, S, D), dtype=jnp.float32)
        return {'x': x, 'Wq': Wq, 'bq': bq, 'Wk': Wk, 'bk': bk, 'Wv': Wv, 'bv': bv, 'Wm': Wm, 'bm': bm}
    _L1_attn_all = _L1_attn_setup()
    _L1_attn_in = {k: v for k, v in _L1_attn_all.items() if k in ('Wq', 'bq', 'Wk', 'bk', 'Wv', 'bv', 'Wm', 'bm')}
    del _L1_attn_all

    def _L1_ffn_setup():
        import jax, jax.numpy as jnp
        import numpy as np
        B, N, D = (4, 256, 128)
        SPARSITY = 0.01
        key = jax.random.key(seed)
        k1, k2, k3 = jax.random.split(key, 3)
        x = jax.random.normal(k1, (B, N, D), dtype=jnp.float32)
        spatial = jax.random.normal(k2, (D, D), dtype=jnp.float32) * 0.02
        freq = jnp.fft.fft(spatial, axis=-1)
        k = int(D * SPARSITY)
        mag = jnp.abs(freq)
        kth = jax.lax.top_k(mag, k)[0][:, -1:]
        w_sparse = jnp.where(mag >= kth, freq, 0.0 + 0j)
        bias = jax.random.normal(k3, (D,), dtype=jnp.float32) * 0.01
        return {'x': x, 'w_freq_real': jnp.real(w_sparse).astype(jnp.float32), 'w_freq_imag': jnp.imag(w_sparse).astype(jnp.float32), 'bias': bias}
    _L1_ffn_all = _L1_ffn_setup()
    _L1_ffn_in = {k: v for k, v in _L1_ffn_all.items() if k in ('w_freq_real', 'w_freq_imag', 'bias')}
    del _L1_ffn_all
    return {'x': x, 'ctx_768': ctx_768, 'L0_xattn_W_d2v': _L0_xattn_in['W_d2v'], 'L0_xattn_b_d2v': _L0_xattn_in['b_d2v'], 'L0_xattn_W_img': _L0_xattn_in['W_img'], 'L0_xattn_b_img': _L0_xattn_in['b_img'], 'L0_xattn_W_txt': _L0_xattn_in['W_txt'], 'L0_xattn_b_txt': _L0_xattn_in['b_txt'], 'L0_xattn_W_att0': _L0_xattn_in['W_att0'], 'L0_xattn_b_att0': _L0_xattn_in['b_att0'], 'L0_xattn_W_att1': _L0_xattn_in['W_att1'], 'L0_xattn_b_att1': _L0_xattn_in['b_att1'], 'L0_xattn_W_f1': _L0_xattn_in['W_f1'], 'L0_xattn_b_f1': _L0_xattn_in['b_f1'], 'L0_xattn_W_f2': _L0_xattn_in['W_f2'], 'L0_xattn_b_f2': _L0_xattn_in['b_f2'], 'L0_attn_W_q': _L0_attn_in['W_q'], 'L0_attn_W_k': _L0_attn_in['W_k'], 'L0_attn_W_v': _L0_attn_in['W_v'], 'L0_attn_W_o': _L0_attn_in['W_o'], 'L0_ffn_gate_w1': _L0_ffn_in['gate_w1'], 'L0_ffn_gate_b1': _L0_ffn_in['gate_b1'], 'L0_ffn_gate_w2': _L0_ffn_in['gate_w2'], 'L0_ffn_gate_b2': _L0_ffn_in['gate_b2'], 'L0_ffn_W1': _L0_ffn_in['W1'], 'L0_ffn_b1': _L0_ffn_in['b1'], 'L0_ffn_W2': _L0_ffn_in['W2'], 'L0_ffn_b2': _L0_ffn_in['b2'], 'L0_ffn_TW1': _L0_ffn_in['TW1'], 'L0_ffn_Tb1': _L0_ffn_in['Tb1'], 'L0_ffn_TW2': _L0_ffn_in['TW2'], 'L0_ffn_Tb2': _L0_ffn_in['Tb2'], 'L1_xattn_Wq': _L1_xattn_in['Wq'], 'L1_xattn_bq': _L1_xattn_in['bq'], 'L1_xattn_Wk': _L1_xattn_in['Wk'], 'L1_xattn_bk': _L1_xattn_in['bk'], 'L1_xattn_Wv': _L1_xattn_in['Wv'], 'L1_xattn_bv': _L1_xattn_in['bv'], 'L1_xattn_Wo': _L1_xattn_in['Wo'], 'L1_xattn_bo': _L1_xattn_in['bo'], 'L1_attn_Wq': _L1_attn_in['Wq'], 'L1_attn_bq': _L1_attn_in['bq'], 'L1_attn_Wk': _L1_attn_in['Wk'], 'L1_attn_bk': _L1_attn_in['bk'], 'L1_attn_Wv': _L1_attn_in['Wv'], 'L1_attn_bv': _L1_attn_in['bv'], 'L1_attn_Wm': _L1_attn_in['Wm'], 'L1_attn_bm': _L1_attn_in['bm'], 'L1_ffn_w_freq_real': _L1_ffn_in['w_freq_real'], 'L1_ffn_w_freq_imag': _L1_ffn_in['w_freq_imag'], 'L1_ffn_bias': _L1_ffn_in['bias']}

def reference(x, ctx_768, L0_xattn_W_d2v, L0_xattn_b_d2v, L0_xattn_W_img, L0_xattn_b_img, L0_xattn_W_txt, L0_xattn_b_txt, L0_xattn_W_att0, L0_xattn_b_att0, L0_xattn_W_att1, L0_xattn_b_att1, L0_xattn_W_f1, L0_xattn_b_f1, L0_xattn_W_f2, L0_xattn_b_f2, L0_attn_W_q, L0_attn_W_k, L0_attn_W_v, L0_attn_W_o, L0_ffn_gate_w1, L0_ffn_gate_b1, L0_ffn_gate_w2, L0_ffn_gate_b2, L0_ffn_W1, L0_ffn_b1, L0_ffn_W2, L0_ffn_b2, L0_ffn_TW1, L0_ffn_Tb1, L0_ffn_TW2, L0_ffn_Tb2, L1_xattn_Wq, L1_xattn_bq, L1_xattn_Wk, L1_xattn_bk, L1_xattn_Wv, L1_xattn_bv, L1_xattn_Wo, L1_xattn_bo, L1_attn_Wq, L1_attn_bq, L1_attn_Wk, L1_attn_bk, L1_attn_Wv, L1_attn_bv, L1_attn_Wm, L1_attn_bm, L1_ffn_w_freq_real, L1_ffn_w_freq_imag, L1_ffn_bias):
    import jax
    import jax.numpy as jnp

    def _L0_xattn_ref(text_embeddings, dinov2_features, W_d2v, b_d2v, W_img, b_img, W_txt, b_txt, W_att0, b_att0, W_att1, b_att1, W_f1, b_f1, W_f2, b_f2):
        import jax, jax.numpy as jnp
        import numpy as np
        import math
        E = 128
        EV = 128
        FFN = 512
        DINO = 96
        B, S, P = (64, 64, 32)

        def bitnet_linear(x, W, b):
            w_scale = jnp.maximum(jnp.mean(jnp.abs(W)), 1e-05)
            qW = jnp.sign(W) * (jnp.abs(W) > 0.5 * w_scale).astype(W.dtype)
            i_scale = jnp.maximum(jnp.max(jnp.abs(x)), 1e-08) / 127.0
            qx = jnp.clip(jnp.round(x / i_scale), -128.0, 127.0)
            out = jnp.einsum('...i,oi->...o', qx, qW) * (w_scale * i_scale)
            return out + b
        b, s, e = text_embeddings.shape
        vis = bitnet_linear(dinov2_features, W_d2v, b_d2v)
        image_embeds = bitnet_linear(vis, W_img, b_img)
        fused = bitnet_linear(text_embeddings, W_txt, b_txt)
        inv_sqrt_e = 1.0 / math.sqrt(e)
        for Wa, ba in ((W_att0, b_att0), (W_att1, b_att1)):
            kv = bitnet_linear(image_embeds, Wa, ba)
            k = jnp.concatenate([kv, kv], axis=-1)
            scores = jnp.einsum('bse,bpe->bsp', fused, k) * inv_sqrt_e
            attn = jax.nn.softmax(scores, axis=-1)
            fused = fused + 0.1 * jnp.einsum('bsp,bpe->bse', attn, k)
        avg_img = jnp.mean(image_embeds, axis=1, keepdims=True)
        concatenated = jnp.concatenate([fused, jnp.broadcast_to(avg_img, (b, s, e))], axis=-1)
        h = jax.nn.relu(bitnet_linear(concatenated, W_f1, b_f1))
        return bitnet_linear(h, W_f2, b_f2)

    def _L0_attn_ref(X, W_q, W_k, W_v, W_o):
        import jax, jax.numpy as jnp
        import numpy as np
        D_MODEL = 128
        N_HEADS = 16
        N_GROUPS = 4
        D_K = D_MODEL // N_HEADS
        HEADS_PER_GROUP = N_HEADS // N_GROUPS

        def rope(x):
            s, d = (x.shape[1], x.shape[2])
            theta = 1.0 / 10000.0 ** (jnp.arange(d // 2, dtype=jnp.float32) / (d // 2))
            ang = jnp.arange(s, dtype=jnp.float32)[:, None] * theta[None, :]
            cos, sin = (jnp.cos(ang), jnp.sin(ang))
            xe, xo = (x[..., 0::2], x[..., 1::2])
            return jnp.concatenate([xe * cos - xo * sin, xe * sin + xo * cos], axis=-1)
        b, s, _ = X.shape
        Xr = rope(X)
        Q = (Xr @ W_q.T).reshape(b, s, N_HEADS, D_K).transpose(0, 2, 1, 3)
        K = (Xr @ W_k.T).reshape(b, s, N_GROUPS, D_K).transpose(0, 2, 1, 3)
        V = (Xr @ W_v.T).reshape(b, s, N_GROUPS, D_K).transpose(0, 2, 1, 3)
        Q = Q.reshape(b, N_GROUPS, HEADS_PER_GROUP, s, D_K)
        scores = jnp.einsum('bghsd,bgtd->bghst', Q, K) / jnp.sqrt(jnp.float32(D_K))
        mask = jnp.triu(jnp.ones((s, s), dtype=scores.dtype), k=1) * -1000000000.0
        attn = jax.nn.softmax(scores + mask, axis=-1)
        out = jnp.einsum('bghst,bgtd->bghsd', attn, V)
        out = out.reshape(b, N_HEADS, s, D_K).transpose(0, 2, 1, 3).reshape(b, s, D_MODEL)
        return out @ W_o.T

    def _L0_ffn_ref(hidden_states, gate_w1, gate_b1, gate_w2, gate_b2, W1, b1, W2, b2, TW1, Tb1, TW2, Tb2):
        import jax, jax.numpy as jnp
        import numpy as np
        B, S, H, F, E = (8, 256, 128, 512, 8)
        INIT_LAMBDA = 0.2
        x = hidden_states
        h = jax.nn.relu(jnp.einsum('bsh,oh->bso', x, gate_w1) + gate_b1)
        g = jnp.einsum('bso,eo->bse', h, gate_w2) + gate_b2
        g = g.mean(axis=1)
        mW1 = W1 + jnp.einsum('be,efh->bfh', g, TW1)
        mb1 = b1 + g @ Tb1
        mW2 = W2 + jnp.einsum('be,ehf->bhf', g, TW2)
        mb2 = b2 + g @ Tb2
        u = jax.nn.gelu(jnp.einsum('bsh,bfh->bsf', x, mW1) + mb1[:, None, :])
        out = jnp.einsum('bsf,bhf->bsh', u, mW2) + mb2[:, None, :]
        return out

    def _L1_xattn_ref(query, key_value, Wq, bq, Wk, bk, Wv, bv, Wo, bo):
        import jax, jax.numpy as jnp
        import numpy as np
        NUM_HEADS = 16
        CLAMP = 10000.0
        B, Nq, Cq = query.shape
        Nkv = key_value.shape[1]
        H = NUM_HEADS
        D = Cq // H
        scale = D ** (-0.5)
        q = (query @ Wq + bq).reshape(B, Nq, H, D).transpose(0, 2, 1, 3)
        k = (key_value @ Wk + bk).reshape(B, Nkv, H, D).transpose(0, 2, 1, 3)
        v = (key_value @ Wv + bv).reshape(B, Nkv, H, D).transpose(0, 2, 1, 3)
        attn = jnp.einsum('bhqd,bhkd->bhqk', q, k) * scale
        attn = jnp.clip(attn, -CLAMP, CLAMP)
        attn = jax.nn.softmax(attn, axis=-1)
        attn = jnp.where(jnp.any(jnp.isnan(attn)), jnp.asarray(1.0 / Nkv, attn.dtype), attn)
        x = jnp.einsum('bhqk,bhkd->bqhd', attn, v).reshape(B, Nq, Cq)
        return x @ Wo + bo

    def _L1_attn_ref(x, Wq, bq, Wk, bk, Wv, bv, Wm, bm):
        import jax, jax.numpy as jnp
        import numpy as np
        B, S, D = (4, 256, 128)
        H = 16
        HS = D // H
        SCALE = HS ** 0.5
        bs, seq, _ = x.shape

        def heads(w, b):
            return (x @ w + b).reshape(bs, seq, H, HS).transpose(0, 2, 1, 3)
        q = heads(Wq, bq)
        k = heads(Wk, bk)
        v = heads(Wv, bv)
        scores = jnp.einsum('bhqd,bhkd->bhqk', q, k) / SCALE
        causal_mask = jnp.arange(seq)[None, :] > jnp.arange(seq)[:, None]
        scores = jnp.where(causal_mask, jnp.float32(-1000000000000.0), scores)
        probs = jax.nn.softmax(scores, axis=-1)
        attn = jnp.einsum('bhqk,bhkd->bhqd', probs, v)
        attn = attn.transpose(0, 2, 1, 3).reshape(bs, seq, H * HS)
        return attn @ Wm + bm

    def _L1_ffn_ref(x, w_freq_real, w_freq_imag, bias):
        import jax, jax.numpy as jnp
        import numpy as np
        B, N, D = (4, 256, 128)
        SPARSITY = 0.01
        w = jax.lax.complex(w_freq_real, w_freq_imag)
        x_freq = jnp.fft.fft(x, axis=-1)
        y_freq = jnp.einsum('bnd,do->bno', x_freq, w)
        y = jnp.real(jnp.fft.ifft(y_freq, axis=-1))
        return y + bias
    x = x + _L0_xattn_ref(_layernorm(x, axis=-1), ctx_768, L0_xattn_W_d2v, L0_xattn_b_d2v, L0_xattn_W_img, L0_xattn_b_img, L0_xattn_W_txt, L0_xattn_b_txt, L0_xattn_W_att0, L0_xattn_b_att0, L0_xattn_W_att1, L0_xattn_b_att1, L0_xattn_W_f1, L0_xattn_b_f1, L0_xattn_W_f2, L0_xattn_b_f2)
    x = x + _L0_attn_ref(_layernorm(x, axis=-1), L0_attn_W_q, L0_attn_W_k, L0_attn_W_v, L0_attn_W_o)
    x = x + _L0_ffn_ref(_layernorm(x, axis=-1), L0_ffn_gate_w1, L0_ffn_gate_b1, L0_ffn_gate_w2, L0_ffn_gate_b2, L0_ffn_W1, L0_ffn_b1, L0_ffn_W2, L0_ffn_b2, L0_ffn_TW1, L0_ffn_Tb1, L0_ffn_TW2, L0_ffn_Tb2)
    x = x + _L1_xattn_ref(_layernorm(x, axis=-1), ctx_768, L1_xattn_Wq, L1_xattn_bq, L1_xattn_Wk, L1_xattn_bk, L1_xattn_Wv, L1_xattn_bv, L1_xattn_Wo, L1_xattn_bo)
    x = x + _L1_attn_ref(_layernorm(x, axis=-1), L1_attn_Wq, L1_attn_bq, L1_attn_Wk, L1_attn_bk, L1_attn_Wv, L1_attn_bv, L1_attn_Wm, L1_attn_bm)
    x = x + _L1_ffn_ref(_layernorm(x, axis=-1), L1_ffn_w_freq_real, L1_ffn_w_freq_imag, L1_ffn_bias)
    return x

_drawn_inputs = setup_inputs


def setup_inputs(seed=0):
    import zlib

    import numpy as np

    out = dict(_drawn_inputs(seed))
    spreads = {'L0_xattn_b_d2v': (0.0, 0.1),
     'L0_xattn_b_img': (0.0, 0.1),
     'L0_xattn_b_txt': (0.0, 0.1),
     'L0_xattn_b_att0': (0.0, 0.8),
     'L0_xattn_b_att1': (0.0, 0.8),
     'L0_xattn_b_f1': (0.0, 0.1),
     'L0_xattn_b_f2': (0.0, 0.1),
     'L0_ffn_gate_b1': (0.0, 0.8),
     'L0_ffn_gate_b2': (0.20000000298023224, 0.6),
     'L1_xattn_bq': (0.0, 0.456),
     'L1_xattn_bk': (0.0, 0.8),
     'L1_xattn_bv': (0.0, 0.1),
     'L1_xattn_bo': (0.0, 0.1)}
    factors = {'L0_xattn_W_att0': 3.233,
     'L0_xattn_W_att1': 3.143,
     'L0_attn_W_q': 8.0,
     'L0_attn_W_k': 8.0,
     'L0_attn_W_v': 2.97,
     'L0_attn_W_o': 2.833,
     'L0_ffn_gate_w1': 8.0,
     'L0_ffn_gate_w2': 8.0,
     'L0_ffn_b1': 8.0,
     'L0_ffn_b2': 3.203,
     'L0_ffn_Tb1': 8.0,
     'L0_ffn_Tb2': 6.849,
     'L1_attn_Wq': 3.062,
     'L1_attn_bq': 8.0,
     'L1_attn_Wk': 3.054,
     'L1_attn_bk': 8.0,
     'L1_ffn_bias': 7.719}
    for name, (base, spread) in spreads.items():
        noise = np.random.default_rng([zlib.crc32(name.encode()), seed]).standard_normal(out[name].shape)
        drawn = base * np.exp(spread * noise) if base else spread * noise
        out[name] = jnp.asarray(drawn.astype(out[name].dtype))
    for name, factor in factors.items():
        out[name] = (out[name] * factor).astype(out[name].dtype)
    return out
```

```python
import numpy as np
import concourse.bass as bass
from concourse import mybir
from contextlib import ExitStack

B, S, D = 16, 32, 128
P, DC = 512, 96
N = B * S
T = N // 128
CP = B * P
NCH = CP // 512
FF = 512
FC = FF // 128
E = 8
E1 = E + 1
H, HD = 16, 8
R = 4
LN_EPS = 1e-5
HEAD_SCALE = float(HD) ** -0.5
OFFSET = 1152.0
MAGIC = 1.5 * 2.0 ** 23 + 0x6400 + 128
ROUND = 1.5 * 2.0 ** 23
F16_TOP = 2048.0
CLIP = 10000.0

X_COLS = {"d2v": (0, 128), "img": (128, 128), "txt": (256, 128), "att0": (384, 64),
          "att1": (448, 64), "f1": (512, 1024), "f2": (1536, 512)}
X_COUNT = [DC * D, D * D, D * D, D * 64, D * 64, 2 * D * FF, FF * D]
A_NAMES = ["q0", "k0", "v0", "o0", "gate1", "wo", "q1", "k1", "v1", "m1", "wr", "wi", "wk", "wv"]
A_COL = {n: 128 * i for i, n in enumerate(A_NAMES)}
A_WQR = 128 * len(A_NAMES)
A_G2 = A_WQR + 512
A_END = A_G2 + E
C_ID, C_COS, C_SIN = 0, 128, 192
C_HM, C_RM, C_MK0, C_MK1 = 256, 260, 264, 392
C_DC, C_DS, C_DCN, C_DSN, C_CNT = 520, 648, 776, 904, 1032
C_END = 1040
K_D2V, K_IMG, K_ATT, K_F1, K_G1, K_Z = 0, 1, 2, 3, 7, 8
K_BK, K_BV, K_BQR = 9, 10, 11
K_Q1, K_K1, K_V1 = 15, 16, 17
K_B1, K_TB1 = 18, 22
K_END = K_TB1 + FC * E
R_TXT, R_A0, R_A1, R_F2, R_BO, R_BM, R_FB, R_B2, R_G2 = (128 * i for i in range(9))
R_BQ = R_G2 + E
R_END = R_BQ + 128
Y_BANK = ((6, 7, 0), (1, 2, 3))


def perceiver(nc, x_in, ctx_in, wx_in, wa_in, w1_in, w2_in, const_in, cols_in, rows_in, out):
    f32, bf16, f16 = mybir.dt.float32, mybir.dt.bfloat16, mybir.dt.float16
    ALU, ACT, AX = mybir.AluOpType, mybir.ActivationFunctionType, mybir.AxisListType.X
    ctx = ExitStack()
    with ctx:
        def sb(name, shape, dt=f32):
            return ctx.enter_context(nc.sbuf_tensor(name, shape, dt))

        def sem(name):
            return ctx.enter_context(nc.semaphore(name))

        cx = sb("cx", [128, CP])
        yq = sb("yq", [128, CP])
        big = sb("big", [128, 2, CP])
        w1 = sb("w1", [128, E1 * FF])
        wa = sb("wa", [128, A_END])
        sa = sb("sa", [128, 2048 + B * R * 36])
        tern = sb("tern", [128, 2048], bf16)
        cst = sb("cst", [128, C_END])
        cols = sb("cols", [128, K_END])
        rows = sb("rows", [128, R_END])
        ones = sb("ones", [128, 128])
        identb = sb("identb", [128, 128], bf16)
        maskb = sb("maskb", [128, 2, 128], bf16)
        noff = sb("noff", [128, 128], bf16)
        x = sb("x", [128, T, D])
        xn = sb("xn", [128, T, D])
        tmp = sb("tmp", [128, T, D])
        fused = sb("fused", [128, T, D])
        xT = sb("xT", [128, N])
        qTs = sb("qTs", [128, N])
        bn = sb("bn", [128, T, 6])
        mv = sb("mv", [128, T, 2])
        veps = sb("veps", [128, T])
        rstd = sb("rstd", [128, T])
        mhalf = sb("mhalf", [128, T])
        sm = sb("sm", [128, 464])
        diag = sb("diag", [128, 128])
        avg = sb("avg", [128, B])
        avgq = sb("avgq", [128, B])
        avgb = sb("avgb", [128, B], bf16)
        qb = sb("qb", [128, T, D], bf16)
        qT = sb("qT", [128, N], bf16)
        csum = sb("csum", [128, B])
        meanv = sb("meanv", [128, B])
        flags = sb("flags", [128, 2], mybir.dt.int32)
        gbc = sb("gbc", [128, E, B])
        gtok = sb("gtok", [128, T, E])
        mb1 = sb("mb1", [128, FC, B])
        mix = sb("mix", [128, 512])
        lin = sb("lin", [128, 128])
        ft = sb("ft", [128, 2, 128])
        PS = ctx.enter_context(nc.psum_tensor("PS", [128, 8, 512], f32))

        wx = sa[:, 0:2048]
        kexp = sa[:, 0:2048].rearrange("p (h n) -> p h n", h=4)
        vexp = sa[:, 2048:].rearrange("p (b r c) -> p b r c", b=B, r=R)
        zz = sa[:, 0:E * N].rearrange("p (e n) -> p e n", e=E)
        work = w1[:, FF:FF + 2048].rearrange("p (r n) -> p r n", r=4)
        wt = w1[:, FF + 2048:FF + 4096].rearrange("p (r n) -> p r n", r=4)
        xrep = w1[:, FF + 2048:FF + 4096]
        lt = w1[:, FF:FF + 4096].rearrange("p (r n) -> p r n", r=8)
        w2 = yq[:, 0:FC * E1 * D].rearrange("p (c e d) -> p c e d", c=FC, e=E1)
        u = yq[:, FC * E1 * D:FC * E1 * D + FC * N].rearrange("p (c n) -> p c n", c=FC)
        qe = yq[:, 0:4096].bitcast(f16).rearrange("p (r b n) -> p r b n", r=R, b=B)
        lp = yq[:, 4096:8192].rearrange("p (s n) -> p s n", s=8)
        tb2 = tern[:, :].bitcast(f32)
        qs16 = tern[:, :].bitcast(f16).rearrange("p (r n) -> p r n", r=R)
        y16 = yq[:, :].bitcast(f16).rearrange("p (n two) -> p n two", two=2)[:, :, 0]
        khl = yq[:, :].bitcast(f16).rearrange("p (two n) -> p two n", two=2)
        kst = big[:, :, :].rearrange("p a n -> p (a n)").bitcast(f16).rearrange("p (r n) -> p r n", r=R)
        ident = cst[:, C_ID:C_ID + 128]
        hm = cst[:, C_HM:C_HM + 4]
        rm = cst[:, C_RM:C_RM + 4]

        M_V, M_G, M_SI, M_INV = 0, 20, 30, 40
        M_ABS, M_WS, M_TH, M_NTH = 50, 58, 66, 74
        M_SC = 82
        M_NMX, M_DEN, M_RD = 96, 104, 112
        M_KB, M_Z4, M_RD64 = 120, 124, 128
        M_AL, M_BE, M_ES, M_BKS, M_BQS, M_QB = 192, 193, 194, 195, 196, 200
        M_ABC = 204
        M_MX = 208
        M_HM = 224
        M_MAG, M_WA = 250, 251
        M_SAM = 256
        M_BND = 320
        M_LO, M_HI = M_BND + 6, M_BND + 7
        M_NAN = 336

        L_BANK = (0, 1, 2, 7)

        def on_act(i):
            return i % 4 == 3 or i % 8 == 5

        def n_act(i):
            return sum(on_act(j) for j in range(i))

        def n_dve(i):
            return i - n_act(i)

        def s1(i, n=1):
            return sm[:, i:i + n]

        KEYS_AFTER_ROUND = (((2, 2), (3, 3)), ((6, 4), (7, 5), (8, 2), (9, 3)))
        KEYS_IN_FF = ((10, 4), (11, 6), (12, 0), (13, 1), (14, 2), (15, 3))
        VALUES = (tuple((c, c % 4) for c in range(8)), tuple((c, 2 + c % 4) for c in range(8, 11)),
                  (), tuple((c, 4 + c % 2) for c in range(11, 16)))

        def col(i, n=1):
            return cols[:, i:i + n]

        def row(i, n=128):
            return rows[:, i:i + n]

        def A(name, p=128):
            return wa[0:p, A_COL[name]:A_COL[name] + 128]

        def TW(name):
            c, n = X_COLS[name]
            return tern[:, c:c + n]

        names = ["ld_x", "ld_wx", "ld_wa", "ld_w1", "ld_w2", "ld_cst", "ld_cols", "ld_rows", "ld_tb2", "kst_done",
                 "out_done", "consts", "casts", "wabs", "ws_ps", "ln_veps", "ln_rstd", "ln_out", "gm_diag", "gm_ps",
                 "ternary", "txt_q", "txt_tp", "txt_qT", "txt_ps", "fk_tok", "fk_tp", "fkT",
                 "scale_ready", "f2_scale", "vp_ev", "ft_ok", "ctx_sums", "clip_step", "flag_ok", "nan_ok", "quant_dve", "quant_act", "quant_pool", "ctx_mm", "ctx_ev",
                 "kv_mm", "kv_ev", "sc_ps", "sc_max", "sc_exp", "sc_tp", "sc_tev", "sc_teva", "pv_ps",
                 "f1_in", "f1_tp", "f1_qT", "f1_ps", "f1_ev", "f2_qd", "f2_qa", "f2_ps", "x_up",
                 "xt_ps", "xt_ev", "xrep_ok", "qk_ps", "q_ev", "k_evd", "k_eva", "v_ps", "v_ev", "vones", "sa_ps", "sa_sub", "sa_exp",
                 "sa_tp", "sa_tevd", "sa_teva", "sa_pv", "sa_o", "ot_ps", "ot_ev", "wo_ps",
                 "g_ps", "g_relu", "g_x", "g_bc_ps", "z_ready", "u_ps", "u_pre", "u_act", "y_ps", "y_used",
                 "kp_ps", "kp_h", "kp_l", "vp_ps", "bound_in", "bound_ps", "scales_ok", "root_in", "root",
                 "lq_ps", "lq_ev", "lq_e", "ls_ps", "ls_max", "ls_bias", "ls_exp", "ls_rd", "ls_nrm",
                 "lt_ps", "lt_evd", "lt_eva", "lo_ps", "lo_sum",
                 "ft_ps", "lin_ps", "lin_ok", "fin_ps", "dve_link", "act_link", "pool_link"]

        s = {n: sem(n) for n in names}
        ld_ws = [sem(f"ld_ws{e}") for e in range(1, E1)]
        ld_ctx = [sem(f"ld_ctx{i}") for i in range(8)]
        block = ctx.enter_context(nc.Block())

        def chunk(c):
            return slice(512 * c, 512 * c + 512)

        def tile(t):
            return slice(128 * t, 128 * t + 128)

        @block.sync
        def _(sp):
            sp.dma_start(x[:, :, :], x_in.rearrange("(t p) d -> p t d", p=128)).then_inc(s["ld_x"], 16)
            sp.dma_start(cst[:, :], const_in).then_inc(s["ld_cst"], 16)
            sp.dma_start(wx, wx_in).then_inc(s["ld_wx"], 16)
            sp.dma_start(cols[:, :], cols_in).then_inc(s["ld_cols"], 16)
            w = CP // 8
            for i in range(8):
                sp.dma_start(cx[0:DC + 1, i * w:(i + 1) * w], ctx_in[:, i * w:(i + 1) * w]).then_inc(ld_ctx[i], 16)
            sp.dma_start(rows[:, :], rows_in[:, 0:R_END]).then_inc(s["ld_rows"], 16)
            sp.dma_start(wa[:, :], wa_in).then_inc(s["ld_wa"], 16)
            sp.dma_start(w1[:, 0:FF], w1_in[:, 0:FF]).then_inc(s["ld_w1"], 16)
            sp.wait_ge(s["f2_ps"], 1)
            sp.dma_start(tb2, rows_in[:, R_END:R_END + E * D]).then_inc(s["ld_tb2"], 16)
            sp.wait_ge(s["pv_ps"], 2)
            sp.wait_ge(s["kp_h"], NCH)
            sp.wait_ge(s["kp_l"], NCH)
            for r in range(R):
                for part in range(4):
                    sp.dma_start(kst[32 * part:32 * part + 32, r, :],
                                 khl[32 * r:32 * r + 32, part % 2, :]).then_inc(s["kst_done"], 16)
            sp.wait_ge(s["kst_done"], 16 * 16)
            sp.dma_start(w2, w2_in.rearrange("p (c e d) -> p c e d", c=FC, e=E1)).then_inc(s["ld_w2"], 16)
            sp.wait_ge(s["sa_pv"], 1)
            for e in range(1, E1):
                sp.dma_start(w1[:, e * FF:(e + 1) * FF], w1_in[:, e * FF:(e + 1) * FF]).then_inc(ld_ws[e - 1], 16)
            sp.wait_ge(s["x_up"], 6)
            sp.dma_start(out.rearrange("(t p) d -> p t d", p=128), x[:, :, :]).then_inc(s["out_done"], 16)
            sp.wait_ge(s["out_done"], 16)

        @block.gpsimd
        def _(pool):
            links = [0]

            def link(ins):
                links[0] += 1
                ins.then_inc(s["pool_link"], 1)
                pool.wait_ge(s["pool_link"], links[0])

            pool.memset(mhalf[:, :], -0.5)
            link(pool.memset(sm[:, :], 0.0))
            pool.memset(s1(M_MAG), MAGIC)
            pool.memset(s1(M_QB + 2), 0.5)
            pool.memset(noff[:, :], -OFFSET)
            pool.memset(ones[:, :], 1.0).then_inc(s["consts"], 1)
            pool.wait_ge(s["ld_cst"], 16)
            pool.tensor_copy(identb[:, :], ident)
            pool.tensor_copy(maskb[:, :, :], cst[:, C_MK0:C_MK0 + 256].rearrange("p (a b) -> p a b", a=2))\
                .then_inc(s["casts"], 1)

            def rstd_of(n):
                pool.wait_ge(s["ln_veps"], n + 1)
                pool.tensor_tensor(rstd[:, :], veps[:, :], mhalf[:, :], ALU.pow).then_inc(s["ln_rstd"], 1)

            def quantise(layer, src, pn):
                pool.wait_ge(s["scale_ready"], layer + 1)
                for c in range(1, NCH, 4):
                    pool.tensor_scalar(yq[0:pn, chunk(c)], src[0:pn, chunk(c)], sm[0:pn, M_INV + layer:M_INV + layer + 1],
                                       MAGIC, ALU.mult, ALU.add).then_inc(s["quant_pool"], 1)

            def value_ones(k):
                for b in range(B):
                    last = pool.tensor_copy(vexp[:, b, :, 32:36], rm.unsqueeze(1).broadcast_to([128, R, 4]))
                last.then_inc(s["vones"], 1)

            rstd_of(0)
            quantise(0, cx, DC)
            quantise(1, big[:, 0, :], 128)
            quantise(2, big[:, 0, :], 128)
            pool.wait_ge(s["root_in"], 1)
            pool.tensor_tensor(s1(M_QB + 1), s1(M_QB), s1(M_QB + 2), ALU.pow).then_inc(s["root"], 1)
            value_ones(0)
            rstd_of(1)
            rstd_of(2)
            pool.wait_ge(s["u_ps"], FC)
            value_ones(1)
            rstd_of(3)

            def row_bias(i):
                pool.wait_ge(s["ls_max"], i + 1)
                if i >= 8:
                    pool.wait_ge(s["ls_exp"], i - 7)
                pool.tensor_scalar(s1(M_NMX + i % 8), s1(M_MX + i % 8), s1(M_ES), 1.0, ALU.mult, ALU.mult)\
                    .then_inc(s["ls_bias"], 1)

            def normalise(i):
                pool.tensor_scalar(lp[:, i % 8, :], lp[:, i % 8, :], s1(M_RD + i % 8), 1.0,
                                   ALU.mult, ALU.mult).then_inc(s["ls_nrm"], 1)

            for b in range(B + 1):
                for r in range(R):
                    if b < B:
                        row_bias(R * b + r)
                    if b >= 1 and r == 1:
                        pool.wait_ge(s["ls_rd"], b)
                    if b >= 1 and r >= 1:
                        normalise(R * (b - 1) + r - 1)
                if b >= 1:
                    normalise(R * (b - 1) + R - 1)
            rstd_of(4)
            rstd_of(5)

        @block.scalar
        def _(act):
            links = [0]

            def link(ins):
                links[0] += 1
                ins.then_inc(s["act_link"], 1)
                act.wait_ge(s["act_link"], links[0])

            def affine(o, i, scale=1.0, bias=0.0, func=ACT.Identity, **kw):
                return nc.scalar.activation(o, i, func, bias=bias, scale=scale, **kw)

            act.wait_ge(s["ld_wx"], 16)
            act.wait_ge(s["consts"], 1)
            for n, (c, w) in enumerate(X_COLS.values()):
                last = nc.scalar.activation(big[:, 0, c:c + w], wx[:, c:c + w], ACT.Abs, accum_out=s1(M_ABS + n))
            last.then_inc(s["wabs"], 1)

            def quantise(layer, src, pn):
                act.wait_ge(s["scale_ready"], layer + 1)
                for c in range(3, NCH, 4):
                    affine(yq[0:pn, chunk(c)], src[0:pn, chunk(c)], scale=sm[0:pn, M_INV + layer:M_INV + layer + 1],
                           bias=sm[0:pn, M_MAG:M_MAG + 1]).then_inc(s["quant_act"], 1)

            def ctx_evacuate(layer, bias, with_sum=False):
                for c in range(NCH):
                    act.wait_ge(s["ctx_mm"], NCH * layer + c + 1)
                    kw = {"accum_out": avg[:, c:c + 1]} if with_sum else {}
                    affine(big[:, 0, chunk(c)], PS[:, c % 4, :], scale=s1(M_SC + layer), bias=bias, **kw)\
                        .then_inc(s["ctx_ev"], 1)

            act.wait_ge(s["txt_tp"], 1)
            nc.scalar.copy(qT[:, :], PS[:, 6, 0:256].bitcast(bf16)).then_inc(s["txt_qT"], 1)
            for b in range(B):
                act.wait_ge(ld_ctx[b // 2], 16)
                last = affine(big[0:DC + 1, 1, chunk(b)], cx[0:DC + 1, chunk(b)], accum_out=csum[0:DC + 1, b:b + 1])
            last.then_inc(s["ctx_sums"], 1)
            act.wait_ge(s["ld_wa"], 16)
            nc.scalar.activation(mix[:, 0:128], A("wk"), ACT.Abs)
            nc.scalar.activation(mix[:, 128:256].rearrange("p (r n) -> p r n", r=R),
                                 wa[:, A_WQR:A_WQR + 512].rearrange("p (r n) -> p r n", r=R)[:, :, 0:32],
                                 ACT.Square).then_inc(s["bound_in"], 1)
            act.wait_ge(s["ft_ps"], 1)
            nc.scalar.copy(ft[:, 0, :], PS[:, 0, 0:128])
            affine(ft[:, 1, :], PS[:, 0, 128:256], scale=-1.0).then_inc(s["ft_ok"], 1)
            act.wait_ge(s["lin_ps"], 1)
            nc.scalar.copy(lin[:, :], PS[:, 1, 0:128]).then_inc(s["lin_ok"], 1)
            quantise(0, cx, DC)
            ctx_evacuate(0, col(K_D2V))
            quantise(1, big[:, 0, :], 128)
            ctx_evacuate(1, col(K_IMG), True)
            quantise(2, big[:, 0, :], 128)
            ctx_evacuate(2, col(K_ATT))

            def key_high(c, bank):
                act.wait_ge(s["kp_ps"], c + 1)
                affine(khl[:, 0, chunk(c)], PS[:, bank, :], scale=s1(M_AL)).then_inc(s["kp_h"], 1)

            act.wait_ge(s["scales_ok"], 1)
            for j in range(2):
                act.wait_ge(s["fk_tp"], j + 1)
                affine(xT[:, :], PS[:, 7, :], scale=float(D) ** -0.5).then_inc(s["fkT"], 1)
                for t in range(T):
                    act.wait_ge(s["sc_max"], T * j + t + 1)
                    if j:
                        act.wait_ge(s["sc_tp"], t + 1)
                    nc.scalar.activation(work[:, t, :], PS[:, t, :], ACT.Exp, bias=s1(M_NMX + t),
                                         accum_out=s1(M_DEN + t)).then_inc(s["sc_exp"], 1)
                for t in range(1, T, 2):
                    act.wait_ge(s["sc_tp"], T * j + t + 1)
                    nc.scalar.copy(wt[:, t, :], PS[:, 4 + t % 2, :]).then_inc(s["sc_teva"], 1)
                    key_high(4 * j + t // 2, t // 2)
                for c, bank in KEYS_AFTER_ROUND[j]:
                    key_high(c, bank)

            act.wait_ge(s["f1_tp"], 1)
            nc.scalar.copy(qT[:, :], PS[:, 6, 0:256].bitcast(bf16)).then_inc(s["f1_qT"], 1)
            for fc in range(FC):
                act.wait_ge(s["f1_ps"], fc + 1)
                affine(work[:, fc, :], PS[:, fc, :], scale=s1(M_SC + 5), bias=col(K_F1 + fc), func=ACT.Relu)\
                    .then_inc(s["f1_ev"], 1)
            for c, bank in KEYS_IN_FF[:2]:
                key_high(c, bank)
            act.wait_ge(s["f2_scale"], 1)
            for fc in (1, 3):
                affine(wt[:, fc, :], work[:, fc, :], scale=s1(M_INV + 6), bias=s1(M_MAG)).then_inc(s["f2_qa"], 1)
            for c, bank in KEYS_IN_FF[2:]:
                key_high(c, bank)

            def context_values(part):
                for c, bank in VALUES[part]:
                    act.wait_ge(s["vp_ps"], c + 1)
                    nc.scalar.copy(cx[:, chunk(c)], PS[:, bank, :]).then_inc(s["vp_ev"], 1)

            context_values(0)

            def rows_to_features(n):
                act.wait_ge(s["xt_ps"], n)
                nc.scalar.copy(xT[:, :], PS[:, 7, :]).then_inc(s["xt_ev"], 1)

            def self_attention(k):
                act.wait_ge(s["qk_ps"], 3 * k + 1)
                affine(qTs[:, :], PS[:, 4, :], bias=col(K_Q1) if k else 0.0).then_inc(s["q_ev"], 1)
                act.wait_ge(s["qk_ps"], 3 * k + 3)
                for h in (2, 3):
                    affine(kexp[:, h, :], PS[:, 3, :], scale=hm[:, h:h + 1], bias=s1((M_KB if k else M_Z4) + h))\
                        .then_inc(s["k_eva"], 1)

                def values(half):
                    act.wait_ge(s["v_ps"], 2 * k + half + 1)
                    b0 = 8 * (1 - half)
                    src = PS[:, 4 + b0 // 4:6 + b0 // 4, :].rearrange("p a (b r c) -> p (a b) r c", b=4, r=R)
                    for h in range(4):
                        affine(vexp[:, b0:b0 + 8, :, 8 * h:8 * h + 8], src[:, :, :, 8 * h:8 * h + 8],
                               scale=rm[:, h:h + 1]).then_inc(s["v_ev"], 1)

                values(0)
                for r in range(R):
                    act.wait_ge(s["sa_sub"], R * k + r + 1)
                    nc.scalar.activation(work[:, r, :], work[:, r, :], ACT.Exp, scale=HEAD_SCALE)\
                        .then_inc(s["sa_exp"], 1)
                    if r == 1:
                        values(1)
                for r in (1, 3):
                    act.wait_ge(s["sa_tp"], R * k + r + 1)
                    nc.scalar.copy(wt[:, r, :], PS[:, r, :]).then_inc(s["sa_teva"], 1)
                act.wait_ge(s["ot_ps"], k + 1)
                affine(xT[:, :], PS[:, 6, :], bias=col(K_V1) if k else 0.0).then_inc(s["ot_ev"], 1)

            rows_to_features(1)
            self_attention(0)
            context_values(1)
            rows_to_features(2)
            context_values(2)
            act.wait_ge(s["g_ps"], 1)
            affine(fused[:, :, :].rearrange("p t d -> p (t d)"), PS[:, 0, :], bias=col(K_G1), func=ACT.Relu)\
                .then_inc(s["g_relu"], 1)
            for fc in range(FC):
                act.wait_ge(s["u_pre"], fc + 1)
                nc.scalar.activation(u[:, fc, :], u[:, fc, :], ACT.Gelu_apprx_tanh).then_inc(s["u_act"], 1)
            context_values(3)
            rows_to_features(3)
            for r in range(R):
                act.wait_ge(s["lq_ps"], r + 1)
                affine(kexp[:, r, :], PS[:, r, :], scale=s1(M_BE), bias=s1(M_BQS + r)).then_inc(s["lq_ev"], 1)

            def evacuate(i):
                act.wait_ge(s["lt_ps"], i + 1)
                nc.scalar.copy(lt[:, i % 8, :], PS[:, 3 + i % 2, :]).then_inc(s["lt_eva"], 1)

            for b in range(B + 2):
                for r in range(R):
                    if b < B:
                        i = R * b + r
                        act.wait_ge(s["ls_bias"], i + 1)
                        if i >= 8:
                            act.wait_ge(s["lt_ps"], i - 7)
                            act.wait_ge(s["ls_rd"], b - 1)
                        nc.scalar.activation(lp[:, i % 8, :], PS[:, L_BANK[i % 4], :], ACT.Exp, bias=s1(M_NMX + i % 8),
                                             scale=s1(M_ES), accum_out=s1(M_DEN + i % 8)).then_inc(s["ls_exp"], 1)
                    if b >= 2 and on_act(R * (b - 2) + r):
                        evacuate(R * (b - 2) + r)
            rows_to_features(4)
            self_attention(1)
            rows_to_features(5)

        @block.vector
        def _(dve):
            V = nc.vector
            links = [0]

            def link(ins):
                links[0] += 1
                ins.then_inc(s["dve_link"], 1)
                dve.wait_ge(s["dve_link"], links[0])

            def layer_norm(n, out_tile, done=None):
                for t in range(T):
                    last = V.bn_stats(bn[:, t, :], x[:, t, :])
                link(last)
                for t in range(T):
                    last = V.bn_aggr(mv[:, t, :], bn[:, t, :])
                link(last)
                V.tensor_scalar(veps[:, :], mv[:, :, 1], LN_EPS, None, ALU.add).then_inc(s["ln_veps"], 1)
                dve.wait_ge(s["ln_rstd"], n + 1)
                for t in range(T):
                    last = V.tensor_scalar(out_tile[:, t, :], x[:, t, :], mv[:, t, 0:1], rstd[:, t:t + 1],
                                           ALU.subtract, ALU.mult)
                if done is None:
                    link(last)
                else:
                    last.then_inc(done, 1)

            n_gmax = [0]

            def global_scale(i, ncols, ws, pn=128):
                if ncols > 1:
                    link(V.tensor_reduce(s1(M_V + 18), s1(M_V, ncols), AX, ALU.max))
                v = s1(M_V + 18) if ncols > 1 else s1(M_V)
                V.tensor_scalar(diag[:, :], ident, v, None, ALU.mult).then_inc(s["gm_diag"], 1)
                n_gmax[0] += 1
                dve.wait_ge(s["gm_ps"], n_gmax[0])
                link(V.tensor_reduce(s1(M_G + i), PS[:, 7, 0:128], AX, ALU.max))
                link(V.tensor_scalar(s1(M_SI + i), s1(M_G + i), 1e-8, 1.0 / 127.0, ALU.max, ALU.mult))
                V.tensor_tensor(s1(M_SC + i), s1(ws), s1(M_SI + i), ALU.mult)
                return V.reciprocal(s1(M_INV + i), s1(M_SI + i))

            dve.wait_ge(s["ld_x"], 16)
            dve.wait_ge(s["consts"], 1)
            layer_norm(0, xn)
            link(V.tensor_reduce(s1(M_V), xn[:, :, :].rearrange("p t d -> p (t d)"), AX, ALU.max,
                                 apply_absolute_value=True))
            dve.wait_ge(s["ws_ps"], 1)
            dve.wait_ge(s["ld_cst"], 16)
            link(V.tensor_tensor(s1(M_WS, 7), PS[:, 7, 128:135], cst[:, C_CNT:C_CNT + 7], ALU.mult))
            link(V.tensor_scalar(s1(M_WS, 7), s1(M_WS, 7), 1e-5, None, ALU.max))
            V.tensor_scalar(s1(M_TH, 7), s1(M_WS, 7), 0.5, None, ALU.mult)
            V.tensor_copy(sm[0:64, M_WA:M_WA + 1], sm[0:64, M_WS + 3:M_WS + 4])
            V.tensor_copy(sm[64:128, M_WA:M_WA + 1], sm[64:128, M_WS + 4:M_WS + 5])
            link(V.tensor_scalar(s1(M_NTH, 7), s1(M_WS, 7), -0.5, None, ALU.mult))
            link(global_scale(3, 1, M_WS + 2))
            for n, (c, w) in enumerate(X_COLS.values()):
                V.tensor_scalar(tern[:, c:c + w], wx[:, c:c + w], s1(M_NTH + n), None, ALU.is_lt)
                if n == 2:
                    link(V.tensor_scalar(tmp[:, :, :], xn[:, :, :], s1(M_INV + 3), ROUND, ALU.mult, ALU.add))
                    V.tensor_scalar(qb[:, :, :], tmp[:, :, :], ROUND, None, ALU.subtract).then_inc(s["txt_q"], 1)
            link(V.tensor_copy(s1(M_BND + 15), s1(M_BND + 14)))
            for n, (c, w) in enumerate(X_COLS.values()):
                V.scalar_tensor_tensor(tern[:, c:c + w], wx[:, c:c + w], s1(M_TH + n), tern[:, c:c + w],
                                       ALU.is_gt, ALU.subtract).then_inc(s["ternary"], 1)
            dve.wait_ge(s["txt_ps"], 1)
            dve.wait_ge(s["ld_rows"], 16)
            V.scalar_tensor_tensor(fused[:, :, :], PS[:, 5, :].rearrange("p (t d) -> p t d", t=T), s1(M_SC + 3),
                                   row(R_TXT).unsqueeze(1).broadcast_to([128, T, D]), ALU.mult, ALU.add)
            link(V.memset(s1(M_V, 16), 0.0))

            for i in range(8):
                w = CP // 8
                dve.wait_ge(ld_ctx[i], 16)
                last = V.tensor_reduce(sm[0:DC, M_V + i:M_V + i + 1], cx[0:DC, i * w:(i + 1) * w], AX, ALU.max,
                                       apply_absolute_value=True)
            link(last)
            for layer in range(3):
                src, pn = (cx, DC) if layer == 0 else (big[:, 0, :], 128)
                if layer:
                    for c in range(NCH):
                        dve.wait_ge(s["ctx_ev"], NCH * (layer - 1) + c + 1)
                        last = V.tensor_reduce(s1(M_V + c), big[:, 0, chunk(c)], AX, ALU.max, apply_absolute_value=True)
                    link(last)
                last = global_scale(layer, 8 if layer == 0 else NCH, (M_WS, M_WS + 1, M_WA)[layer])
                last.then_inc(s["scale_ready"], 1)
                dve.wait_ge(s["scale_ready"], layer + 1)
                for c in range(0, NCH, 2):
                    V.tensor_scalar(yq[0:pn, chunk(c)], src[0:pn, chunk(c)], sm[0:pn, M_INV + layer:M_INV + layer + 1],
                                    MAGIC, ALU.mult, ALU.add).then_inc(s["quant_dve"], 1)
            def bound_step(n):
                if n == 0:
                    V.tensor_reduce(s1(M_BND), PS[:, 6, 0:128], AX, ALU.max)
                    V.tensor_reduce(s1(M_BND + 1), PS[:, 6, 128:256], AX, ALU.max)
                    V.tensor_scalar(s1(M_BND + 3), s1(M_G), 1.0, None, ALU.max)
                    link(V.tensor_reduce(s1(M_BND + 2), row(R_BQ), AX, ALU.max, apply_absolute_value=True))
                elif n == 1:
                    V.tensor_tensor(s1(M_BND + 4), s1(M_BND), s1(M_BND + 3), ALU.mult)
                    V.tensor_scalar(s1(M_QB), s1(M_BND + 1), float(D), None, ALU.mult).then_inc(s["root_in"], 1)
                    V.tensor_scalar(meanv[:, :], PS[:, 6, 256:256 + B], 1.0 / P, None, ALU.mult)
                    V.tensor_scalar(s1(M_KB, 4), hm, col(K_K1), None, ALU.mult)
                elif n == 2:
                    dve.wait_ge(s["root"], 1)
                    link(V.tensor_tensor(s1(M_BND + 5), s1(M_QB + 1), s1(M_BND + 2), ALU.add))
                    link(V.tensor_scalar(s1(M_BND + 4, 2), s1(M_BND + 4, 2), 1e-30, 1.0 / F16_TOP, ALU.max, ALU.mult))
                elif n == 3:
                    V.reciprocal(s1(M_AL, 2), s1(M_BND + 4, 2))
                    link(V.scalar_tensor_tensor(s1(M_ES), s1(M_BND + 4), HEAD_SCALE, s1(M_BND + 5),
                                                ALU.mult, ALU.mult))
                elif n == 4:
                    V.tensor_scalar(flags[:, 0:1], s1(M_ES), HD * F16_TOP ** 2, 0.99 * CLIP, ALU.mult, ALU.is_le)\
                        .then_inc(s["flag_ok"], 1)
                    V.tensor_scalar(s1(M_BQS, 4), col(K_BQR, 4), s1(M_BE), None, ALU.mult)
                    link(V.reciprocal(s1(M_HI), s1(M_ES)))
                elif n == 5:
                    link(V.tensor_scalar(s1(M_LO), s1(M_HI), -CLIP, None, ALU.mult))
                    V.tensor_scalar(s1(M_HI), s1(M_HI), CLIP, None, ALU.mult).then_inc(s["scales_ok"], 1)

            dve.wait_ge(s["bound_ps"], 1)
            for c in range(NCH):
                dve.wait_ge(s["kv_mm"], c + 1)
                V.tensor_copy(big[:, 1, chunk(c)], PS[:, 4 + c % 2, :]).then_inc(s["kv_ev"], 1)
                if c % 2:
                    bound_step(c // 2)

            def key_low(c, bank):
                dve.wait_ge(s["kp_h"], c + 1)
                V.scalar_tensor_tensor(khl[:, 1, chunk(c)], PS[:, bank, :], s1(M_AL), khl[:, 0, chunk(c)],
                                       ALU.mult, ALU.subtract).then_inc(s["kp_l"], 1)

            for j in range(2):
                if j:
                    V.memset(tmp[:, :, 0:64], 0.0)
                else:
                    V.memset(tmp[:, :, 64:128], 0.0)
                V.tensor_tensor(tmp[:, :, 64 * j:64 * j + 64], fused[:, :, 0:64], fused[:, :, 64:128], ALU.add)\
                    .then_inc(s["fk_tok"], 1)
                if j:
                    for c, bank in KEYS_AFTER_ROUND[0]:
                        key_low(c, bank)
                for t in range(T):
                    dve.wait_ge(s["sc_ps"], T * j + t + 1)
                    V.tensor_reduce(s1(M_NMX + t), PS[:, t, :], AX, ALU.max, negate=True).then_inc(s["sc_max"], 1)
                dve.wait_ge(s["fk_tok"], j + 1)
                V.scalar_tensor_tensor(fused[:, :, :], row(R_A0 + 128 * j).unsqueeze(1).broadcast_to([128, T, D]), 0.1,
                                       fused[:, :, :], ALU.mult, ALU.add)
                for t in range(0, T, 2):
                    dve.wait_ge(s["sc_tp"], T * j + t + 1)
                    V.tensor_copy(wt[:, t, :], PS[:, 4 + t % 2, :]).then_inc(s["sc_tev"], 1)
                key_low(4 * j, 0)
                key_low(4 * j + 1, 1)
                dve.wait_ge(s["sc_exp"], T * j + T)
                V.reciprocal(s1(M_RD, T), s1(M_DEN, T))
                link(V.tensor_tensor(s1(M_RD + 5), s1(M_WS + 3 + j), s1(M_SI + 2), ALU.mult))
                link(V.tensor_scalar(s1(M_RD, T), s1(M_RD, T), s1(M_RD + 5), 0.1, ALU.mult, ALU.mult))
                dve.wait_ge(s["pv_ps"], j + 1)
                for t in range(T):
                    last = V.scalar_tensor_tensor(fused[:, t, :], PS[:, 6, tile(t)], s1(M_RD + t), fused[:, t, :],
                                                  ALU.mult, ALU.add)
                link(last)

            V.tensor_reduce(s1(M_V), fused[:, :, :].rearrange("p t d -> p (t d)"), AX, ALU.max, apply_absolute_value=True)
            link(V.tensor_scalar(avgq[:, :], avg[:, :], 1.0 / P, None, ALU.mult))
            link(V.tensor_reduce(s1(M_V + 1), avgq[:, :], AX, ALU.max, apply_absolute_value=True))
            link(global_scale(5, 2, M_WS + 5))
            V.tensor_scalar(avgq[:, :], avgq[:, :], s1(M_INV + 5), ROUND, ALU.mult, ALU.add)
            link(V.tensor_scalar(tmp[:, :, :], fused[:, :, :], s1(M_INV + 5), ROUND, ALU.mult, ALU.add))
            V.tensor_scalar(avgb[:, :], avgq[:, :], ROUND, None, ALU.subtract)
            V.tensor_scalar(qb[:, :, :], tmp[:, :, :], ROUND, None, ALU.subtract).then_inc(s["f1_in"], 1)
            for c, bank in KEYS_AFTER_ROUND[1]:
                key_low(c, bank)
            V.tensor_tensor(x[:, :, :], x[:, :, :], row(R_F2).unsqueeze(1).broadcast_to([128, T, D]), ALU.add)
            for fc in range(FC):
                dve.wait_ge(s["f1_ev"], fc + 1)
                last = V.tensor_reduce(s1(M_V + fc), work[:, fc, :], AX, ALU.max)
            link(last)
            global_scale(6, FC, M_WS + 6).then_inc(s["f2_scale"], 1)
            dve.wait_ge(s["f2_scale"], 1)
            for fc in (0, 2):
                V.tensor_scalar(wt[:, fc, :], work[:, fc, :], s1(M_INV + 6), MAGIC, ALU.mult, ALU.add)\
                    .then_inc(s["f2_qd"], 1)
            for c, bank in KEYS_IN_FF:
                key_low(c, bank)
            dve.wait_ge(s["f2_ps"], 1)
            flat = "p t d -> p (t d)"
            V.scalar_tensor_tensor(x[:, :, :].rearrange(flat), PS[:, 5, :], s1(M_SC + 6), x[:, :, :].rearrange(flat),
                                   ALU.mult, ALU.add).then_inc(s["x_up"], 1)

            dve.wait_ge(s["x_up"], 1)
            layer_norm(1, xn)
            pair = xn[:, :, :].rearrange("p t (n two) -> p t n two", two=2)
            cos = cst[:, C_COS:C_COS + 64].unsqueeze(1).broadcast_to([128, T, 64])
            sin = cst[:, C_SIN:C_SIN + 64].unsqueeze(1).broadcast_to([128, T, 64])
            V.tensor_tensor(fused[:, :, 0:64], pair[:, :, :, 0], cos, ALU.mult)
            V.tensor_tensor(tmp[:, :, 0:64], pair[:, :, :, 1], sin, ALU.mult)
            V.tensor_tensor(fused[:, :, 64:128], pair[:, :, :, 0], sin, ALU.mult)
            link(V.tensor_tensor(tmp[:, :, 64:128], pair[:, :, :, 1], cos, ALU.mult))
            V.tensor_tensor(fused[:, :, 0:64], fused[:, :, 0:64], tmp[:, :, 0:64], ALU.subtract)
            V.tensor_tensor(fused[:, :, 64:128], fused[:, :, 64:128], tmp[:, :, 64:128], ALU.add).then_inc(s["ln_out"], 1)

            def self_attention(k):
                dve.wait_ge(s["xt_ev"], (1, 4)[k])
                V.tensor_copy(xrep.rearrange("p (b h q) -> p b h q", b=B, h=4),
                              xT[:, :].rearrange("p (b q) -> p b q", q=S).unsqueeze(2).broadcast_to([128, B, 4, S]))\
                    .then_inc(s["xrep_ok"], 1)
                dve.wait_ge(s["qk_ps"], 3 * k + 2)
                for h in (0, 1):
                    V.tensor_scalar(kexp[:, h, :], PS[:, 5, :], col(K_K1) if k else s1(M_Z4), hm[:, h:h + 1],
                                    ALU.add, ALU.mult).then_inc(s["k_evd"], 1)
                for r in range(R):
                    dve.wait_ge(s["sa_ps"], R * k + r + 1)
                    mx = s1(M_SAM + 16 * r, 16)
                    sc = PS[:, r, :].rearrange("p (g n) -> p g n", n=S)
                    link(V.tensor_reduce(mx, sc, AX, ALU.max))
                    V.tensor_tensor(work[:, r, :].rearrange("p (g n) -> p g n", n=S), sc,
                                    mx.unsqueeze(2).broadcast_to([128, 16, S]), ALU.subtract).then_inc(s["sa_sub"], 1)
                for r in (0, 2):
                    dve.wait_ge(s["sa_tp"], R * k + r + 1)
                    V.tensor_copy(wt[:, r, :], PS[:, r, :]).then_inc(s["sa_tevd"], 1)
                dve.wait_ge(s["sa_pv"], k + 1)
                pv = [PS[:, 4 + a, 0:288].rearrange("p (g c) -> p g c", c=36) for a in range(2)]
                for a in range(2):
                    last = V.reciprocal(s1(M_RD64 + 32 * a, 32).rearrange("p (g h) -> p g h", h=4), pv[a][:, :, 32:36])
                link(last)
                for a in range(2):
                    rd = s1(M_RD64 + 32 * a, 32).rearrange("p (g h) -> p g h", h=4).unsqueeze(3)\
                        .broadcast_to([128, 8, 4, HD])
                    last = V.tensor_tensor(tmp[:, 2 * a:2 * a + 2, :].rearrange("p t (r h d) -> p (t r) h d", r=R, h=4),
                                           pv[a][:, :, 0:32].rearrange("p g (h d) -> p g h d", h=4), rd, ALU.mult)
                last.then_inc(s["sa_o"], 1)

            def add_product(n_ps, bank, ps_sem):
                dve.wait_ge(ps_sem, n_ps)
                V.tensor_tensor(x[:, :, :].rearrange(flat), x[:, :, :].rearrange(flat), PS[:, bank, :], ALU.add)\
                    .then_inc(s["x_up"], 1)

            def add_bias(r):
                link(V.tensor_tensor(x[:, :, :], x[:, :, :], row(r).unsqueeze(1).broadcast_to([128, T, D]), ALU.add))

            self_attention(0)
            add_product(1, 7, s["wo_ps"])
            dve.wait_ge(s["x_up"], 2)

            layer_norm(2, xn, s["ln_out"])
            dve.wait_ge(s["g_relu"], 1)
            link(V.tensor_reduce(s1(M_HM, 16), fused[:, :, :].rearrange("p t (b q) -> p (t b) q", q=S), AX, ALU.add))
            V.tensor_tensor(mix[:, 0:128].rearrange("p (e b) -> p e b", e=E),
                            wa[:, A_G2:A_G2 + E].unsqueeze(2).broadcast_to([128, E, B]),
                            s1(M_HM, 16).unsqueeze(1).broadcast_to([128, E, B]), ALU.mult).then_inc(s["g_x"], 1)
            dve.wait_ge(s["g_bc_ps"], 1)
            link(V.scalar_tensor_tensor(gbc[:, :, :], PS[:, 1, 0:128].rearrange("p (e b) -> p e b", e=E), 1.0 / S,
                                        row(R_G2, E).unsqueeze(2).broadcast_to([128, E, B]), ALU.mult, ALU.add))
            for e in range(E):
                V.tensor_tensor(zz[:, e, :].rearrange("p (b q) -> p b q", q=S), xT[:, :].rearrange("p (b q) -> p b q", q=S),
                                gbc[:, e, :].unsqueeze(2).broadcast_to([128, B, S]), ALU.mult).then_inc(s["z_ready"], 1)
            be = "p (c b e) -> p c b e"
            link(V.tensor_tensor(mix[:, :].rearrange(be, c=FC, b=B),
                                 gbc[:, :, :].rearrange("p e b -> p b e").unsqueeze(1).broadcast_to([128, FC, B, E]),
                                 col(K_TB1, FC * E).rearrange("p (c e) -> p c e", c=FC).unsqueeze(2)
                                 .broadcast_to([128, FC, B, E]), ALU.mult))
            link(V.tensor_reduce(mb1[:, :, :], mix[:, :].rearrange(be, c=FC, b=B), AX, ALU.add))
            link(V.tensor_tensor(mb1[:, :, :], mb1[:, :, :], col(K_B1, FC).unsqueeze(2).broadcast_to([128, FC, B]), ALU.add))
            te = "p (t e b) -> p t e b"
            link(V.tensor_tensor(mix[:, 0:128].rearrange(te, t=T, e=E),
                                 gbc[:, :, :].rearrange("p e (t b) -> p t e b", t=T),
                                 rm.unsqueeze(1).unsqueeze(1).broadcast_to([128, T, E, 4]), ALU.mult))
            link(V.tensor_reduce(gtok[:, :, :], mix[:, 0:128].rearrange(te, t=T, e=E), AX, ALU.add))
            add_bias(R_B2)
            dve.wait_ge(s["ld_tb2"], 16)
            for e in range(E):
                for t in range(T):
                    last = V.scalar_tensor_tensor(x[:, t, :], tb2[:, tile(e)], gtok[:, t, e:e + 1], x[:, t, :],
                                                  ALU.mult, ALU.add)
                link(last)
                if e % 2:
                    fc = e // 2
                    dve.wait_ge(s["u_ps"], fc + 1)
                    V.tensor_tensor(u[:, fc, :].rearrange("p (b q) -> p b q", q=S),
                                    PS[:, 2 + fc, :].rearrange("p (b q) -> p b q", q=S),
                                    mb1[:, fc, :].unsqueeze(2).broadcast_to([128, B, S]), ALU.add).then_inc(s["u_pre"], 1)
            for t in range(T):
                for g in range(3):
                    dve.wait_ge(s["y_ps"], 3 * t + g + 1)
                    for n in range(3):
                        e = 3 * g + n
                        ps = PS[:, Y_BANK[t % 2][g], 128 * n:128 * n + 128]
                        if e == 0:
                            last = V.tensor_tensor(x[:, t, :], ps, x[:, t, :], ALU.add)
                        else:
                            last = V.scalar_tensor_tensor(x[:, t, :], ps, gtok[:, t, e - 1:e], x[:, t, :],
                                                          ALU.mult, ALU.add)
                        link(last)
                if t == T - 1:
                    last = V.tensor_copy(s1(M_BND + 15), s1(M_BND + 14))
                    last.then_inc(s["y_used"], 1)
                else:
                    V.tensor_copy(s1(M_BND + 8 + t), s1(M_BND + 14)).then_inc(s["y_used"], 1)
            V.tensor_copy(s1(M_BND + 12), s1(M_BND + 14)).then_inc(s["x_up"], 1)
            dve.wait_ge(s["x_up"], 3)

            layer_norm(3, xn, s["ln_out"])
            dve.wait_ge(s["ln_out"], 3)
            add_bias(R_BO)
            for r in range(R):
                dve.wait_ge(s["lq_ev"], r + 1)
                link(V.tensor_copy(qs16[:, r, :], kexp[:, r, :]))
                link(V.tensor_tensor(qs16[64:128, r, :], kexp[64:128, r, :], qs16[64:128, r, :], ALU.subtract))
                for h in range(4):
                    V.tensor_scalar(qe[:, r, :, 32 * h:32 * h + 32], qs16[:, r, :].rearrange("p (b q) -> p b q", q=S),
                                    hm[:, h:h + 1], None, ALU.mult).then_inc(s["lq_e"], 1)

            dve.wait_ge(s["flag_ok"], 1)
            in_bounds = dve.value_load(flags[0:1, 0:1], min_val=0, max_val=1)

            def clip(i):
                sc = PS[:, L_BANK[i % 4], :]
                V.tensor_copy(mix[:, :], sc).then_inc(s["clip_step"], 1)
                dve.wait_ge(s["clip_step"], 3 * i + 1)
                V.tensor_tensor(mix[:, :], mix[:, :], mix[:, :], ALU.not_equal).then_inc(s["clip_step"], 1)
                dve.wait_ge(s["clip_step"], 3 * i + 2)
                V.tensor_reduce(s1(M_NAN + 64 + i), mix[:, :], AX, ALU.max)
                V.tensor_scalar(sc, sc, s1(M_LO), s1(M_HI), ALU.max, ALU.min).then_inc(s["clip_step"], 1)
                dve.wait_ge(s["clip_step"], 3 * i + 3)

            def sum_heads(g):
                dve.wait_ge(s["lo_ps"], 4 * g + 4)
                o = qTs[:, tile(g)].rearrange("p (b q) -> p b q", q=S)
                ps = PS[:, 5 + g % 2, :].rearrange("p (b h q) -> p b h q", b=4, h=4)
                link(V.tensor_scalar(o, ps[:, :, 0, :], hm[:, 0:1], None, ALU.mult))
                for h in range(1, 4):
                    last = V.scalar_tensor_tensor(o, ps[:, :, h, :], hm[:, h:h + 1], o, ALU.mult, ALU.add)
                    if h < 3:
                        link(last)
                last.then_inc(s["lo_sum"], 1)

            for b in range(B + 2):
                if b % 4 == 3 and b >= 7:
                    sum_heads(b // 4 - 1)
                for r in range(R):
                    if b < B:
                        i = R * b + r
                        dve.wait_ge(s["ls_ps"], i + 1)
                        if i >= 8:
                            dve.wait_ge(s["ls_bias"], i - 7)
                        with dve.If(in_bounds == 0):
                            clip(i)
                        V.tensor_reduce(s1(M_MX + i % 8), PS[:, L_BANK[i % 4], :], AX, ALU.max, negate=True)\
                            .then_inc(s["ls_max"], 1)
                    if 1 <= b <= B and r == 1:
                        dve.wait_ge(s["ls_exp"], R * b)
                        if b >= 3:
                            dve.wait_ge(s["ls_nrm"], R * (b - 2))
                        k = 4 * ((b - 1) % 2)
                        V.tensor_tensor(s1(M_NAN + 4 * (b - 1), 4), s1(M_DEN + k, 4), s1(M_DEN + k, 4), ALU.not_equal)
                        V.reciprocal(s1(M_RD + k, 4), s1(M_DEN + k, 4)).then_inc(s["ls_rd"], 1)
                        if b == B:
                            dve.wait_ge(s["ls_rd"], B)
                            link(V.tensor_reduce(s1(M_V), s1(M_NAN, 128), AX, ALU.max))
                            V.tensor_scalar(diag[:, :], ident, s1(M_V), None, ALU.mult).then_inc(s["gm_diag"], 1)
                    if b >= 2 and not on_act(R * (b - 2) + r):
                        i = R * (b - 2) + r
                        dve.wait_ge(s["lt_ps"], i + 1)
                        if b >= 4:
                            dve.wait_ge(s["lo_ps"], b - 3)
                        V.tensor_copy(lt[:, i % 8, :], PS[:, 3 + i % 2, :]).then_inc(s["lt_evd"], 1)
            sum_heads(3)
            dve.wait_ge(s["gm_ps"], n_gmax[0] + 1)
            link(V.tensor_reduce(s1(M_V + 1), PS[:, 7, 0:128], AX, ALU.max))
            link(V.tensor_scalar(flags[:, 1:2], s1(M_V + 1), 0.0, None, ALU.is_gt))
            dve.wait_ge(s["lo_sum"], 4)
            V.copy_predicated(qTs[:, :].rearrange("p (b q) -> p b q", q=S),
                              flags[:, 1:2].unsqueeze(2).broadcast_to([128, B, S]),
                              meanv[:, :].unsqueeze(2).broadcast_to([128, B, S])).then_inc(s["nan_ok"], 1)
            add_product(2, 7, s["wo_ps"])
            dve.wait_ge(s["x_up"], 4)

            layer_norm(4, xn, s["ln_out"])
            dve.wait_ge(s["ln_out"], 4)
            add_bias(R_BM)
            self_attention(1)
            add_product(3, 7, s["wo_ps"])
            dve.wait_ge(s["x_up"], 5)

            layer_norm(5, xn, s["ln_out"])
            dve.wait_ge(s["ln_out"], 5)
            add_bias(R_FB)
            add_product(1, 6, s["fin_ps"])

        @block.tensor
        def _(pe):
            def mm(o, lhsT, rhs, start=True, stop=True, **kw):
                return nc.tensor.matmul(o, lhsT, rhs, start=start, stop=stop, **kw)

            n_gmax = [0]

            def spread_max():
                n_gmax[0] += 1
                pe.wait_ge(s["gm_diag"], n_gmax[0])
                mm(PS[:, 7, 0:128], ones[:, :], diag[:, :]).then_inc(s["gm_ps"], 1)

            def transpose_rows(bank, src, idm, f=None):
                for t in range(T):
                    o = PS[:, bank, tile(t)] if f is None else PS[:, bank, 0:256].bitcast(bf16)[:, tile(t)]
                    last = nc.tensor.transpose(o, src[:, t, :], idm)
                return last

            pe.wait_ge(s["wabs"], 1)
            pe.wait_ge(s["consts"], 1)
            mm(PS[:, 7, 128:135], ones[:, :], s1(M_ABS, 7)).then_inc(s["ws_ps"], 1)
            pe.wait_ge(s["casts"], 1)
            spread_max()
            pe.wait_ge(s["txt_q"], 1)
            transpose_rows(6, qb, identb[:, :], 1).then_inc(s["txt_tp"], 1)
            pe.wait_ge(s["txt_qT"], 1)
            pe.wait_ge(s["ternary"], 3)
            for t in range(T):
                last = mm(PS[:, 5, tile(t)], qT[:, tile(t)], TW("txt"))
            last.then_inc(s["txt_ps"], 1)

            def quantised(layer, c):
                if c % 2 == 0:
                    pe.wait_ge(s["quant_dve"], 8 * layer + c // 2 + 1)
                elif c % 4 == 1:
                    pe.wait_ge(s["quant_pool"], 4 * layer + c // 4 + 1)
                else:
                    pe.wait_ge(s["quant_act"], 4 * layer + c // 4 + 1)

            pe.wait_ge(s["ternary"], 7)
            pe.wait_ge(s["ld_wa"], 16)
            cosm, sinm = cst[:, C_DC:C_DC + 128], cst[:, C_DS:C_DS + 128]
            cosn, nsinn = cst[:, C_DCN:C_DCN + 128], cst[:, C_DSN:C_DSN + 128]
            mm(PS[:, 0, 0:128], A("wr"), cosm, stop=False)
            mm(PS[:, 0, 0:128], A("wi"), sinm, start=False)
            mm(PS[:, 0, 128:256], A("wi"), cosn, stop=False)
            mm(PS[:, 0, 128:256], A("wr"), nsinn, start=False).then_inc(s["ft_ps"], 1)
            pe.wait_ge(s["bound_in"], 1)
            pe.wait_ge(s["ctx_sums"], 1)
            mm(PS[:, 6, 0:128], ones[:, :], mix[:, 0:128])
            mm(PS[:, 6, 128:256], ones[:, :], mix[:, 128:256])
            mm(PS[:, 6, 256:256 + B], A("wv", DC + 1), csum[0:DC + 1, :]).then_inc(s["bound_ps"], 1)
            pe.wait_ge(s["ft_ok"], 1)
            mm(PS[:, 1, 0:128], ft[:, 0, :], cosn, stop=False)
            mm(PS[:, 1, 0:128], ft[:, 1, :], sinm, start=False).then_inc(s["lin_ps"], 1)

            att = tern[:, 384:512]
            noff4 = noff[:, :].unsqueeze(1).broadcast_to([128, 4, 128])
            for layer in range(3):
                w = (TW("d2v")[0:DC, :], TW("img"), att)[layer]
                pn = DC if layer == 0 else 128
                spread_max()
                if layer == 0:
                    pe.wait_ge(s["lin_ok"], 1)
                for c in range(NCH):
                    quantised(layer, c)
                    if NCH * layer + c >= 4:
                        pe.wait_ge(s["ctx_ev"], NCH * layer + c - 3)
                    mm(PS[:, c % 4, :], w, y16[0:pn, chunk(c)], stop=False)
                    mm(PS[:, c % 4, :], w, noff4[0:pn], start=False).then_inc(s["ctx_mm"], 1)
                    if layer == 2:
                        if c >= 2:
                            pe.wait_ge(s["kv_ev"], c - 1)
                        for k in range(4):
                            o = PS[:, 4 + c % 2, tile(k)]
                            mm(o, y16[:, 512 * c + 128 * k:512 * c + 128 * k + 128], att, stop=False)
                            last = mm(o, noff[:, :], att, start=False)
                        last.then_inc(s["kv_mm"], 1)

            wk, wv = A("wk", DC + 1), A("wv", DC + 1)

            def keys(c, bank):
                mm(PS[:, bank, :], wk, cx[0:DC + 1, chunk(c)]).then_inc(s["kp_ps"], 1)

            for j in range(2):
                pe.wait_ge(s["fk_tok"], j + 1)
                transpose_rows(7, tmp, ident).then_inc(s["fk_tp"], 1)
                pe.wait_ge(s["fkT"], j + 1)
                pe.wait_ge(s["ctx_ev"], 3 * NCH)
                pe.wait_ge(s["kv_ev"], NCH)
                for t in range(T):
                    if j:
                        pe.wait_ge(s["kp_l"], t + 1)
                    for b in range(4):
                        c = 128 * t + 32 * b
                        last = mm(PS[32 * b:32 * b + 32, t, :], xT[:, c:c + 32], big[:, 0, chunk(4 * t + b)])
                    last.then_inc(s["sc_ps"], 1)
                for t in range(T):
                    pe.wait_ge(s["sc_exp"], T * j + t + 1)
                    if t >= 2:
                        if t % 2:
                            pe.wait_ge(s["sc_teva"], 2 * j + 1)
                        else:
                            pe.wait_ge(s["sc_tev"], 2 * j + 1)
                    for k in range(4):
                        last = nc.tensor.transpose(PS[:, 4 + t % 2, tile(k)], work[:, t, tile(k)], ident)
                    last.then_inc(s["sc_tp"], 1)
                    if t % 2:
                        keys(4 * j + t // 2, t // 2)
                for t in range(T):
                    if t % 2:
                        pe.wait_ge(s["sc_teva"], 2 * j + t // 2 + 1)
                    else:
                        pe.wait_ge(s["sc_tev"], 2 * j + t // 2 + 1)
                    for k in range(4):
                        for b in range(4):
                            c = 512 * (4 * t + b) + 128 * k + 64 * j
                            last = mm(PS[32 * b:32 * b + 32, 6, tile(t)],
                                      wt[:, t, 128 * k + 32 * b:128 * k + 32 * b + 32],
                                      big[:, 1, c:c + 64].unsqueeze(1).broadcast_to([128, 2, 64]),
                                      start=(k == 0), stop=(k == 3))
                last.then_inc(s["pv_ps"], 1)
                for c, bank in KEYS_AFTER_ROUND[j]:
                    keys(c, bank)

            spread_max()
            pe.wait_ge(s["f1_in"], 1)
            transpose_rows(6, qb, identb[:, :], 1).then_inc(s["f1_tp"], 1)
            pe.wait_ge(s["f1_qT"], 1)
            avg_rows = avgb[:, :].unsqueeze(2).broadcast_to([128, B, S])
            for fc in range(FC):
                if fc < 2:
                    pe.wait_ge(s["kp_l"], 6)
                else:
                    pe.wait_ge(s["kp_l"], 7 + fc)
                mm(PS[:, fc, :], TW("f1")[:, 128 * fc:128 * fc + 128], qT[:, :], stop=False)
                mm(PS[:, fc, :], TW("f1")[:, FF + 128 * fc:FF + 128 * fc + 128], avg_rows, start=False)\
                    .then_inc(s["f1_ps"], 1)
            for c, bank in KEYS_IN_FF[:2]:
                keys(c, bank)
            spread_max()
            for n, (c, bank) in enumerate(KEYS_IN_FF[2:]):
                pe.wait_ge(s["f1_ev"], n + 1)
                keys(c, bank)
            pe.wait_ge(s["f2_qd"], 2)
            pe.wait_ge(s["f2_qa"], 2)
            wt16 = w1[:, FF + 2048:FF + 4096].bitcast(f16).rearrange("p (r n two) -> p r n two", r=4, two=2)[:, :, :, 0]
            for t in range(T):
                for fc in range(FC):
                    w = TW("f2")[:, tile(fc)]
                    mm(PS[:, 5, tile(t)], wt16[:, fc, tile(t)], w, start=(fc == 0), stop=False)
                    last = mm(PS[:, 5, tile(t)], noff[:, :], w, start=False, stop=(fc == FC - 1))
            last.then_inc(s["f2_ps"], 1)

            def context_values(part):
                for n, (c, bank) in enumerate(VALUES[part]):
                    if part == 0 and c < 4:
                        pe.wait_ge(s["kp_l"], 13 + c)
                    elif n >= (2 if part == 3 else 4):
                        pe.wait_ge(s["vp_ev"], c - (1 if part == 3 else 3))
                    for k in range(4):
                        a = 512 * c + 128 * k
                        last = mm(PS[:, bank, tile(k)], cx[0:DC + 1, a:a + 128], wv)
                    last.then_inc(s["vp_ps"], 1)

            context_values(0)
            def rows_to_features(n, src):
                pe.wait_ge(s["ln_out"], n)
                transpose_rows(7, src, ident).then_inc(s["xt_ps"], 1)

            def self_attention(k):
                q, kk, v, o = ("q1", "k1", "v1", "m1") if k else ("q0", "k0", "v0", "o0")
                pe.wait_ge(s["xt_ev"], (1, 4)[k])
                mm(PS[:, 4, :], A(q), xT[:, :]).then_inc(s["qk_ps"], 1)
                mm(PS[:, 5, :], A(kk), xT[:, :]).then_inc(s["qk_ps"], 1)
                if k == 0:
                    pe.wait_ge(s["vp_ev"], len(VALUES[0]))
                mm(PS[:, 3, :], A(kk), xT[:, :]).then_inc(s["qk_ps"], 1)

                def values(half):
                    for b in range(8 * (1 - half), 8 * (2 - half)):
                        last = mm(PS[:, 4 + b // 4, tile(b % 4)],
                                  xrep[:, tile(b)], A(v))
                    last.then_inc(s["v_ps"], 1)

                pe.wait_ge(s["xrep_ok"], k + 1)
                values(0)
                pe.wait_ge(s["q_ev"], k + 1)
                pe.wait_ge(s["k_evd"], 2 * k + 2)
                values(1)
                pe.wait_ge(s["k_eva"], 2 * k + 2)
                for r in range(R):
                    mm(PS[:, r, :], identb[:, :], maskb[:, k, :].unsqueeze(1).broadcast_to([128, 4, 128]), stop=False,
                       skip_group_check=True)
                for r in range(R):
                    for b in range(B):
                        t, b4 = b // 4, b % 4
                        last = mm(PS[32 * b4:32 * b4 + 32, r, tile(t)], qTs[32 * r:32 * r + 32, 32 * b:32 * b + 32],
                                  kexp[32 * r:32 * r + 32, :, 32 * b:32 * b + 32], start=False, stop=(b >= 12),
                                  skip_group_check=True)
                    last.then_inc(s["sa_ps"], 1)
                for r in range(R):
                    pe.wait_ge(s["sa_exp"], R * k + r + 1)
                    for t in range(T):
                        last = nc.tensor.transpose(PS[:, r, tile(t)], work[:, r, tile(t)], ident)
                    last.then_inc(s["sa_tp"], 1)
                pe.wait_ge(s["v_ev"], 8 * k + 8)
                pe.wait_ge(s["vones"], k + 1)
                for r in range(R):
                    if r % 2:
                        pe.wait_ge(s["sa_teva"], 2 * k + r // 2 + 1)
                    else:
                        pe.wait_ge(s["sa_tevd"], 2 * k + r // 2 + 1)
                    for b in range(B):
                        t, b4 = b // 4, b % 4
                        c = 144 * (t % 2) + 36 * r
                        last = mm(PS[32 * b4:32 * b4 + 32, 4 + t // 2, c:c + 36], wt[:, r, 32 * b:32 * b + 32],
                                  vexp[:, b, r, :])
                last.then_inc(s["sa_pv"], 1)
                pe.wait_ge(s["sa_o"], k + 1)
                transpose_rows(6, tmp, ident).then_inc(s["ot_ps"], 1)
                pe.wait_ge(s["ot_ev"], k + 1)
                for t in range(T):
                    last = mm(PS[:, 7, tile(t)], xT[:, tile(t)], A(o))
                last.then_inc(s["wo_ps"], 1)

            rows_to_features(1, fused)
            self_attention(0)
            context_values(1)

            rows_to_features(2, xn)
            pe.wait_ge(s["xt_ev"], 2)
            mm(PS[:, 0, :], A("gate1"), xT[:, :]).then_inc(s["g_ps"], 1)
            context_values(2)
            pe.wait_ge(s["g_x"], 1)
            mm(PS[:, 1, 0:128], ones[:, :], mix[:, 0:128]).then_inc(s["g_bc_ps"], 1)
            pe.wait_ge(s["ld_w1"], 16)
            pe.wait_ge(s["vp_ev"], sum(len(v) for v in VALUES[:3]))
            for fc in range(FC):
                for e in range(E1):
                    if e and fc == 0:
                        pe.wait_ge(s["z_ready"], e)
                        pe.wait_ge(ld_ws[e - 1], 16)
                    last = mm(PS[:, 2 + fc, :], w1[:, FF * e + 128 * fc:FF * e + 128 * fc + 128],
                              zz[:, e - 1, :] if e else xT[:, :], start=(e == 0), stop=(e == E))
                last.then_inc(s["u_ps"], 1)
            pe.wait_ge(s["u_act"], FC)
            pe.wait_ge(s["ld_w2"], 16)
            for t in range(T):
                if t >= 2:
                    pe.wait_ge(s["y_used"], t - 1)
                for g in range(3):
                    for fc in range(FC):
                        last = mm(PS[:, Y_BANK[t % 2][g], 0:384], u[:, fc, tile(t)], w2[:, fc, 3 * g:3 * g + 3, :],
                                  start=(fc == 0), stop=(fc == FC - 1))
                    last.then_inc(s["y_ps"], 1)

            context_values(3)
            rows_to_features(3, xn)
            pe.wait_ge(s["xt_ev"], 3)
            for r in range(R):
                mm(PS[:, r, :], wa[:, A_WQR + 128 * r:A_WQR + 128 * r + 128], xT[:, :]).then_inc(s["lq_ps"], 1)
            for b in range(B + 3):
                for r in range(R):
                    if b < B:
                        i = R * b + r
                        if i >= 4:
                            pe.wait_ge(s["ls_exp"], i - 3)
                        if b == 0:
                            pe.wait_ge(s["lq_e"], 4 * r + 4)
                        if i == 0:
                            pe.wait_ge(s["lq_ev"], R)
                            pe.wait_ge(s["kst_done"], 16 * 16)
                            pe.wait_ge(s["vp_ev"], NCH)
                        mm(PS[:, L_BANK[i % 4], :], qe[:, r, b, :], kst[:, r, chunk(b)]).then_inc(s["ls_ps"], 1)
                    if 2 <= b < B + 2:
                        i = R * (b - 2) + r
                        pe.wait_ge(s["ls_nrm"], i + 1)
                        if i >= 2:
                            if on_act(i - 2):
                                pe.wait_ge(s["lt_eva"], n_act(i - 1))
                            else:
                                pe.wait_ge(s["lt_evd"], n_dve(i - 1))
                        for k in range(4):
                            last = nc.tensor.transpose(PS[:, 3 + i % 2, tile(k)], lp[:, i % 8, tile(k)], ident)
                        last.then_inc(s["lt_ps"], 1)
                if b >= 3:
                    bb = b - 3
                    pe.wait_ge(s["lt_eva"], n_act(R * bb + R))
                    pe.wait_ge(s["lt_evd"], n_dve(R * bb + R))
                    if bb % 4 == 0 and bb >= 8:
                        pe.wait_ge(s["lo_sum"], bb // 4 - 1)
                    for k in range(4):
                        for r in range(R):
                            v0 = 512 * bb + 128 * k + 32 * r
                            last = mm(PS[32 * r:32 * r + 32, 5 + (bb // 4) % 2, tile(bb % 4)], cx[:, v0:v0 + 32],
                                      lt[:, (R * bb + r) % 8, tile(k)], start=(k == 0), stop=(k == 3))
                    last.then_inc(s["lo_ps"], 1)
                if b == B + 1:
                    spread_max()
            pe.wait_ge(s["nan_ok"], 1)
            for t in range(T):
                last = mm(PS[:, 7, tile(t)], qTs[:, tile(t)], A("wo"))
            last.then_inc(s["wo_ps"], 1)

            rows_to_features(4, xn)
            self_attention(1)
            rows_to_features(5, xn)
            pe.wait_ge(s["xt_ev"], 5)
            for t in range(T):
                last = mm(PS[:, 6, tile(t)], xT[:, tile(t)], lin[:, :])
            last.then_inc(s["fin_ps"], 1)


def _constants():
    c = np.zeros((128, C_END), np.float32)
    p = np.arange(128)
    c[:, C_ID:C_ID + 128] = np.eye(128)
    theta = (1.0 / 10000.0 ** (np.arange(64, dtype=np.float32) / 64)).astype(np.float32)
    ang = (p % S).astype(np.float32)[:, None] * theta[None, :]
    c[:, C_COS:C_COS + 64] = np.cos(ang)
    c[:, C_SIN:C_SIN + 64] = np.sin(ang)
    c[:, C_HM:C_HM + 4] = ((p // HD) % 4)[:, None] == np.arange(4)[None, :]
    c[:, C_RM:C_RM + 4] = (p // 32)[:, None] == np.arange(4)[None, :]
    later = (p % S)[None, :] > (p % S)[:, None]
    c[:, C_MK0:C_MK0 + 128] = later * -1e9
    c[:, C_MK1:C_MK1 + 128] = later * -1e12
    a = 2 * np.pi * ((p[:, None] * p[None, :]) % D) / D
    c[:, C_DC:C_DC + 128], c[:, C_DS:C_DS + 128] = np.cos(a), np.sin(a)
    c[:, C_DCN:C_DCN + 128], c[:, C_DSN:C_DSN + 128] = np.cos(a) / D, -np.sin(a) / D
    c[:, C_CNT:C_CNT + 7] = 1.0 / np.array(X_COUNT)
    return c


def _pad(a, rows=128):
    z = np.zeros((rows, a.shape[1]), np.float32)
    z[:a.shape[0]] = a
    return z


def kernel(**inputs):
    import concourse.bacc as _bacc
    from concourse import mybir as _mybir
    from concourse.bass_utils import run_bass_kernel_spmd as _run

    v = {k: np.asarray(a) for k, a in inputs.items()}
    X, SA0, F0 = "L0_xattn_", "L0_attn_", "L0_ffn_"
    X1, SA1, F1 = "L1_xattn_", "L1_attn_", "L1_ffn_"

    def rep_heads(w):
        return np.repeat(w.reshape(R, 1, HD, D), 4, axis=1).reshape(D, D).T

    wx = np.concatenate([_pad(v[X + "W_d2v"].T), v[X + "W_img"].T, v[X + "W_txt"].T, v[X + "W_att0"].T,
                         v[X + "W_att1"].T, v[X + "W_f1"].T[:128], v[X + "W_f1"].T[128:]]
                        + [v[X + "W_f2"].T[128 * c:128 * c + 128] for c in range(FC)], axis=1)
    wqr = np.tile(v[X1 + "Wq"].reshape(D, R, 1, 32), (1, 1, 4, 1)).reshape(D, 512)
    wa = np.concatenate(
        [v[SA0 + "W_q"].T, rep_heads(v[SA0 + "W_k"]), rep_heads(v[SA0 + "W_v"]), v[SA0 + "W_o"].T,
         v[F0 + "gate_w1"].T, v[X1 + "Wo"], v[SA1 + "Wq"], v[SA1 + "Wk"], v[SA1 + "Wv"], v[SA1 + "Wm"],
         v[F1 + "w_freq_real"], v[F1 + "w_freq_imag"],
         _pad(np.concatenate([v[X1 + "Wk"], v[X1 + "bk"][None]])), _pad(np.concatenate([v[X1 + "Wv"], v[X1 + "bv"][None]])),
         wqr, v[F0 + "gate_w2"].T], axis=1)
    w1 = np.concatenate([v[F0 + "W1"][None], v[F0 + "TW1"]]).transpose(2, 0, 1).reshape(D, E1 * FF)
    w2 = np.concatenate([v[F0 + "W2"][None], v[F0 + "TW2"]])
    w2 = w2.reshape(E1, D, FC, 128).transpose(3, 2, 0, 1).reshape(128, FC * E1 * D)
    tb1 = v[F0 + "Tb1"].reshape(E, FC, 128).transpose(2, 1, 0).reshape(128, FC * E)
    c1 = lambda a: a.reshape(-1, 128).T
    cols = np.concatenate([c1(v[X + "b_d2v"]), c1(v[X + "b_img"]),
                           c1(np.concatenate([v[X + "b_att0"], v[X + "b_att1"]])), c1(v[X + "b_f1"]),
                           c1(v[F0 + "gate_b1"]), np.zeros((128, 3), np.float32),
                           c1(np.tile(v[X1 + "bq"].reshape(R, 1, 32), (1, 4, 1)).reshape(512)),
                           c1(v[SA1 + "bq"]), c1(v[SA1 + "bk"]), c1(v[SA1 + "bv"]), c1(v[F0 + "b1"]), tb1], axis=1)
    assert cols.shape[1] == K_END
    a0, a1 = v[X + "b_att0"], v[X + "b_att1"]
    row = np.concatenate([v[X + "b_txt"], a0, a0, a1, a1, v[X + "b_f2"], v[X1 + "bo"], v[SA1 + "bm"], v[F1 + "bias"],
                          v[F0 + "b2"], v[F0 + "gate_b2"], v[X1 + "bq"], v[F0 + "Tb2"].reshape(-1)])
    assert row.shape[0] == R_END + E * D
    arrays = {
        "x_in": v["x"].reshape(N, D), "ctx_in": np.concatenate([v["ctx_768"].reshape(CP, DC).T, np.ones((1, CP), np.float32)]), "wx_in": wx, "wa_in": wa,
        "w1_in": w1, "w2_in": w2, "const_in": _constants(), "cols_in": cols, "rows_in": np.tile(row[None], (128, 1)),
    }
    arrays = {k: np.ascontiguousarray(a) for k, a in arrays.items()}
    nc = _bacc.Bacc("TRN2", target_bir_lowering=False, num_devices=1)
    args = [nc.dram_tensor(k, a.shape, _mybir.dt.float32, kind="ExternalInput").ap() for k, a in arrays.items()]
    args.append(nc.dram_tensor("out", (N, D), _mybir.dt.float32, kind="ExternalOutput").ap())
    perceiver(nc, *args)
    return _run(nc, [arrays], core_ids=[0]).results[0]["out"].reshape(B, S, D)
```

```python
import numpy as np
import concourse.bass as bass
from concourse import mybir
from contextlib import ExitStack

B, S, D = 16, 32, 128
P, DC = 512, 96
N = B * S
T = N // 128
CP = B * P
NCH = CP // 512
FF = 512
FC = FF // 128
E = 8
E1 = E + 1
H, HD = 16, 8
R = 4
LN_EPS = 1e-5
HEAD_SCALE = float(HD) ** -0.5
OFFSET = 1152.0
MAGIC = 1.5 * 2.0 ** 23 + 0x6400 + 128
ROUND = 1.5 * 2.0 ** 23
F16_TOP = 2048.0
MAX_FACTOR = 1024.0
MAX_FACTOR_PAIR = float(np.full(2, MAX_FACTOR, np.float16).view(np.float32)[0])
CLIP = 10000.0

X_COLS = {"d2v": (0, 128), "img": (128, 128), "txt": (256, 128), "att0": (384, 64),
          "att1": (448, 64), "f1": (512, 1024), "f2": (1536, 512)}
X_COUNT = [DC * D, D * D, D * D, D * 64, D * 64, 2 * D * FF, FF * D]
A_NAMES = ["q0", "k0", "v0", "o0", "gate1", "wo", "q1", "k1", "v1", "m1", "wr", "wi", "wk", "wv"]
A_COL = {n: 128 * i for i, n in enumerate(A_NAMES)}
A_WQR = 128 * len(A_NAMES)
A_G2 = A_WQR + 512
A_END = A_G2 + E
C_ID, C_COS, C_SIN = 0, 128, 192
C_HM, C_RM, C_MK0, C_MK1 = 256, 260, 264, 392
C_DC, C_DS, C_DCN, C_DSN, C_CNT = 520, 648, 776, 904, 1032
C_END = 1040
K_D2V, K_IMG, K_ATT, K_F1, K_G1, K_Z = 0, 1, 2, 3, 7, 8
K_BK, K_BV, K_BQR = 9, 10, 11
K_Q1, K_K1, K_V1 = 15, 16, 17
K_B1, K_TB1 = 18, 22
K_END = K_TB1 + FC * E
R_TXT, R_A0, R_A1, R_F2, R_BO, R_BM, R_FB, R_B2, R_G2 = (128 * i for i in range(9))
R_BQ = R_G2 + E
R_END = R_BQ + 128
Y_BANK = ((6, 7, 0), (1, 2, 3))


def perceiver(nc, x_in, ctx_in, wx_in, wa_in, w1_in, w2_in, const_in, cols_in, rows_in, out):
    f32, bf16, f16 = mybir.dt.float32, mybir.dt.bfloat16, mybir.dt.float16
    ALU, ACT, AX = mybir.AluOpType, mybir.ActivationFunctionType, mybir.AxisListType.X
    ctx = ExitStack()
    with ctx:
        def sb(name, shape, dt=f32):
            return ctx.enter_context(nc.sbuf_tensor(name, shape, dt))

        def sem(name):
            return ctx.enter_context(nc.semaphore(name))

        cx = sb("cx", [128, CP])
        yq = sb("yq", [128, CP])
        big = sb("big", [128, 2, CP])
        w1 = sb("w1", [128, E1 * FF])
        wa = sb("wa", [128, A_END])
        sa = sb("sa", [128, 2048 + B * R * 36])
        tern = sb("tern", [128, 2048], bf16)
        cst = sb("cst", [128, C_END])
        cols = sb("cols", [128, K_END])
        rows = sb("rows", [128, R_END])
        ones = sb("ones", [128, 128])
        identh = sb("identh", [128, 128], f16)
        mparts = sb("mparts", [128, 2, R, 3], f16)
        mrest = sb("mrest", [128, 2, R])
        identb = sb("identb", [128, 128], bf16)
        maskb = sb("maskb", [128, 2, 128], bf16)
        noff = sb("noff", [128, 128], bf16)
        x = sb("x", [128, T, D])
        xn = sb("xn", [128, T, D])
        tmp = sb("tmp", [128, T, D])
        fused = sb("fused", [128, T, D])
        xT = sb("xT", [128, N])
        qTs = sb("qTs", [128, N])
        bn = sb("bn", [128, T, 6])
        mv = sb("mv", [128, T, 2])
        veps = sb("veps", [128, T])
        rstd = sb("rstd", [128, T])
        mhalf = sb("mhalf", [128, T])
        sm = sb("sm", [128, 464])
        diag = sb("diag", [128, 128])
        avg = sb("avg", [128, B])
        avgq = sb("avgq", [128, B])
        avgb = sb("avgb", [128, B], bf16)
        qb = sb("qb", [128, T, D], bf16)
        qT = sb("qT", [128, N], bf16)
        csum = sb("csum", [128, B])
        meanv = sb("meanv", [128, B])
        flags = sb("flags", [128, 2], mybir.dt.int32)
        gbc = sb("gbc", [128, E, B])
        gtok = sb("gtok", [128, T, E])
        mb1 = sb("mb1", [128, FC, B])
        mix = sb("mix", [128, 512])
        lin = sb("lin", [128, 128])
        PS = ctx.enter_context(nc.psum_tensor("PS", [128, 8, 512], f32))

        wx = sa[:, 0:2048]
        ft = mix[:, 256:512].rearrange("p (a b) -> p a b", a=2)
        kexp = sa[:, 0:2048].rearrange("p (h n) -> p h n", h=4)
        vexp = sa[:, 2048:].rearrange("p (b r c) -> p b r c", b=B, r=R)
        zz = sa[:, 0:E * N].rearrange("p (e n) -> p e n", e=E)
        work = w1[:, FF:FF + 2048].rearrange("p (r n) -> p r n", r=4)
        wt = w1[:, FF + 2048:FF + 4096].rearrange("p (r n) -> p r n", r=4)
        xrep = w1[:, FF + 2048:FF + 4096]
        nd = w1[:, FF + 2048:FF + 3072].rearrange("p (v n) -> p v n", v=2)
        w2 = yq[:, 0:FC * E1 * D].rearrange("p (c e d) -> p c e d", c=FC, e=E1)
        u = yq[:, FC * E1 * D:FC * E1 * D + FC * N].rearrange("p (c n) -> p c n", c=FC)
        qe = yq[:, 0:4096].bitcast(f16).rearrange("p (r b n) -> p r b n", r=R, b=B)
        pt8 = yq[:, 4096:8192].rearrange("p (s n) -> p s n", s=8)
        pt4 = w1[:, FF:FF + 2048].rearrange("p (s n) -> p s n", s=4)
        tb2 = tern[:, :].bitcast(f32)
        qs16 = tern[:, :].bitcast(f16).rearrange("p (r n) -> p r n", r=R)
        y16 = yq[:, :].bitcast(f16).rearrange("p (n two) -> p n two", two=2)[:, :, 0]
        khl = yq[:, :].bitcast(f16).rearrange("p (two n) -> p two n", two=2)
        kst = big[:, :, :].rearrange("p a n -> p (a n)").bitcast(f16).rearrange("p (r n) -> p r n", r=R)
        ident = cst[:, C_ID:C_ID + 128]
        hm = cst[:, C_HM:C_HM + 4]
        rm = cst[:, C_RM:C_RM + 4]

        M_V, M_G, M_SI, M_INV = 0, 20, 30, 40
        M_ABS, M_WS, M_TH, M_NTH = 50, 58, 66, 74
        M_SC = 82
        M_NMX, M_DEN, M_RD = 96, 104, 112
        M_Z4, M_RD64 = 124, 128
        M_AL, M_BE, M_ES, M_BKS, M_BQS, M_QB = 192, 193, 194, 195, 196, 200
        M_ABC = 204
        M_MX = 208
        M_HM = 224
        M_MAG, M_WA = 250, 251
        M_SAM = 256
        M_BND = 320
        M_LO, M_HI = M_BND + 6, M_BND + 7
        M_NAN = 336

        S_BANK, ST_BANK, M_BANK, O_BANK = (0, 1, 2), (3, 4), 7, (5, 6)

        def s1(i, n=1):
            return sm[:, i:i + n]

        KEYS_AFTER_ROUND = (((2, 2), (3, 3)), ((6, 4), (7, 5), (8, 2), (9, 3)))
        KEYS_IN_FF = ((10, 4), (11, 6), (12, 0), (13, 1), (14, 2), (15, 3))
        VALUES = (tuple((c, c % 4) for c in range(8)), tuple((c, c - 4) for c in range(8, 11)),
                  (), tuple((c, 4 + c % 2) for c in range(11, 16)))

        def pt(i):
            return pt8[:, i % 12, :] if i % 12 < 8 else pt4[:, i % 12 - 8, :]

        def head_queries(r, h):
            return qe[0:96, r, :, 32 * h:32 * h + 32]

        def split_queries(r):
            return qs16[0:96, r, :].rearrange("p (b q) -> p b q", q=S)

        def col(i, n=1):
            return cols[:, i:i + n]

        def row(i, n=128):
            return rows[:, i:i + n]

        def A(name, p=128):
            return wa[0:p, A_COL[name]:A_COL[name] + 128]

        def TW(name):
            c, n = X_COLS[name]
            return tern[:, c:c + n]

        names = ["ld_x", "ld_wx", "ld_wa", "ld_w1", "ld_w2", "ld_cst", "ld_cols", "ld_rows", "ld_tb2", "kst_done",
                 "out_done", "consts", "casts", "wabs", "ws_ps", "ln_veps", "ln_rstd", "ln_out", "gm_diag", "gm_ps",
                 "ternary", "txt_q", "txt_tp", "txt_qT", "txt_ps", "fk_tok", "fk_tp", "fkT",
                 "scale_ready", "f2_scale", "vp_ev", "ft_ok", "ctx_sums", "clip_step", "flag_ok", "nan_ok", "quant_dve", "quant_act", "quant_pool", "ctx_mm", "ctx_ev",
                 "kv_mm", "kv_ev", "sc_ps", "sc_max", "sc_exp", "sc_tp", "sc_tev", "sc_teva", "pv_ps",
                 "f1_in", "f1_tp", "f1_qT", "f1_ps", "f1_ev", "f2_qd", "f2_qa", "f2_ps", "x_up", "x_tile", "x_done", "k_plain", "k_evp",
                 "xt_ps", "xt_ev", "xrep_ok", "qk_ps", "q_ev", "k_evd", "k_eva", "v_ps", "v_ev", "vones", "sa_ps", "sa_sub", "sa_exp",
                 "sa_tp", "sa_tevd", "sa_teva", "sa_pv", "sa_o", "ot_ps", "ot_ev", "wo_ps",
                 "g_ps", "g_relu", "g_x", "g_bc_ps", "z_ready", "u_ps", "u_pre", "u_act", "y_ps", "y_used",
                 "kp_ps", "kp_h", "kp_l", "vp_ps", "bound_in", "bound_ps", "scales_ok", "root_in", "root",
                 "lq_ps", "lq_ev", "lq_low", "lq_e", "lq_e2", "lq_e3", "key_ones", "ls_ps", "ls_max", "ls_parts", "split", "sum_step", "ls_rows_ps", "ls_rows", "lt_raw", "lt_clipped",
                 "lt_ps", "lt_exp", "lo_ps", "lo_sum",
                 "ft_ps", "lin_ps", "lin_ok", "fin_ps", "dve_link", "act_link", "pool_link"]

        s = {n: sem(n) for n in names}
        ld_ws = [sem(f"ld_ws{e}") for e in range(1, E1)]
        ld_ctx = [sem(f"ld_ctx{i}") for i in range(8)]
        block = ctx.enter_context(nc.Block())

        def chunk(c):
            return slice(512 * c, 512 * c + 512)

        def tile(t):
            return slice(128 * t, 128 * t + 128)

        @block.sync
        def _(sp):
            sp.dma_start(x[:, :, :], x_in.rearrange("(t p) d -> p t d", p=128)).then_inc(s["ld_x"], 16)
            sp.dma_start(cst[:, :], const_in).then_inc(s["ld_cst"], 16)
            sp.dma_start(wx, wx_in).then_inc(s["ld_wx"], 16)
            sp.dma_start(cols[:, :], cols_in).then_inc(s["ld_cols"], 16)
            w = CP // 8
            for i in range(8):
                sp.dma_start(cx[0:DC + 1, i * w:(i + 1) * w], ctx_in[:, i * w:(i + 1) * w]).then_inc(ld_ctx[i], 16)
            sp.dma_start(rows[:, :], rows_in[:, 0:R_END]).then_inc(s["ld_rows"], 16)
            sp.dma_start(wa[:, :], wa_in).then_inc(s["ld_wa"], 16)
            sp.dma_start(w1[:, 0:FF], w1_in[:, 0:FF]).then_inc(s["ld_w1"], 16)
            sp.wait_ge(s["f2_ps"], 1)
            sp.dma_start(tb2, rows_in[:, R_END:R_END + E * D]).then_inc(s["ld_tb2"], 16)
            sp.wait_ge(s["pv_ps"], 2)
            sp.wait_ge(s["kp_h"], NCH)
            sp.wait_ge(s["kp_l"], NCH)
            for r in range(R):
                for part in range(3):
                    sp.dma_start(kst[32 * part:32 * part + 32, r, :],
                                 khl[32 * r:32 * r + 32, part % 2, :]).then_inc(s["kst_done"], 16)
            sp.wait_ge(s["kst_done"], 3 * R * 16)
            sp.dma_start(w2, w2_in.rearrange("p (c e d) -> p c e d", c=FC, e=E1)).then_inc(s["ld_w2"], 16)
            sp.wait_ge(s["sa_pv"], 1)
            for e in range(1, E1):
                sp.dma_start(w1[:, e * FF:(e + 1) * FF], w1_in[:, e * FF:(e + 1) * FF]).then_inc(ld_ws[e - 1], 16)
            sp.wait_ge(s["x_done"], T)
            sp.dma_start(out.rearrange("(t p) d -> p t d", p=128), x[:, :, :]).then_inc(s["out_done"], 16)
            sp.wait_ge(s["out_done"], 16)

        @block.gpsimd
        def _(pool):
            links = [0]

            def link(ins):
                links[0] += 1
                ins.then_inc(s["pool_link"], 1)
                pool.wait_ge(s["pool_link"], links[0])

            def rstd_of(n):
                pool.wait_ge(s["ln_veps"], n + 1)
                pool.tensor_tensor(rstd[:, :], veps[:, :], mhalf[:, :], ALU.pow).then_inc(s["ln_rstd"], 1)

            pool.memset(mhalf[:, :], -0.5)
            link(pool.memset(sm[:, :], 0.0))
            pool.memset(s1(M_MAG), MAGIC)
            pool.memset(s1(M_QB + 2), 0.5)
            pool.memset(noff[:, :], -OFFSET)
            pool.memset(ones[:, :], 1.0).then_inc(s["consts"], 1)
            rstd_of(0)
            pool.wait_ge(s["ld_cst"], 16)
            pool.tensor_copy(identb[:, :], ident)
            pool.tensor_copy(identh[:, :], ident)
            pool.tensor_copy(maskb[:, :, :], cst[:, C_MK0:C_MK0 + 256].rearrange("p (a b) -> p a b", a=2))\
                .then_inc(s["casts"], 1)

            def quantise(layer, src, pn):
                pool.wait_ge(s["scale_ready"], layer + 1)
                for c in range(1, NCH, 4):
                    pool.tensor_scalar(yq[0:pn, chunk(c)], src[0:pn, chunk(c)], sm[0:pn, M_INV + layer:M_INV + layer + 1],
                                       MAGIC, ALU.mult, ALU.add).then_inc(s["quant_pool"], 1)

            def last_keys_head(k):
                pool.wait_ge(s["k_plain"], k + 1)
                pool.tensor_scalar(kexp[:, 3, :], mix[:, :], hm[:, 3:4], 1.0, ALU.mult, ALU.mult).then_inc(s["k_evp"], 1)

            def value_ones(k):
                for b in range(B):
                    last = pool.tensor_copy(vexp[:, b, :, 32:36], rm.unsqueeze(1).broadcast_to([128, R, 4]))
                last.then_inc(s["vones"], 1)

            quantise(0, cx, DC)
            quantise(1, big[:, 0, :], 128)
            quantise(2, big[:, 0, :], 128)
            pool.wait_ge(s["root_in"], 1)
            pool.tensor_tensor(s1(M_QB + 1), s1(M_QB), s1(M_QB + 2), ALU.pow).then_inc(s["root"], 1)
            value_ones(0)
            rstd_of(1)
            last_keys_head(0)
            pool.wait_ge(s["pv_ps"], 2)
            pool.wait_ge(s["k_evp"], 1)
            link(pool.memset(big[96:99, 0, :], MAX_FACTOR_PAIR))
            rstd_of(2)
            pool.wait_ge(s["ln_rstd"], 3)
            pool.memset(big[96:99, 1, :], MAX_FACTOR_PAIR).then_inc(s["key_ones"], 1)
            pool.wait_ge(s["key_ones"], 1)
            pool.wait_ge(s["u_ps"], FC)
            value_ones(1)
            rstd_of(3)
            for r in range(R):
                pool.wait_ge(s["lq_low"], r + 1)
                pool.tensor_scalar(head_queries(r, 3), split_queries(r), hm[0:96, 3:4], 1.0, ALU.mult, ALU.mult)\
                    .then_inc(s["lq_e3"], 1)
            rstd_of(4)
            last_keys_head(1)
            rstd_of(5)

        @block.scalar
        def _(act):
            links = [0]

            def link(ins):
                links[0] += 1
                ins.then_inc(s["act_link"], 1)
                act.wait_ge(s["act_link"], links[0])

            def affine(o, i, scale=1.0, bias=0.0, func=ACT.Identity, **kw):
                return nc.scalar.activation(o, i, func, bias=bias, scale=scale, **kw)

            act.wait_ge(s["ld_wx"], 16)
            act.wait_ge(s["consts"], 1)
            for n, (c, w) in enumerate(X_COLS.values()):
                last = nc.scalar.activation(big[:, 0, c:c + w], wx[:, c:c + w], ACT.Abs, accum_out=s1(M_ABS + n))
            last.then_inc(s["wabs"], 1)

            def quantise(layer, src, pn):
                act.wait_ge(s["scale_ready"], layer + 1)
                for c in range(3, NCH, 4):
                    affine(yq[0:pn, chunk(c)], src[0:pn, chunk(c)], scale=sm[0:pn, M_INV + layer:M_INV + layer + 1],
                           bias=sm[0:pn, M_MAG:M_MAG + 1]).then_inc(s["quant_act"], 1)

            def ctx_evacuate(layer, bias, with_sum=False):
                for c in range(NCH):
                    act.wait_ge(s["ctx_mm"], NCH * layer + c + 1)
                    kw = {"accum_out": avg[:, c:c + 1]} if with_sum else {}
                    affine(big[:, 0, chunk(c)], PS[:, c % 4, :], scale=s1(M_SC + layer), bias=bias, **kw)\
                        .then_inc(s["ctx_ev"], 1)

            for b in range(B):
                act.wait_ge(ld_ctx[b // 2], 16)
                last = affine(big[0:DC + 1, 1, chunk(b)], cx[0:DC + 1, chunk(b)], accum_out=csum[0:DC + 1, b:b + 1])
            last.then_inc(s["ctx_sums"], 1)
            quantise(0, cx, DC)
            act.wait_ge(s["ld_cols"], 16)
            ctx_evacuate(0, col(K_D2V))
            act.wait_ge(s["ld_wa"], 16)
            nc.scalar.activation(mix[:, 0:128], A("wk"), ACT.Abs)
            nc.scalar.activation(mix[:, 128:256].rearrange("p (r n) -> p r n", r=R),
                                 wa[:, A_WQR:A_WQR + 512].rearrange("p (r n) -> p r n", r=R)[:, :, 0:32],
                                 ACT.Square).then_inc(s["bound_in"], 1)
            act.wait_ge(s["ft_ps"], 1)
            nc.scalar.copy(ft[:, 0, :], PS[:, 4, 0:128])
            affine(ft[:, 1, :], PS[:, 4, 128:256], scale=-1.0).then_inc(s["ft_ok"], 1)
            act.wait_ge(s["txt_tp"], 1)
            nc.scalar.copy(qT[:, :], PS[:, 6, 0:256].bitcast(bf16)).then_inc(s["txt_qT"], 1)
            quantise(1, big[:, 0, :], 128)
            ctx_evacuate(1, col(K_IMG), True)
            act.wait_ge(s["lin_ps"], 1)
            nc.scalar.copy(lin[:, :], PS[:, 6, 384:512]).then_inc(s["lin_ok"], 1)
            quantise(2, big[:, 0, :], 128)
            ctx_evacuate(2, col(K_ATT))

            def key_high(c, bank):
                act.wait_ge(s["kp_ps"], c + 1)
                affine(khl[:, 0, chunk(c)], PS[:, bank, :], scale=s1(M_AL)).then_inc(s["kp_h"], 1)

            act.wait_ge(s["scales_ok"], 1)
            for j in range(2):
                act.wait_ge(s["fk_tp"], j + 1)
                affine(xT[:, :], PS[:, 7, :], scale=float(D) ** -0.5).then_inc(s["fkT"], 1)
                for t in range(T):
                    act.wait_ge(s["sc_max"], T * j + t + 1)
                    if j:
                        act.wait_ge(s["sc_tp"], t + 1)
                    nc.scalar.activation(work[:, t, :], PS[:, t, :], ACT.Exp, bias=s1(M_NMX + t),
                                         accum_out=s1(M_DEN + t)).then_inc(s["sc_exp"], 1)
                for t in range(1, T, 2):
                    act.wait_ge(s["sc_tp"], T * j + t + 1)
                    nc.scalar.copy(wt[:, t, :], PS[:, 4 + t % 2, :]).then_inc(s["sc_teva"], 1)
                    key_high(4 * j + t // 2, t // 2)
                for c, bank in KEYS_AFTER_ROUND[j]:
                    key_high(c, bank)

            act.wait_ge(s["f1_tp"], 1)
            nc.scalar.copy(qT[:, :], PS[:, 6, 0:256].bitcast(bf16)).then_inc(s["f1_qT"], 1)
            for fc in range(FC):
                act.wait_ge(s["f1_ps"], fc + 1)
                affine(work[:, fc, :], PS[:, fc, :], scale=s1(M_SC + 5), bias=col(K_F1 + fc), func=ACT.Relu)\
                    .then_inc(s["f1_ev"], 1)
            for c, bank in KEYS_IN_FF[:2]:
                key_high(c, bank)
            act.wait_ge(s["f2_scale"], 1)
            for fc in (1, 3):
                affine(wt[:, fc, :], work[:, fc, :], scale=s1(M_INV + 6), bias=s1(M_MAG)).then_inc(s["f2_qa"], 1)
            for c, bank in KEYS_IN_FF[2:]:
                key_high(c, bank)

            def context_values(part):
                for c, bank in VALUES[part]:
                    act.wait_ge(s["vp_ps"], c + 1)
                    nc.scalar.copy(cx[:, chunk(c)], PS[:, bank, :]).then_inc(s["vp_ev"], 1)

            context_values(0)

            def rows_to_features(n):
                act.wait_ge(s["xt_ps"], n)
                nc.scalar.copy(xT[:, :], PS[:, 7, :]).then_inc(s["xt_ev"], 1)

            def self_attention(k):
                act.wait_ge(s["qk_ps"], 2 * k + 1)
                affine(qTs[:, :], PS[:, 4, :], bias=col(K_Q1) if k else 0.0).then_inc(s["q_ev"], 1)
                act.wait_ge(s["k_plain"], k + 1)
                affine(kexp[:, 2, :], mix[:, :], scale=hm[:, 2:3]).then_inc(s["k_eva"], 1)

                def values(half):
                    act.wait_ge(s["v_ps"], 2 * k + half + 1)
                    b0 = 8 * (1 - half)
                    src = PS[:, 4 + b0 // 4:6 + b0 // 4, :].rearrange("p a (b r c) -> p (a b) r c", b=4, r=R)
                    for h in range(4):
                        affine(vexp[:, b0:b0 + 8, :, 8 * h:8 * h + 8], src[:, :, :, 8 * h:8 * h + 8],
                               scale=rm[:, h:h + 1]).then_inc(s["v_ev"], 1)

                values(0)
                for r in range(R):
                    act.wait_ge(s["sa_sub"], R * k + r + 1)
                    nc.scalar.activation(work[:, r, :], work[:, r, :], ACT.Exp, scale=HEAD_SCALE)\
                        .then_inc(s["sa_exp"], 1)
                    if r == 1:
                        values(1)
                for r in (1, 3):
                    act.wait_ge(s["sa_tp"], R * k + r + 1)
                    nc.scalar.copy(wt[:, r, :], PS[:, r, :]).then_inc(s["sa_teva"], 1)
                act.wait_ge(s["ot_ps"], k + 1)
                affine(xT[:, :], PS[:, 6, :], bias=col(K_V1) if k else 0.0).then_inc(s["ot_ev"], 1)

            rows_to_features(1)
            self_attention(0)
            context_values(1)
            rows_to_features(2)
            context_values(2)
            act.wait_ge(s["g_ps"], 1)
            affine(fused[:, :, :].rearrange("p t d -> p (t d)"), PS[:, 0, :], bias=col(K_G1), func=ACT.Relu)\
                .then_inc(s["g_relu"], 1)
            for fc in range(FC):
                act.wait_ge(s["u_pre"], fc + 1)
                nc.scalar.activation(u[:, fc, :], u[:, fc, :], ACT.Gelu_apprx_tanh).then_inc(s["u_act"], 1)
            context_values(3)
            rows_to_features(3)
            for r in range(R):
                act.wait_ge(s["lq_ps"], r + 1)
                affine(kexp[:, r, :], PS[:, r, :], scale=s1(M_BE), bias=s1(M_BQS + r)).then_inc(s["lq_ev"], 1)
            for r in range(R):
                act.wait_ge(s["lq_low"], r + 1)
                affine(head_queries(r, 2), split_queries(r), scale=hm[0:96, 2:3]).then_inc(s["lq_e2"], 1)

            for b in range(1, B + 2):
                for r in range(R):
                    if b >= 2:
                        i = R * (b - 2) + r
                        act.wait_ge(s["lt_ps"], i + 1)
                        if i >= 12:
                            act.wait_ge(s["lo_ps"], b - 4)
                        nc.scalar.activation(pt(i), PS[:, ST_BANK[i % 2], :], ACT.Exp, scale=s1(M_ES))\
                            .then_inc(s["lt_exp"], 1)
                    if r == 2 and b <= B:
                        act.wait_ge(s["ls_rows_ps"], b)
                        nc.scalar.copy(qe[96:99, :, b - 1, :], PS[96:99, M_BANK, :].rearrange("p (r n) -> p r n", r=R))\
                            .then_inc(s["ls_rows"], 1)
            rows_to_features(4)
            self_attention(1)
            rows_to_features(5)

        @block.vector
        def _(dve):
            V = nc.vector
            links = [0]

            def link(ins):
                links[0] += 1
                ins.then_inc(s["dve_link"], 1)
                dve.wait_ge(s["dve_link"], links[0])

            def layer_norm(n, out_tile, done=None, product=None):
                for t in range(T):
                    if product is not None:
                        ps_sem, k = product
                        dve.wait_ge(ps_sem, T * k + t + 1)
                        V.tensor_tensor(x[:, t, :], x[:, t, :], PS[:, t, 0:128], ALU.add).then_inc(s["x_tile"], 1)
                        n_tiles[0] += 1
                        if t:
                            dve.wait_ge(s["x_tile"], n_tiles[0] - 1)
                            V.bn_stats(bn[:, t - 1, :], x[:, t - 1, :])
                        if t == T - 1:
                            dve.wait_ge(s["x_tile"], n_tiles[0])
                            last = V.bn_stats(bn[:, t, :], x[:, t, :])
                    else:
                        last = V.bn_stats(bn[:, t, :], x[:, t, :])
                link(last)
                for t in range(T):
                    last = V.bn_aggr(mv[:, t, :], bn[:, t, :])
                link(last)
                V.tensor_scalar(veps[:, :], mv[:, :, 1], LN_EPS, None, ALU.add).then_inc(s["ln_veps"], 1)
                dve.wait_ge(s["ln_rstd"], n + 1)
                for t in range(T):
                    last = V.tensor_scalar(out_tile[:, t, :], x[:, t, :], mv[:, t, 0:1], rstd[:, t:t + 1],
                                           ALU.subtract, ALU.mult)
                    if done is not None:
                        last.then_inc(done, 1)
                if done is None:
                    link(last)

            n_gmax, n_tiles = [0], [0]

            def scales_of(i, ws):
                n_gmax[0] += 1
                dve.wait_ge(s["gm_ps"], n_gmax[0])
                link(V.tensor_reduce(s1(M_G + i), PS[:, 7, 0:128], AX, ALU.max))
                link(V.tensor_scalar(s1(M_SI + i), s1(M_G + i), 1e-8, 1.0 / 127.0, ALU.max, ALU.mult))
                V.tensor_tensor(s1(M_SC + i), s1(ws), s1(M_SI + i), ALU.mult)
                return V.reciprocal(s1(M_INV + i), s1(M_SI + i))

            def global_scale(i, ncols, ws, pn=128):
                if ncols > 1:
                    link(V.tensor_reduce(s1(M_V + 18), s1(M_V, ncols), AX, ALU.max))
                v = s1(M_V + 18) if ncols > 1 else s1(M_V)
                V.tensor_scalar(diag[:, :], ident, v, None, ALU.mult).then_inc(s["gm_diag"], 1)
                return scales_of(i, ws)

            dve.wait_ge(s["ld_x"], 16)
            dve.wait_ge(s["consts"], 1)
            layer_norm(0, xn)
            link(V.tensor_reduce(s1(M_V), xn[:, :, :].rearrange("p t d -> p (t d)"), AX, ALU.max,
                                 apply_absolute_value=True))
            dve.wait_ge(s["ld_cst"], 16)
            V.tensor_scalar(diag[:, :], ident, s1(M_V), None, ALU.mult).then_inc(s["gm_diag"], 1)

            def ctx_maxima(i0, i1):
                for i in range(i0, i1):
                    w = CP // 8
                    dve.wait_ge(ld_ctx[i], 16)
                    last = V.tensor_reduce(sm[0:DC, M_V + i:M_V + i + 1], cx[0:DC, i * w:(i + 1) * w], AX, ALU.max,
                                           apply_absolute_value=True)
                return last

            def ternary_of(which):
                for n, (c, w) in enumerate(X_COLS.values()):
                    if n in which:
                        last = V.tensor_scalar(tern[:, c:c + w], wx[:, c:c + w], s1(M_NTH + n), None, ALU.is_lt)
                link(last)
                for n, (c, w) in enumerate(X_COLS.values()):
                    if n in which:
                        V.scalar_tensor_tensor(tern[:, c:c + w], wx[:, c:c + w], s1(M_TH + n), tern[:, c:c + w],
                                               ALU.is_gt, ALU.subtract).then_inc(s["ternary"], 1)

            dve.wait_ge(s["gm_diag"], 1)
            link(V.memset(s1(M_V, 16), 0.0))
            ctx_maxima(0, 3)
            dve.wait_ge(s["ws_ps"], 1)
            link(V.tensor_tensor(s1(M_WS, 7), PS[:, 7, 128:135], cst[:, C_CNT:C_CNT + 7], ALU.mult))
            link(V.tensor_scalar(s1(M_WS, 7), s1(M_WS, 7), 1e-5, None, ALU.max))
            V.tensor_scalar(s1(M_TH, 7), s1(M_WS, 7), 0.5, None, ALU.mult)
            V.tensor_copy(sm[0:64, M_WA:M_WA + 1], sm[0:64, M_WS + 3:M_WS + 4])
            V.tensor_copy(sm[64:128, M_WA:M_WA + 1], sm[64:128, M_WS + 4:M_WS + 5])
            link(V.tensor_scalar(s1(M_NTH, 7), s1(M_WS, 7), -0.5, None, ALU.mult))
            ternary_of((0,))
            link(scales_of(3, M_WS + 2))
            link(ctx_maxima(3, 8))

            for layer in range(3):
                src, pn = (cx, DC) if layer == 0 else (big[:, 0, :], 128)
                if layer:
                    for c in range(NCH):
                        dve.wait_ge(s["ctx_ev"], NCH * (layer - 1) + c + 1)
                        last = V.tensor_reduce(s1(M_V + c), big[:, 0, chunk(c)], AX, ALU.max, apply_absolute_value=True)
                    link(last)
                last = global_scale(layer, 8 if layer == 0 else NCH, (M_WS, M_WS + 1, M_WA)[layer])
                last.then_inc(s["scale_ready"], 1)
                dve.wait_ge(s["scale_ready"], layer + 1)
                for c in range(0, NCH, 2):
                    V.tensor_scalar(yq[0:pn, chunk(c)], src[0:pn, chunk(c)], sm[0:pn, M_INV + layer:M_INV + layer + 1],
                                    MAGIC, ALU.mult, ALU.add).then_inc(s["quant_dve"], 1)
                if layer == 0:
                    link(V.tensor_scalar(tmp[:, :, :], xn[:, :, :], s1(M_INV + 3), ROUND, ALU.mult, ALU.add))
                    V.tensor_scalar(qb[:, :, :], tmp[:, :, :], ROUND, None, ALU.subtract).then_inc(s["txt_q"], 1)
                    ternary_of((1, 2, 3, 4))
                elif layer == 1:
                    dve.wait_ge(s["txt_ps"], 1)
                    dve.wait_ge(s["ld_rows"], 16)
                    V.scalar_tensor_tensor(fused[:, :, :], PS[:, 5, :].rearrange("p (t d) -> p t d", t=T), s1(M_SC + 3),
                                           row(R_TXT).unsqueeze(1).broadcast_to([128, T, D]), ALU.mult, ALU.add)
            def bound_step(n):
                if n == 0:
                    V.tensor_reduce(s1(M_BND), PS[:, 6, 0:128], AX, ALU.max)
                    V.tensor_reduce(s1(M_BND + 1), PS[:, 6, 128:256], AX, ALU.max)
                    V.tensor_scalar(s1(M_BND + 3), s1(M_G), 1.0, None, ALU.max)
                    link(V.tensor_reduce(s1(M_BND + 2), row(R_BQ), AX, ALU.max, apply_absolute_value=True))
                elif n == 1:
                    V.tensor_tensor(s1(M_BND + 4), s1(M_BND), s1(M_BND + 3), ALU.mult)
                    V.tensor_scalar(s1(M_QB), s1(M_BND + 1), float(D), None, ALU.mult).then_inc(s["root_in"], 1)
                    V.tensor_scalar(meanv[:, :], PS[:, 6, 256:256 + B], 1.0 / P, None, ALU.mult)
                elif n == 2:
                    dve.wait_ge(s["root"], 1)
                    link(V.tensor_tensor(s1(M_BND + 5), s1(M_QB + 1), s1(M_BND + 2), ALU.add))
                    link(V.tensor_scalar(s1(M_BND + 4, 2), s1(M_BND + 4, 2), 1e-30, 1.0 / F16_TOP, ALU.max, ALU.mult))
                elif n == 3:
                    V.reciprocal(s1(M_AL, 2), s1(M_BND + 4, 2))
                    link(V.scalar_tensor_tensor(s1(M_ES), s1(M_BND + 4), HEAD_SCALE, s1(M_BND + 5),
                                                ALU.mult, ALU.mult))
                elif n == 4:
                    V.tensor_scalar(flags[:, 0:1], s1(M_ES), HD * F16_TOP ** 2, 0.99 * CLIP, ALU.mult, ALU.is_le)\
                        .then_inc(s["flag_ok"], 1)
                    V.tensor_scalar(s1(M_BQS, 4), col(K_BQR, 4), s1(M_BE), None, ALU.mult)
                    link(V.reciprocal(s1(M_HI), s1(M_ES)))
                elif n == 5:
                    link(V.tensor_scalar(s1(M_LO), s1(M_HI), -CLIP, None, ALU.mult))
                    V.tensor_scalar(s1(M_HI), s1(M_HI), CLIP, None, ALU.mult).then_inc(s["scales_ok"], 1)

            dve.wait_ge(s["bound_ps"], 1)
            dve.wait_ge(s["lin_ok"], 1)
            dve.wait_ge(s["ld_cols"], 16)
            for c in range(NCH):
                dve.wait_ge(s["kv_mm"], c + 1)
                V.tensor_copy(big[:, 1, chunk(c)], PS[:, 4 + c % 2, :]).then_inc(s["kv_ev"], 1)
                if c % 2:
                    bound_step(c // 2)

            def key_low(c, bank):
                dve.wait_ge(s["kp_h"], c + 1)
                V.scalar_tensor_tensor(khl[:, 1, chunk(c)], PS[:, bank, :], s1(M_AL), khl[:, 0, chunk(c)],
                                       ALU.mult, ALU.subtract).then_inc(s["kp_l"], 1)

            for j in range(2):
                if j:
                    V.memset(tmp[:, :, 0:64], 0.0)
                else:
                    V.memset(tmp[:, :, 64:128], 0.0)
                V.tensor_tensor(tmp[:, :, 64 * j:64 * j + 64], fused[:, :, 0:64], fused[:, :, 64:128], ALU.add)\
                    .then_inc(s["fk_tok"], 1)
                if j:
                    for c, bank in KEYS_AFTER_ROUND[0]:
                        key_low(c, bank)
                for t in range(T):
                    dve.wait_ge(s["sc_ps"], T * j + t + 1)
                    V.tensor_reduce(s1(M_NMX + t), PS[:, t, :], AX, ALU.max, negate=True).then_inc(s["sc_max"], 1)
                dve.wait_ge(s["fk_tok"], j + 1)
                V.scalar_tensor_tensor(fused[:, :, :], row(R_A0 + 128 * j).unsqueeze(1).broadcast_to([128, T, D]), 0.1,
                                       fused[:, :, :], ALU.mult, ALU.add)
                for t in range(0, T, 2):
                    dve.wait_ge(s["sc_tp"], T * j + t + 1)
                    V.tensor_copy(wt[:, t, :], PS[:, 4 + t % 2, :]).then_inc(s["sc_tev"], 1)
                key_low(4 * j, 0)
                key_low(4 * j + 1, 1)
                if j == 0:
                    ternary_of((5, 6))
                dve.wait_ge(s["sc_exp"], T * j + T)
                V.reciprocal(s1(M_RD, T), s1(M_DEN, T))
                link(V.tensor_tensor(s1(M_RD + 5), s1(M_WS + 3 + j), s1(M_SI + 2), ALU.mult))
                link(V.tensor_scalar(s1(M_RD, T), s1(M_RD, T), s1(M_RD + 5), 0.1, ALU.mult, ALU.mult))
                dve.wait_ge(s["pv_ps"], j + 1)
                for t in range(T):
                    last = V.scalar_tensor_tensor(fused[:, t, :], PS[:, 6, tile(t)], s1(M_RD + t), fused[:, t, :],
                                                  ALU.mult, ALU.add)
                link(last)

            V.tensor_reduce(s1(M_V), fused[:, :, :].rearrange("p t d -> p (t d)"), AX, ALU.max, apply_absolute_value=True)
            link(V.tensor_scalar(avgq[:, :], avg[:, :], 1.0 / P, None, ALU.mult))
            link(V.tensor_reduce(s1(M_V + 1), avgq[:, :], AX, ALU.max, apply_absolute_value=True))
            link(global_scale(5, 2, M_WS + 5))
            V.tensor_scalar(avgq[:, :], avgq[:, :], s1(M_INV + 5), ROUND, ALU.mult, ALU.add)
            link(V.tensor_scalar(tmp[:, :, :], fused[:, :, :], s1(M_INV + 5), ROUND, ALU.mult, ALU.add))
            V.tensor_scalar(avgb[:, :], avgq[:, :], ROUND, None, ALU.subtract)
            V.tensor_scalar(qb[:, :, :], tmp[:, :, :], ROUND, None, ALU.subtract).then_inc(s["f1_in"], 1)
            for c, bank in KEYS_AFTER_ROUND[1]:
                key_low(c, bank)
            V.tensor_tensor(x[:, :, :], x[:, :, :], row(R_F2).unsqueeze(1).broadcast_to([128, T, D]), ALU.add)
            for fc in range(FC):
                dve.wait_ge(s["f1_ev"], fc + 1)
                last = V.tensor_reduce(s1(M_V + fc), work[:, fc, :], AX, ALU.max)
            link(last)
            global_scale(6, FC, M_WS + 6).then_inc(s["f2_scale"], 1)
            dve.wait_ge(s["f2_scale"], 1)
            for fc in (0, 2):
                V.tensor_scalar(wt[:, fc, :], work[:, fc, :], s1(M_INV + 6), MAGIC, ALU.mult, ALU.add)\
                    .then_inc(s["f2_qd"], 1)
            for c, bank in KEYS_IN_FF:
                key_low(c, bank)
            dve.wait_ge(s["f2_ps"], 1)
            flat = "p t d -> p (t d)"
            V.scalar_tensor_tensor(x[:, :, :].rearrange(flat), PS[:, 5, :], s1(M_SC + 6), x[:, :, :].rearrange(flat),
                                   ALU.mult, ALU.add).then_inc(s["x_up"], 1)

            dve.wait_ge(s["x_up"], 1)
            layer_norm(1, xn)
            pair = xn[:, :, :].rearrange("p t (n two) -> p t n two", two=2)
            cos = cst[:, C_COS:C_COS + 64].unsqueeze(1).broadcast_to([128, T, 64])
            sin = cst[:, C_SIN:C_SIN + 64].unsqueeze(1).broadcast_to([128, T, 64])
            V.tensor_tensor(fused[:, :, 0:64], pair[:, :, :, 0], cos, ALU.mult)
            V.tensor_tensor(tmp[:, :, 0:64], pair[:, :, :, 1], sin, ALU.mult)
            V.tensor_tensor(fused[:, :, 64:128], pair[:, :, :, 0], sin, ALU.mult)
            link(V.tensor_tensor(tmp[:, :, 64:128], pair[:, :, :, 1], cos, ALU.mult))
            V.tensor_tensor(fused[:, :, 0:64], fused[:, :, 0:64], tmp[:, :, 0:64], ALU.subtract)
            V.tensor_tensor(fused[:, :, 64:128], fused[:, :, 64:128], tmp[:, :, 64:128], ALU.add).then_inc(s["ln_out"], T)

            def self_attention(k):
                dve.wait_ge(s["xt_ev"], (1, 4)[k])
                V.tensor_copy(xrep.rearrange("p (b h q) -> p b h q", b=B, h=4),
                              xT[:, :].rearrange("p (b q) -> p b q", q=S).unsqueeze(2).broadcast_to([128, B, 4, S]))\
                    .then_inc(s["xrep_ok"], 1)
                dve.wait_ge(s["qk_ps"], 2 * k + 2)
                V.tensor_scalar(mix[:, :], PS[:, 5, :], col(K_K1) if k else s1(M_Z4), None, ALU.add)\
                    .then_inc(s["k_plain"], 1)
                dve.wait_ge(s["k_plain"], k + 1)
                for h in (0, 1):
                    V.tensor_scalar(kexp[:, h, :], mix[:, :], hm[:, h:h + 1], None, ALU.mult).then_inc(s["k_evd"], 1)
                for r in range(R):
                    dve.wait_ge(s["sa_ps"], R * k + r + 1)
                    mx = s1(M_SAM + 16 * r, 16)
                    sc = PS[:, r, :].rearrange("p (g n) -> p g n", n=S)
                    link(V.tensor_reduce(mx, sc, AX, ALU.max))
                    V.tensor_tensor(work[:, r, :].rearrange("p (g n) -> p g n", n=S), sc,
                                    mx.unsqueeze(2).broadcast_to([128, 16, S]), ALU.subtract).then_inc(s["sa_sub"], 1)
                for r in (0, 2):
                    dve.wait_ge(s["sa_tp"], R * k + r + 1)
                    V.tensor_copy(wt[:, r, :], PS[:, r, :]).then_inc(s["sa_tevd"], 1)
                dve.wait_ge(s["sa_pv"], k + 1)
                pv = [PS[:, 4 + a, 0:288].rearrange("p (g c) -> p g c", c=36) for a in range(2)]
                for a in range(2):
                    last = V.reciprocal(s1(M_RD64 + 32 * a, 32).rearrange("p (g h) -> p g h", h=4), pv[a][:, :, 32:36])
                link(last)
                for a in range(2):
                    rd = s1(M_RD64 + 32 * a, 32).rearrange("p (g h) -> p g h", h=4).unsqueeze(3)\
                        .broadcast_to([128, 8, 4, HD])
                    last = V.tensor_tensor(tmp[:, 2 * a:2 * a + 2, :].rearrange("p t (r h d) -> p (t r) h d", r=R, h=4),
                                           pv[a][:, :, 0:32].rearrange("p g (h d) -> p g h d", h=4), rd, ALU.mult)
                last.then_inc(s["sa_o"], 1)

            def add_bias(r):
                link(V.tensor_tensor(x[:, :, :], x[:, :, :], row(r).unsqueeze(1).broadcast_to([128, T, D]), ALU.add))

            self_attention(0)

            layer_norm(2, xn, s["ln_out"], (s["wo_ps"], 0))
            dve.wait_ge(s["g_relu"], 1)
            link(V.tensor_reduce(s1(M_HM, 16), fused[:, :, :].rearrange("p t (b q) -> p (t b) q", q=S), AX, ALU.add))
            V.tensor_tensor(mix[:, 0:128].rearrange("p (e b) -> p e b", e=E),
                            wa[:, A_G2:A_G2 + E].unsqueeze(2).broadcast_to([128, E, B]),
                            s1(M_HM, 16).unsqueeze(1).broadcast_to([128, E, B]), ALU.mult).then_inc(s["g_x"], 1)
            dve.wait_ge(s["g_bc_ps"], 1)
            link(V.scalar_tensor_tensor(gbc[:, :, :], PS[:, 1, 0:128].rearrange("p (e b) -> p e b", e=E), 1.0 / S,
                                        row(R_G2, E).unsqueeze(2).broadcast_to([128, E, B]), ALU.mult, ALU.add))
            for e in range(E):
                V.tensor_tensor(zz[:, e, :].rearrange("p (b q) -> p b q", q=S), xT[:, :].rearrange("p (b q) -> p b q", q=S),
                                gbc[:, e, :].unsqueeze(2).broadcast_to([128, B, S]), ALU.mult).then_inc(s["z_ready"], 1)
            be = "p (c b e) -> p c b e"
            link(V.tensor_tensor(mix[:, :].rearrange(be, c=FC, b=B),
                                 gbc[:, :, :].rearrange("p e b -> p b e").unsqueeze(1).broadcast_to([128, FC, B, E]),
                                 col(K_TB1, FC * E).rearrange("p (c e) -> p c e", c=FC).unsqueeze(2)
                                 .broadcast_to([128, FC, B, E]), ALU.mult))
            link(V.tensor_reduce(mb1[:, :, :], mix[:, :].rearrange(be, c=FC, b=B), AX, ALU.add))
            link(V.tensor_tensor(mb1[:, :, :], mb1[:, :, :], col(K_B1, FC).unsqueeze(2).broadcast_to([128, FC, B]), ALU.add))
            te = "p (t e b) -> p t e b"
            link(V.tensor_tensor(mix[:, 0:128].rearrange(te, t=T, e=E),
                                 gbc[:, :, :].rearrange("p e (t b) -> p t e b", t=T),
                                 rm.unsqueeze(1).unsqueeze(1).broadcast_to([128, T, E, 4]), ALU.mult))
            link(V.tensor_reduce(gtok[:, :, :], mix[:, 0:128].rearrange(te, t=T, e=E), AX, ALU.add))
            add_bias(R_B2)
            dve.wait_ge(s["ld_tb2"], 16)
            for e in range(E):
                for t in range(T):
                    last = V.scalar_tensor_tensor(x[:, t, :], tb2[:, tile(e)], gtok[:, t, e:e + 1], x[:, t, :],
                                                  ALU.mult, ALU.add)
                link(last)
                if e % 2:
                    fc = e // 2
                    dve.wait_ge(s["u_ps"], fc + 1)
                    V.tensor_tensor(u[:, fc, :].rearrange("p (b q) -> p b q", q=S),
                                    PS[:, 2 + fc, :].rearrange("p (b q) -> p b q", q=S),
                                    mb1[:, fc, :].unsqueeze(2).broadcast_to([128, B, S]), ALU.add).then_inc(s["u_pre"], 1)
            for t in range(T):
                for g in range(3):
                    dve.wait_ge(s["y_ps"], 3 * t + g + 1)
                    for n in range(3):
                        e = 3 * g + n
                        ps = PS[:, Y_BANK[t % 2][g], 128 * n:128 * n + 128]
                        if e == 0:
                            last = V.tensor_tensor(x[:, t, :], ps, x[:, t, :], ALU.add)
                        else:
                            last = V.scalar_tensor_tensor(x[:, t, :], ps, gtok[:, t, e - 1:e], x[:, t, :],
                                                          ALU.mult, ALU.add)
                        link(last)
                if t == T - 1:
                    last = V.tensor_copy(s1(M_BND + 15), s1(M_BND + 14))
                    last.then_inc(s["y_used"], 1)
                else:
                    V.tensor_copy(s1(M_BND + 8 + t), s1(M_BND + 14)).then_inc(s["y_used"], 1)
            V.tensor_copy(s1(M_BND + 12), s1(M_BND + 14)).then_inc(s["x_up"], 1)
            dve.wait_ge(s["x_up"], 2)

            layer_norm(3, xn, s["ln_out"])
            dve.wait_ge(s["ln_out"], 3 * T)
            add_bias(R_BO)
            for r in range(R):
                dve.wait_ge(s["lq_ev"], r + 1)
                link(V.tensor_copy(qs16[0:96, r, :], kexp[0:96, r, :]))
                V.tensor_tensor(qs16[64:96, r, :], kexp[64:96, r, :], qs16[64:96, r, :], ALU.subtract).then_inc(s["lq_low"], 1)
                dve.wait_ge(s["lq_low"], r + 1)
                for h in (0, 1):
                    V.tensor_scalar(head_queries(r, h), split_queries(r), hm[0:96, h:h + 1], None, ALU.mult)\
                        .then_inc(s["lq_e"], 1)

            dve.wait_ge(s["flag_ok"], 1)
            in_bounds = dve.value_load(flags[0:1, 0:1], min_val=0, max_val=1)

            def clip(i):
                sc = PS[:, S_BANK[i % 3], :]
                V.tensor_copy(mix[:, :], sc).then_inc(s["clip_step"], 1)
                dve.wait_ge(s["clip_step"], 3 * i + 1)
                V.tensor_tensor(mix[:, :], mix[:, :], mix[:, :], ALU.not_equal).then_inc(s["clip_step"], 1)
                dve.wait_ge(s["clip_step"], 3 * i + 2)
                V.tensor_reduce(s1(M_NAN + 64 + i), mix[:, :], AX, ALU.max)
                V.tensor_scalar(sc, sc, s1(M_LO), s1(M_HI), ALU.max, ALU.min).then_inc(s["clip_step"], 1)
                dve.wait_ge(s["clip_step"], 3 * i + 3)

            def clip_transposed(i):
                dve.wait_ge(s["lt_raw"], i + 1)
                sc = PS[:, ST_BANK[i % 2], :]
                V.tensor_scalar(sc, sc, s1(M_LO), s1(M_HI), ALU.max, ALU.min).then_inc(s["lt_clipped"], 1)

            def split_maximum(b, n):
                k = b % 2
                mx, rest = s1(M_MX + R * k, R), mrest[:, k, :]
                high, mid, low = (mparts[:, k, :, m] for m in range(3))
                if n == 0:
                    if b >= 2:
                        dve.wait_ge(s["ls_rows_ps"], b - 1)
                    V.tensor_scalar(high, mx, 1.0 / MAX_FACTOR, None, ALU.mult).then_inc(s["split"], 1)
                elif n == 1:
                    V.scalar_tensor_tensor(rest, mx, 1.0 / MAX_FACTOR, high, ALU.mult, ALU.subtract)\
                        .then_inc(s["split"], 1)
                elif n == 2:
                    V.tensor_copy(mid, rest).then_inc(s["split"], 1)
                else:
                    V.tensor_tensor(low, rest, mid, ALU.subtract).then_inc(s["ls_parts"], 1)

            def sum_heads(g, n):
                o = nd[:, :, 64 * g:64 * g + 64].rearrange("p v (b q) -> p v b q", q=S)
                ps = PS[:, O_BANK[g % 2], :].rearrange("p (v b h q) -> p v b h q", v=2, b=2, h=4)
                num, den = nd[:, 0, 64 * g:64 * g + 64], nd[:, 1, 64 * g:64 * g + 64]
                if n == 0:
                    dve.wait_ge(s["lo_ps"], 2 * g + 2)
                    last = V.tensor_scalar(o, ps[:, :, :, 0, :], hm[:, 0:1], None, ALU.mult)
                else:
                    dve.wait_ge(s["sum_step"], 6 * g + n)
                    if n < 4:
                        last = V.scalar_tensor_tensor(o, ps[:, :, :, n, :], hm[:, n:n + 1], o, ALU.mult, ALU.add)
                    elif n == 4:
                        V.tensor_tensor(tmp[:, 0, 0:64], den, den, ALU.not_equal).then_inc(s["lo_sum"], 1)
                        last = V.reciprocal(den, den)
                    else:
                        V.tensor_reduce(s1(M_NAN + g), tmp[:, 0, 0:64], AX, ALU.max)
                        last = V.tensor_tensor(qTs[:, 64 * g:64 * g + 64], num, den, ALU.mult)
                last.then_inc(s["sum_step"], 1)

            for b in range(B + 2):
                for r in range(R):
                    if b < B:
                        i = R * b + r
                        dve.wait_ge(s["ls_ps"], i + 1)
                        with dve.If(in_bounds == 0):
                            clip(i)
                        V.tensor_reduce(s1(M_MX + i % 8), PS[:, S_BANK[i % 3], :], AX, ALU.max, negate=True)\
                            .then_inc(s["ls_max"], 1)
                    if b >= 2:
                        with dve.If(in_bounds == 0):
                            clip_transposed(R * (b - 2) + r)
                    if 1 <= b <= B and r == 0:
                        dve.wait_ge(s["ls_max"], R * b)
                        split_maximum(b - 1, 0)
                    if b % 2 and b >= 5 and r >= 1:
                        sum_heads((b - 5) // 2, r - 1)
                    elif b % 2 == 0 and b >= 6 and r < 3:
                        sum_heads((b - 6) // 2, 3 + r)
                    if 1 <= b <= B and r == 0:
                        for n in range(1, 4):
                            dve.wait_ge(s["split"], 3 * b - 3 + n)
                            split_maximum(b - 1, n)
            for g, n in tuple((B // 2 - 2, n) for n in (3, 4, 5)) + tuple((B // 2 - 1, n) for n in range(6)):
                sum_heads(g, n)
            dve.wait_ge(s["sum_step"], 6 * B // 2)
            link(V.tensor_reduce(s1(M_V), s1(M_NAN, 128), AX, ALU.max))
            V.tensor_scalar(diag[:, :], ident, s1(M_V), None, ALU.mult).then_inc(s["gm_diag"], 1)
            dve.wait_ge(s["gm_ps"], n_gmax[0] + 1)
            link(V.tensor_reduce(s1(M_V + 1), PS[:, 7, 0:128], AX, ALU.max))
            link(V.tensor_scalar(flags[:, 1:2], s1(M_V + 1), 0.0, None, ALU.is_gt))
            V.copy_predicated(qTs[:, :].rearrange("p (b q) -> p b q", q=S),
                              flags[:, 1:2].unsqueeze(2).broadcast_to([128, B, S]),
                              meanv[:, :].unsqueeze(2).broadcast_to([128, B, S])).then_inc(s["nan_ok"], 1)

            layer_norm(4, xn, s["ln_out"], (s["wo_ps"], 1))
            dve.wait_ge(s["ln_out"], 4 * T)
            add_bias(R_BM)
            self_attention(1)

            layer_norm(5, xn, s["ln_out"], (s["wo_ps"], 2))
            dve.wait_ge(s["ln_out"], 5 * T)
            add_bias(R_FB)
            for t in range(T):
                dve.wait_ge(s["fin_ps"], t + 1)
                V.tensor_tensor(x[:, t, :], x[:, t, :], PS[:, t, 0:128], ALU.add).then_inc(s["x_done"], 1)

        @block.tensor
        def _(pe):
            def mm(o, lhsT, rhs, start=True, stop=True, **kw):
                return nc.tensor.matmul(o, lhsT, rhs, start=start, stop=stop, **kw)

            n_gmax = [0]

            def spread_max():
                n_gmax[0] += 1
                pe.wait_ge(s["gm_diag"], n_gmax[0])
                mm(PS[:, 7, 0:128], ones[:, :], diag[:, :]).then_inc(s["gm_ps"], 1)

            def transpose_rows(bank, src, idm, f=None):
                for t in range(T):
                    o = PS[:, bank, tile(t)] if f is None else PS[:, bank, 0:256].bitcast(bf16)[:, tile(t)]
                    last = nc.tensor.transpose(o, src[:, t, :], idm)
                return last

            pe.wait_ge(s["consts"], 1)
            spread_max()
            pe.wait_ge(s["wabs"], 1)
            mm(PS[:, 7, 128:135], ones[:, :], s1(M_ABS, 7)).then_inc(s["ws_ps"], 1)
            def quantised(layer, c):
                if c % 2 == 0:
                    pe.wait_ge(s["quant_dve"], 8 * layer + c // 2 + 1)
                elif c % 4 == 1:
                    pe.wait_ge(s["quant_pool"], 4 * layer + c // 4 + 1)
                else:
                    pe.wait_ge(s["quant_act"], 4 * layer + c // 4 + 1)

            cosm, sinm = cst[:, C_DC:C_DC + 128], cst[:, C_DS:C_DS + 128]
            cosn, nsinn = cst[:, C_DCN:C_DCN + 128], cst[:, C_DSN:C_DSN + 128]
            att = tern[:, 384:512]
            noff4 = noff[:, :].unsqueeze(1).broadcast_to([128, 4, 128])
            for layer in range(3):
                w = (TW("d2v")[0:DC, :], TW("img"), att)[layer]
                pn = DC if layer == 0 else 128
                if layer == 1:
                    pe.wait_ge(s["ld_wa"], 16)
                    mm(PS[:, 4, 0:128], A("wr"), cosm, stop=False)
                    mm(PS[:, 4, 0:128], A("wi"), sinm, start=False)
                    mm(PS[:, 4, 128:256], A("wi"), cosn, stop=False)
                    mm(PS[:, 4, 128:256], A("wr"), nsinn, start=False).then_inc(s["ft_ps"], 1)
                    pe.wait_ge(s["casts"], 1)
                    pe.wait_ge(s["txt_q"], 1)
                    transpose_rows(6, qb, identb[:, :], 1).then_inc(s["txt_tp"], 1)
                spread_max()
                if layer == 1:
                    pe.wait_ge(s["txt_qT"], 1)
                    for t in range(T):
                        last = mm(PS[:, 5, tile(t)], qT[:, tile(t)], TW("txt"))
                    last.then_inc(s["txt_ps"], 1)
                    pe.wait_ge(s["bound_in"], 1)
                    pe.wait_ge(s["ctx_sums"], 1)
                    mm(PS[:, 6, 0:128], ones[:, :], mix[:, 0:128])
                    mm(PS[:, 6, 128:256], ones[:, :], mix[:, 128:256])
                    mm(PS[:, 6, 256:256 + B], A("wv", DC + 1), csum[0:DC + 1, :]).then_inc(s["bound_ps"], 1)
                if layer == 2:
                    pe.wait_ge(s["ft_ok"], 1)
                    mm(PS[:, 6, 384:512], ft[:, 0, :], cosn, stop=False)
                    mm(PS[:, 6, 384:512], ft[:, 1, :], sinm, start=False).then_inc(s["lin_ps"], 1)
                pe.wait_ge(s["ternary"], 5 if layer else 1)
                for c in range(NCH):
                    quantised(layer, c)
                    if NCH * layer + c >= 4:
                        pe.wait_ge(s["ctx_ev"], NCH * layer + c - 3)
                    mm(PS[:, c % 4, :], w, y16[0:pn, chunk(c)], stop=False)
                    mm(PS[:, c % 4, :], w, noff4[0:pn], start=False).then_inc(s["ctx_mm"], 1)
                    if layer == 2:
                        if c >= 2:
                            pe.wait_ge(s["kv_ev"], c - 1)
                        for k in range(4):
                            o = PS[:, 4 + c % 2, tile(k)]
                            mm(o, y16[:, 512 * c + 128 * k:512 * c + 128 * k + 128], att, stop=False)
                            last = mm(o, noff[:, :], att, start=False)
                        last.then_inc(s["kv_mm"], 1)

            wk, wv = A("wk", DC + 1), A("wv", DC + 1)

            def keys(c, bank):
                mm(PS[:, bank, :], wk, cx[0:DC + 1, chunk(c)]).then_inc(s["kp_ps"], 1)

            for j in range(2):
                pe.wait_ge(s["fk_tok"], j + 1)
                transpose_rows(7, tmp, ident).then_inc(s["fk_tp"], 1)
                pe.wait_ge(s["fkT"], j + 1)
                pe.wait_ge(s["ctx_ev"], 3 * NCH)
                pe.wait_ge(s["kv_ev"], NCH)
                for t in range(T):
                    if j:
                        pe.wait_ge(s["kp_l"], t + 1)
                    for b in range(4):
                        c = 128 * t + 32 * b
                        last = mm(PS[32 * b:32 * b + 32, t, :], xT[:, c:c + 32], big[:, 0, chunk(4 * t + b)])
                    last.then_inc(s["sc_ps"], 1)
                for t in range(T):
                    pe.wait_ge(s["sc_exp"], T * j + t + 1)
                    if t >= 2:
                        if t % 2:
                            pe.wait_ge(s["sc_teva"], 2 * j + 1)
                        else:
                            pe.wait_ge(s["sc_tev"], 2 * j + 1)
                    for k in range(4):
                        last = nc.tensor.transpose(PS[:, 4 + t % 2, tile(k)], work[:, t, tile(k)], ident)
                    last.then_inc(s["sc_tp"], 1)
                    if t % 2:
                        keys(4 * j + t // 2, t // 2)
                for t in range(T):
                    if t % 2:
                        pe.wait_ge(s["sc_teva"], 2 * j + t // 2 + 1)
                    else:
                        pe.wait_ge(s["sc_tev"], 2 * j + t // 2 + 1)
                    for k in range(4):
                        for b in range(4):
                            c = 512 * (4 * t + b) + 128 * k + 64 * j
                            last = mm(PS[32 * b:32 * b + 32, 6, tile(t)],
                                      wt[:, t, 128 * k + 32 * b:128 * k + 32 * b + 32],
                                      big[:, 1, c:c + 64].unsqueeze(1).broadcast_to([128, 2, 64]),
                                      start=(k == 0), stop=(k == 3))
                last.then_inc(s["pv_ps"], 1)
                for c, bank in KEYS_AFTER_ROUND[j]:
                    keys(c, bank)

            spread_max()
            pe.wait_ge(s["f1_in"], 1)
            transpose_rows(6, qb, identb[:, :], 1).then_inc(s["f1_tp"], 1)
            pe.wait_ge(s["f1_qT"], 1)
            pe.wait_ge(s["ternary"], 7)
            avg_rows = avgb[:, :].unsqueeze(2).broadcast_to([128, B, S])
            for fc in range(FC):
                if fc < 2:
                    pe.wait_ge(s["kp_l"], 6)
                else:
                    pe.wait_ge(s["kp_l"], 7 + fc)
                mm(PS[:, fc, :], TW("f1")[:, 128 * fc:128 * fc + 128], qT[:, :], stop=False)
                mm(PS[:, fc, :], TW("f1")[:, FF + 128 * fc:FF + 128 * fc + 128], avg_rows, start=False)\
                    .then_inc(s["f1_ps"], 1)
            for c, bank in KEYS_IN_FF[:2]:
                keys(c, bank)
            spread_max()
            for n, (c, bank) in enumerate(KEYS_IN_FF[2:]):
                pe.wait_ge(s["f1_ev"], n + 1)
                keys(c, bank)
            pe.wait_ge(s["f2_qd"], 2)
            pe.wait_ge(s["f2_qa"], 2)
            wt16 = w1[:, FF + 2048:FF + 4096].bitcast(f16).rearrange("p (r n two) -> p r n two", r=4, two=2)[:, :, :, 0]
            for t in range(T):
                for fc in range(FC):
                    w = TW("f2")[:, tile(fc)]
                    mm(PS[:, 5, tile(t)], wt16[:, fc, tile(t)], w, start=(fc == 0), stop=False)
                    last = mm(PS[:, 5, tile(t)], noff[:, :], w, start=False, stop=(fc == FC - 1))
            last.then_inc(s["f2_ps"], 1)

            def context_values(part):
                for n, (c, bank) in enumerate(VALUES[part]):
                    if part == 0 and c < 4:
                        pe.wait_ge(s["kp_l"], 13 + c)
                    elif n >= (2 if part == 3 else 4):
                        pe.wait_ge(s["vp_ev"], c - (1 if part == 3 else 3))
                    for k in range(4):
                        a = 512 * c + 128 * k
                        last = mm(PS[:, bank, tile(k)], cx[0:DC + 1, a:a + 128], wv)
                    last.then_inc(s["vp_ps"], 1)

            context_values(0)
            def rows_to_features(n, src):
                for t in range(T):
                    pe.wait_ge(s["ln_out"], T * (n - 1) + t + 1)
                    last = nc.tensor.transpose(PS[:, 7, tile(t)], src[:, t, :], ident)
                last.then_inc(s["xt_ps"], 1)

            def self_attention(k):
                q, kk, v, o = ("q1", "k1", "v1", "m1") if k else ("q0", "k0", "v0", "o0")
                pe.wait_ge(s["xt_ev"], (1, 4)[k])
                mm(PS[:, 4, :], A(q), xT[:, :]).then_inc(s["qk_ps"], 1)
                mm(PS[:, 5, :], A(kk), xT[:, :]).then_inc(s["qk_ps"], 1)

                def values(half):
                    for b in range(8 * (1 - half), 8 * (2 - half)):
                        last = mm(PS[:, 4 + b // 4, tile(b % 4)],
                                  xrep[:, tile(b)], A(v))
                    last.then_inc(s["v_ps"], 1)

                pe.wait_ge(s["xrep_ok"], k + 1)
                values(0)
                if k == 0:
                    pe.wait_ge(s["vp_ev"], len(VALUES[0]))
                for r in range(R):
                    mm(PS[:, r, :], identb[:, :], maskb[:, k, :].unsqueeze(1).broadcast_to([128, 4, 128]), stop=False,
                       skip_group_check=True)
                pe.wait_ge(s["q_ev"], k + 1)
                pe.wait_ge(s["k_plain"], k + 1)
                values(1)
                pe.wait_ge(s["k_evd"], 2 * k + 2)
                pe.wait_ge(s["k_eva"], k + 1)
                pe.wait_ge(s["k_evp"], k + 1)
                for r in range(R):
                    for b in range(B):
                        t, b4 = b // 4, b % 4
                        last = mm(PS[32 * b4:32 * b4 + 32, r, tile(t)], qTs[32 * r:32 * r + 32, 32 * b:32 * b + 32],
                                  kexp[32 * r:32 * r + 32, :, 32 * b:32 * b + 32], start=False, stop=(b >= 12),
                                  skip_group_check=True)
                    last.then_inc(s["sa_ps"], 1)
                for r in range(R):
                    pe.wait_ge(s["sa_exp"], R * k + r + 1)
                    for t in range(T):
                        last = nc.tensor.transpose(PS[:, r, tile(t)], work[:, r, tile(t)], ident)
                    last.then_inc(s["sa_tp"], 1)
                pe.wait_ge(s["v_ev"], 8 * k + 8)
                pe.wait_ge(s["vones"], k + 1)
                for r in range(R):
                    if r % 2:
                        pe.wait_ge(s["sa_teva"], 2 * k + r // 2 + 1)
                    else:
                        pe.wait_ge(s["sa_tevd"], 2 * k + r // 2 + 1)
                    for b in range(B):
                        t, b4 = b // 4, b % 4
                        c = 144 * (t % 2) + 36 * r
                        last = mm(PS[32 * b4:32 * b4 + 32, 4 + t // 2, c:c + 36], wt[:, r, 32 * b:32 * b + 32],
                                  vexp[:, b, r, :])
                last.then_inc(s["sa_pv"], 1)
                pe.wait_ge(s["sa_o"], k + 1)
                transpose_rows(6, tmp, ident).then_inc(s["ot_ps"], 1)
                pe.wait_ge(s["ot_ev"], k + 1)
                for t in range(T):
                    mm(PS[:, t, 0:128], xT[:, tile(t)], A(o)).then_inc(s["wo_ps"], 1)

            rows_to_features(1, fused)
            self_attention(0)
            context_values(1)

            rows_to_features(2, xn)
            pe.wait_ge(s["xt_ev"], 2)
            mm(PS[:, 0, :], A("gate1"), xT[:, :]).then_inc(s["g_ps"], 1)
            context_values(2)
            pe.wait_ge(s["g_x"], 1)
            mm(PS[:, 1, 0:128], ones[:, :], mix[:, 0:128]).then_inc(s["g_bc_ps"], 1)
            pe.wait_ge(s["ld_w1"], 16)
            pe.wait_ge(s["vp_ev"], sum(len(v) for v in VALUES[:3]))
            for fc in range(FC):
                for e in range(E1):
                    if e and fc == 0:
                        pe.wait_ge(s["z_ready"], e)
                        pe.wait_ge(ld_ws[e - 1], 16)
                    last = mm(PS[:, 2 + fc, :], w1[:, FF * e + 128 * fc:FF * e + 128 * fc + 128],
                              zz[:, e - 1, :] if e else xT[:, :], start=(e == 0), stop=(e == E))
                last.then_inc(s["u_ps"], 1)
            pe.wait_ge(s["u_act"], FC)
            pe.wait_ge(s["ld_w2"], 16)
            for t in range(T):
                if t >= 2:
                    pe.wait_ge(s["y_used"], t - 1)
                for g in range(3):
                    for fc in range(FC):
                        last = mm(PS[:, Y_BANK[t % 2][g], 0:384], u[:, fc, tile(t)], w2[:, fc, 3 * g:3 * g + 3, :],
                                  start=(fc == 0), stop=(fc == FC - 1))
                    last.then_inc(s["y_ps"], 1)

            context_values(3)
            rows_to_features(3, xn)
            pe.wait_ge(s["xt_ev"], 3)
            for r in range(R):
                mm(PS[:, r, :], wa[:, A_WQR + 128 * r:A_WQR + 128 * r + 128], xT[:, :]).then_inc(s["lq_ps"], 1)
            pe.wait_ge(s["flag_ok"], 1)
            in_bounds = pe.value_load(flags[0:1, 0:1], min_val=0, max_val=1)

            def scores(i):
                b, r = i // R, i % R
                if i >= 3:
                    pe.wait_ge(s["ls_max"], i - 2)
                if b == 0:
                    pe.wait_ge(s["lq_e"], 2 * r + 2)
                    pe.wait_ge(s["lq_e2"], r + 1)
                    pe.wait_ge(s["lq_e3"], r + 1)
                mm(PS[:, S_BANK[i % 3], :], qe[0:96, r, b, :], kst[0:96, r, chunk(b)]).then_inc(s["ls_ps"], 1)

            def maxima_rows(b):
                pe.wait_ge(s["ls_parts"], b + 1)
                if b >= 1:
                    pe.wait_ge(s["ls_rows"], b)
                for r in range(R):
                    last = mm(PS[96:99, M_BANK, tile(r)], mparts[:, b % 2, r, :], identh[:, :])
                last.then_inc(s["ls_rows_ps"], 1)

            def transposed_scores(i):
                b, r = i // R, i % R
                pe.wait_ge(s["ls_rows"], b + 1)
                if i >= 2:
                    pe.wait_ge(s["lt_exp"], i - 1)

                def products(p0, p1, start):
                    for k in range(4):
                        last = mm(PS[:, ST_BANK[i % 2], tile(k)], kst[p0:p1, r, 512 * b + 128 * k:512 * b + 128 * k + 128],
                                  qe[p0:p1, r, b, :], start=start and k == 0, skip_group_check=True)
                    return last

                with pe.If(in_bounds == 0):
                    products(0, 96, True).then_inc(s["lt_raw"], 1)
                    pe.wait_ge(s["lt_clipped"], i + 1)
                    products(96, 99, False).then_inc(s["lt_ps"], 1)
                with pe.If(in_bounds != 0):
                    products(0, 99, True).then_inc(s["lt_ps"], 1)

            def outputs(b, k):
                if b % 2 == 0 and b >= 4 and k == 0:
                    pe.wait_ge(s["lo_sum"], b // 2 - 1)
                if k == 0:
                    pe.wait_ge(s["lt_exp"], R * b + R)
                bank = O_BANK[(b // 2) % 2]
                first = b % 2 == 0 and k == 0
                for r in range(R):
                    v0 = 512 * b + 128 * k + 32 * r
                    mm(PS[32 * r:32 * r + 32, bank, tile(b % 2)], cx[:, v0:v0 + 32],
                       pt(R * b + r)[:, tile(k)], start=first, stop=False, skip_group_check=True)
                for r in range(R):
                    last = mm(PS[32 * r:32 * r + 32, bank, tile(2 + b % 2)], ones[:, 0:32],
                              pt(R * b + r)[:, tile(k)], start=False, stop=(b % 2 == 1 and k == 3),
                              skip_group_check=True)
                if k == 3:
                    last.then_inc(s["lo_ps"], 1)

            pe.wait_ge(s["lq_ev"], R)
            pe.wait_ge(s["kst_done"], 3 * R * 16)
            pe.wait_ge(s["key_ones"], 1)
            pe.wait_ge(s["vp_ev"], NCH)
            for b in range(B + 4):
                for r in range(R):
                    if b < B:
                        scores(R * b + r)
                    if 2 <= b < B + 2:
                        transposed_scores(R * (b - 2) + r)
                    if r == 0 and b >= 4:
                        outputs(b - 4, 3)
                    elif r >= 1 and 3 <= b < B + 3:
                        outputs(b - 3, r - 1)
                    if r == 2 and 1 <= b <= B:
                        maxima_rows(b - 1)
            spread_max()
            pe.wait_ge(s["nan_ok"], 1)
            for t in range(T):
                mm(PS[:, t, 0:128], qTs[:, tile(t)], A("wo")).then_inc(s["wo_ps"], 1)

            rows_to_features(4, xn)
            self_attention(1)
            rows_to_features(5, xn)
            pe.wait_ge(s["xt_ev"], 5)
            for t in range(T):
                mm(PS[:, t, 0:128], xT[:, tile(t)], lin[:, :]).then_inc(s["fin_ps"], 1)


def _constants():
    c = np.zeros((128, C_END), np.float32)
    p = np.arange(128)
    c[:, C_ID:C_ID + 128] = np.eye(128)
    theta = (1.0 / 10000.0 ** (np.arange(64, dtype=np.float32) / 64)).astype(np.float32)
    ang = (p % S).astype(np.float32)[:, None] * theta[None, :]
    c[:, C_COS:C_COS + 64] = np.cos(ang)
    c[:, C_SIN:C_SIN + 64] = np.sin(ang)
    c[:, C_HM:C_HM + 4] = ((p // HD) % 4)[:, None] == np.arange(4)[None, :]
    c[:, C_RM:C_RM + 4] = (p // 32)[:, None] == np.arange(4)[None, :]
    later = (p % S)[None, :] > (p % S)[:, None]
    c[:, C_MK0:C_MK0 + 128] = later * -1e9
    c[:, C_MK1:C_MK1 + 128] = later * -1e12
    a = 2 * np.pi * ((p[:, None] * p[None, :]) % D) / D
    c[:, C_DC:C_DC + 128], c[:, C_DS:C_DS + 128] = np.cos(a), np.sin(a)
    c[:, C_DCN:C_DCN + 128], c[:, C_DSN:C_DSN + 128] = np.cos(a) / D, -np.sin(a) / D
    c[:, C_CNT:C_CNT + 7] = 1.0 / np.array(X_COUNT)
    return c


def _pad(a, rows=128):
    z = np.zeros((rows, a.shape[1]), np.float32)
    z[:a.shape[0]] = a
    return z


def kernel(**inputs):
    import concourse.bacc as _bacc
    from concourse import mybir as _mybir
    from concourse.bass_utils import run_bass_kernel_spmd as _run

    v = {k: np.asarray(a) for k, a in inputs.items()}
    X, SA0, F0 = "L0_xattn_", "L0_attn_", "L0_ffn_"
    X1, SA1, F1 = "L1_xattn_", "L1_attn_", "L1_ffn_"

    def rep_heads(w):
        return np.repeat(w.reshape(R, 1, HD, D), 4, axis=1).reshape(D, D).T

    wx = np.concatenate([_pad(v[X + "W_d2v"].T), v[X + "W_img"].T, v[X + "W_txt"].T, v[X + "W_att0"].T,
                         v[X + "W_att1"].T, v[X + "W_f1"].T[:128], v[X + "W_f1"].T[128:]]
                        + [v[X + "W_f2"].T[128 * c:128 * c + 128] for c in range(FC)], axis=1)
    wqr = np.tile(v[X1 + "Wq"].reshape(D, R, 1, 32), (1, 1, 4, 1)).reshape(D, 512)
    wa = np.concatenate(
        [v[SA0 + "W_q"].T, rep_heads(v[SA0 + "W_k"]), rep_heads(v[SA0 + "W_v"]), v[SA0 + "W_o"].T,
         v[F0 + "gate_w1"].T, v[X1 + "Wo"], v[SA1 + "Wq"], v[SA1 + "Wk"], v[SA1 + "Wv"], v[SA1 + "Wm"],
         v[F1 + "w_freq_real"], v[F1 + "w_freq_imag"],
         _pad(np.concatenate([v[X1 + "Wk"], v[X1 + "bk"][None]])), _pad(np.concatenate([v[X1 + "Wv"], v[X1 + "bv"][None]])),
         wqr, v[F0 + "gate_w2"].T], axis=1)
    w1 = np.concatenate([v[F0 + "W1"][None], v[F0 + "TW1"]]).transpose(2, 0, 1).reshape(D, E1 * FF)
    w2 = np.concatenate([v[F0 + "W2"][None], v[F0 + "TW2"]])
    w2 = w2.reshape(E1, D, FC, 128).transpose(3, 2, 0, 1).reshape(128, FC * E1 * D)
    tb1 = v[F0 + "Tb1"].reshape(E, FC, 128).transpose(2, 1, 0).reshape(128, FC * E)
    c1 = lambda a: a.reshape(-1, 128).T
    cols = np.concatenate([c1(v[X + "b_d2v"]), c1(v[X + "b_img"]),
                           c1(np.concatenate([v[X + "b_att0"], v[X + "b_att1"]])), c1(v[X + "b_f1"]),
                           c1(v[F0 + "gate_b1"]), np.zeros((128, 3), np.float32),
                           c1(np.tile(v[X1 + "bq"].reshape(R, 1, 32), (1, 4, 1)).reshape(512)),
                           c1(v[SA1 + "bq"]), c1(v[SA1 + "bk"]), c1(v[SA1 + "bv"]), c1(v[F0 + "b1"]), tb1], axis=1)
    assert cols.shape[1] == K_END
    a0, a1 = v[X + "b_att0"], v[X + "b_att1"]
    row = np.concatenate([v[X + "b_txt"], a0, a0, a1, a1, v[X + "b_f2"], v[X1 + "bo"], v[SA1 + "bm"], v[F1 + "bias"],
                          v[F0 + "b2"], v[F0 + "gate_b2"], v[X1 + "bq"], v[F0 + "Tb2"].reshape(-1)])
    assert row.shape[0] == R_END + E * D
    arrays = {
        "x_in": v["x"].reshape(N, D), "ctx_in": np.concatenate([v["ctx_768"].reshape(CP, DC).T, np.ones((1, CP), np.float32)]), "wx_in": wx, "wa_in": wa,
        "w1_in": w1, "w2_in": w2, "const_in": _constants(), "cols_in": cols, "rows_in": np.tile(row[None], (128, 1)),
    }
    arrays = {k: np.ascontiguousarray(a) for k, a in arrays.items()}
    nc = _bacc.Bacc("TRN2", target_bir_lowering=False, num_devices=1)
    args = [nc.dram_tensor(k, a.shape, _mybir.dt.float32, kind="ExternalInput").ap() for k, a in arrays.items()]
    args.append(nc.dram_tensor("out", (N, D), _mybir.dt.float32, kind="ExternalOutput").ap())
    perceiver(nc, *args)
    return _run(nc, [arrays], core_ids=[0]).results[0]["out"].reshape(B, S, D)
```

```python
import numpy as np
import concourse.bass as bass
from concourse import mybir
from contextlib import ExitStack

B, S, D = 16, 32, 128
P, DC = 512, 96
N = B * S
T = N // 128
CP = B * P
NCH = CP // 512
FF = 512
FC = FF // 128
E = 8
E1 = E + 1
H, HD = 16, 8
R = 4
LN_EPS = 1e-5
HEAD_SCALE = float(HD) ** -0.5
OFFSET = 1152.0
MAGIC = 1.5 * 2.0 ** 23 + 0x6400 + 128
ROUND = 1.5 * 2.0 ** 23
F16_TOP = 2048.0
MAX_FACTOR = 1024.0
MAX_FACTOR_PAIR = float(np.full(2, MAX_FACTOR, np.float16).view(np.float32)[0])
CLIP = 10000.0

X_COLS = {"d2v": (0, 128), "img": (128, 128), "txt": (256, 128), "att0": (384, 64),
          "att1": (448, 64), "f1": (512, 1024), "f2": (1536, 512)}
X_COUNT = [DC * D, D * D, D * D, D * 64, D * 64, 2 * D * FF, FF * D]
A_NAMES = ["q0", "k0", "v0", "o0", "gate1", "wo", "q1", "k1", "v1", "m1", "wr", "wi", "wk", "wv"]
A_COL = {n: 128 * i for i, n in enumerate(A_NAMES)}
A_WQR = 128 * len(A_NAMES)
A_G2 = A_WQR + 512
A_END = A_G2 + E
C_ID, C_COS, C_SIN = 0, 128, 192
C_HM, C_RM, C_MK0, C_MK1 = 256, 260, 264, 392
C_DC, C_DS, C_DCN, C_DSN, C_CNT = 520, 648, 776, 904, 1032
C_END = 1040
K_D2V, K_IMG, K_ATT, K_F1, K_G1, K_Z = 0, 1, 2, 3, 7, 8
K_BK, K_BV, K_BQR = 9, 10, 11
K_Q1, K_K1, K_V1 = 15, 16, 17
K_B1, K_TB1 = 18, 22
K_END = K_TB1 + FC * E
R_TXT, R_A0, R_A1, R_F2, R_BO, R_BM, R_FB, R_B2, R_G2 = (128 * i for i in range(9))
R_BQ = R_G2 + E
R_END = R_BQ + 128
Y_BANK = ((6, 7, 0), (1, 2, 3))


def perceiver(nc, x_in, ctx_in, wx_in, wa_in, w1_in, w2_in, const_in, cols_in, rows_in, out):
    f32, bf16, f16 = mybir.dt.float32, mybir.dt.bfloat16, mybir.dt.float16
    ALU, ACT, AX = mybir.AluOpType, mybir.ActivationFunctionType, mybir.AxisListType.X
    ctx = ExitStack()
    with ctx:
        def sb(name, shape, dt=f32):
            return ctx.enter_context(nc.sbuf_tensor(name, shape, dt))

        def sem(name):
            return ctx.enter_context(nc.semaphore(name))

        cx = sb("cx", [128, CP])
        yq = sb("yq", [128, CP])
        big = sb("big", [128, 2, CP])
        w1 = sb("w1", [128, E1 * FF])
        wa = sb("wa", [128, A_END])
        sa = sb("sa", [128, 2048 + B * R * 36])
        tern = sb("tern", [128, 2048], bf16)
        cst = sb("cst", [128, C_END])
        cols = sb("cols", [128, K_END])
        rows = sb("rows", [128, R_END])
        ones = sb("ones", [128, 128])
        identh = sb("identh", [128, 128], f16)
        mparts = sb("mparts", [128, 2, R, 3], f16)
        mrest = sb("mrest", [128, 2, R])
        identb = sb("identb", [128, 128], bf16)
        maskb = sb("maskb", [128, 2, 128], bf16)
        noff = sb("noff", [128, 128], bf16)
        x = sb("x", [128, T, D])
        xn = sb("xn", [128, T, D])
        tmp = sb("tmp", [128, T, D])
        fused = sb("fused", [128, T, D])
        xT = sb("xT", [128, N])
        qTs = sb("qTs", [128, N])
        bn = sb("bn", [128, T, 6])
        mv = sb("mv", [128, T, 2])
        veps = sb("veps", [128, T])
        rstd = sb("rstd", [128, T])
        mhalf = sb("mhalf", [128, T])
        sm = sb("sm", [128, 464])
        diag = sb("diag", [128, 128])
        avg = sb("avg", [128, B])
        avgq = sb("avgq", [128, B])
        avgb = sb("avgb", [128, B], bf16)
        qb = sb("qb", [128, T, D], bf16)
        qT = sb("qT", [128, N], bf16)
        csum = sb("csum", [128, B])
        meanv = sb("meanv", [128, B])
        flags = sb("flags", [128, 2], mybir.dt.int32)
        gbc = sb("gbc", [128, E, B])
        gtok = sb("gtok", [128, T, E])
        mb1 = sb("mb1", [128, FC, B])
        mix = sb("mix", [128, 512])
        lin = sb("lin", [128, 128])
        PS = ctx.enter_context(nc.psum_tensor("PS", [128, 8, 512], f32))

        kv_off = xT[:, 0:128]
        wx = sa[:, 0:2048]
        ft = mix[:, 256:512].rearrange("p (a b) -> p a b", a=2)
        kexp = sa[:, 0:2048].rearrange("p (h n) -> p h n", h=4)
        vexp = sa[:, 2048:].rearrange("p (b r c) -> p b r c", b=B, r=R)
        zz = sa[:, 0:E * N].rearrange("p (e n) -> p e n", e=E)
        work = w1[:, FF:FF + 2048].rearrange("p (r n) -> p r n", r=4)
        wt = w1[:, FF + 2048:FF + 4096].rearrange("p (r n) -> p r n", r=4)
        xrep = w1[:, FF + 2048:FF + 4096]
        nd = w1[:, FF + 2048:FF + 3072].rearrange("p (v n) -> p v n", v=2)
        w2 = yq[:, 0:FC * E1 * D].rearrange("p (c e d) -> p c e d", c=FC, e=E1)
        u = yq[:, FC * E1 * D:FC * E1 * D + FC * N].rearrange("p (c n) -> p c n", c=FC)
        qe = yq[:, 0:4096].bitcast(f16).rearrange("p (r b n) -> p r b n", r=R, b=B)
        pt8 = yq[:, 4096:8192].rearrange("p (s n) -> p s n", s=8)
        pt4 = w1[:, FF:FF + 2048].rearrange("p (s n) -> p s n", s=4)
        tb2 = tern[:, :].bitcast(f32)
        qs16 = tern[:, :].bitcast(f16).rearrange("p (r n) -> p r n", r=R)
        y16 = yq[:, :].bitcast(f16).rearrange("p (n two) -> p n two", two=2)[:, :, 0]
        khl = yq[:, :].bitcast(f16).rearrange("p (two n) -> p two n", two=2)
        kst = big[:, :, :].rearrange("p a n -> p (a n)").bitcast(f16).rearrange("p (r n) -> p r n", r=R)
        ident = cst[:, C_ID:C_ID + 128]
        hm = cst[:, C_HM:C_HM + 4]
        rm = cst[:, C_RM:C_RM + 4]

        M_V, M_G, M_SI, M_INV = 0, 20, 30, 40
        M_ABS, M_WS, M_TH, M_NTH = 50, 58, 66, 74
        M_SC = 82
        M_NMX, M_DEN, M_RD = 96, 104, 112
        M_Z4, M_RD64 = 124, 128
        M_AL, M_BE, M_ES, M_BKS, M_BQS, M_QB = 192, 193, 194, 195, 196, 200
        M_ABC = 204
        M_MX = 208
        M_HM = 224
        M_MAG, M_WA = 250, 251
        M_SAM = 256
        M_BND = 320
        M_LO, M_HI = M_BND + 6, M_BND + 7
        M_NAN = 336

        S_BANK, ST_BANK, M_BANK, O_BANK = (0, 1, 2), (3, 4), 7, (5, 6)

        def s1(i, n=1):
            return sm[:, i:i + n]

        KEYS_AFTER_ROUND = (((2, 2), (3, 3)), ((6, 2), (7, 3), (8, 4), (9, 5)))
        KEYS_IN_FF = ((10, 4), (11, 6), (12, 0), (13, 1), (14, 2), (15, 3))
        VALUES = (tuple((c, c % 4) for c in range(8)),
                  tuple((c, 4 + (c - 8) % 3) for c in range(8, 11)),
                  tuple((c, 5 + c % 2) for c in range(11, NCH)))
        LAG_T, LAG_O, ROWS_AT = 8, 13, 2
        VALUE_STEPS = [(b, r) for b in range(3) for r in range(1, R)][:len(VALUES[2])]

        P_BANK = (4, 6)
        MIX_BANK = (6, 7, 4, 5)

        def pt(i):
            return pt8[:, i % 12, :] if i % 12 < 8 else pt4[:, i % 12 - 8, :]

        def head_queries(r, h):
            return qe[0:96, r, :, 32 * h:32 * h + 32]

        def split_queries(r):
            return qs16[0:96, r, :].rearrange("p (b q) -> p b q", q=S)

        def col(i, n=1):
            return cols[:, i:i + n]

        def row(i, n=128):
            return rows[:, i:i + n]

        def A(name, p=128):
            return wa[0:p, A_COL[name]:A_COL[name] + 128]

        def TW(name):
            c, n = X_COLS[name]
            return tern[:, c:c + n]

        names = ["ld_x", "ld_wx", "ld_wa", "ld_w1", "ld_w2", "ld_cst", "ld_cols", "ld_rows", "ld_tb2", "kst_done",
                 "out_done", "consts", "casts", "wabs", "ws_ps", "ln_veps", "ln_rstd", "ln_out", "gm_diag", "gm_ps",
                 "ternary", "txt_q", "txt_tp", "txt_qT", "txt_ps", "fk_tok", "fk_tp", "fkT",
                 "scale_ready", "f2_scale", "vp_ev", "ft_ok", "ctx_sums", "clip_step", "flag_ok", "nan_ok", "quant_dve", "quant_act", "quant_pool", "ctx_mm", "ctx_ev",
                 "kv_off_ps", "kv_mm", "kv_ev", "sc_ps", "sc_max", "sc_exp", "sc_tp", "sc_tev", "sc_teva", "pv_ps", "pv_read",
                 "f1_in", "f1_tp", "f1_qT", "f1_ps", "f1_ev", "f2_qd", "f2_qa", "f2_ps", "x_up", "x_tile", "x_done", "k_plain", "k_evp",
                 "xt_ps", "xt_ev", "xrep_ok", "qk_ps", "q_ev", "k_evd", "k_eva", "v_ps", "v_ev", "vones", "sa_ps", "sa_sub", "sa_exp",
                 "sa_tp", "sa_tevd", "sa_teva", "sa_pv", "sa_o", "ot_ps", "ot_ev", "wo_ps",
                 "g_ps", "g_relu", "g_x", "g_bc_ps", "z_ready", "u_ps", "u_pre", "u_act", "y_ps", "y_used",
                 "kp_ps", "kp_h", "kp_l", "vp_ps", "bound_in", "bound_ps", "scales_ok", "root_in", "root",
                 "lq_ps", "lq_ev", "lq_low", "lq_e", "lq_e2", "lq_e3", "key_ones", "ls_ps", "ls_max", "ls_parts", "split", "sum_step", "ls_rows_ps", "ls_rows", "lt_raw", "lt_clipped",
                 "lt_ps", "lt_exp", "lo_ps", "den_sum", "nan_marks", "nan_max",
                 "ft_ps", "lin_ps", "lin_ok", "fin_ps", "dve_link", "act_link", "pool_link"]

        s = {n: sem(n) for n in names}
        ld_ws = [sem(f"ld_ws{e}") for e in range(1, E1)]
        ld_ctx = [sem(f"ld_ctx{i}") for i in range(8)]
        block = ctx.enter_context(nc.Block())

        def chunk(c):
            return slice(512 * c, 512 * c + 512)

        def tile(t):
            return slice(128 * t, 128 * t + 128)

        @block.sync
        def _(sp):
            sp.dma_start(x[:, :, :], x_in.rearrange("(t p) d -> p t d", p=128)).then_inc(s["ld_x"], 16)
            sp.dma_start(cst[:, :], const_in).then_inc(s["ld_cst"], 16)
            sp.dma_start(wx, wx_in).then_inc(s["ld_wx"], 16)
            sp.dma_start(cols[:, :], cols_in).then_inc(s["ld_cols"], 16)
            w = CP // 8
            for i in range(8):
                sp.dma_start(cx[0:DC + 1, i * w:(i + 1) * w], ctx_in[:, i * w:(i + 1) * w]).then_inc(ld_ctx[i], 16)
            sp.dma_start(rows[:, :], rows_in[:, 0:R_END]).then_inc(s["ld_rows"], 16)
            sp.dma_start(wa[:, :], wa_in).then_inc(s["ld_wa"], 16)
            sp.dma_start(w1[:, 0:FF], w1_in[:, 0:FF]).then_inc(s["ld_w1"], 16)
            sp.wait_ge(s["f2_ps"], 1)
            sp.dma_start(tb2, rows_in[:, R_END:R_END + E * D]).then_inc(s["ld_tb2"], 16)
            sp.wait_ge(s["pv_ps"], 2 * T)
            sp.wait_ge(s["kp_h"], NCH)
            sp.wait_ge(s["kp_l"], NCH)
            for r in range(R):
                for part in range(3):
                    sp.dma_start(kst[32 * part:32 * part + 32, r, :],
                                 khl[32 * r:32 * r + 32, part % 2, :]).then_inc(s["kst_done"], 16)
            sp.wait_ge(s["kst_done"], 3 * R * 16)
            sp.dma_start(w2, w2_in.rearrange("p (c e d) -> p c e d", c=FC, e=E1)).then_inc(s["ld_w2"], 16)
            sp.wait_ge(s["sa_pv"], 1)
            for e in range(1, E1):
                sp.dma_start(w1[:, e * FF:(e + 1) * FF], w1_in[:, e * FF:(e + 1) * FF]).then_inc(ld_ws[e - 1], 16)
            for t in range(T):
                sp.wait_ge(s["x_done"], t + 1)
                sp.dma_start(out[128 * t:128 * t + 128, :], x[:, t, :]).then_inc(s["out_done"], 16)
            sp.wait_ge(s["out_done"], 16 * T)

        @block.gpsimd
        def _(pool):
            links = [0]

            def link(ins):
                links[0] += 1
                ins.then_inc(s["pool_link"], 1)
                pool.wait_ge(s["pool_link"], links[0])

            def rstd_of(n):
                pool.wait_ge(s["ln_veps"], n + 1)
                pool.tensor_tensor(rstd[:, :], veps[:, :], mhalf[:, :], ALU.pow).then_inc(s["ln_rstd"], 1)

            pool.memset(mhalf[:, :], -0.5)
            link(pool.memset(sm[:, :], 0.0))
            pool.memset(s1(M_MAG), MAGIC)
            pool.memset(s1(M_QB + 2), 0.5)
            pool.memset(noff[:, :], -OFFSET)
            pool.memset(ones[:, :], 1.0).then_inc(s["consts"], 1)
            rstd_of(0)
            pool.wait_ge(s["ld_cst"], 16)
            pool.tensor_copy(identb[:, :], ident)
            pool.tensor_copy(identh[:, :], ident)
            pool.tensor_copy(maskb[:, :, :], cst[:, C_MK0:C_MK0 + 256].rearrange("p (a b) -> p a b", a=2))\
                .then_inc(s["casts"], 1)

            def quantise(layer, src, pn):
                pool.wait_ge(s["scale_ready"], layer + 1)
                for c in range(1, NCH, 4):
                    pool.tensor_scalar(yq[0:pn, chunk(c)], src[0:pn, chunk(c)], sm[0:pn, M_INV + layer:M_INV + layer + 1],
                                       MAGIC, ALU.mult, ALU.add).then_inc(s["quant_pool"], 1)

            def last_keys_head(k):
                pool.wait_ge(s["k_plain"], k + 1)
                pool.tensor_scalar(kexp[:, 3, :], mix[:, :], hm[:, 3:4], 1.0, ALU.mult, ALU.mult).then_inc(s["k_evp"], 1)

            def value_ones(k):
                for b in range(B):
                    last = pool.tensor_copy(vexp[:, b, :, 32:36], rm.unsqueeze(1).broadcast_to([128, R, 4]))
                last.then_inc(s["vones"], 1)

            quantise(0, cx, DC)
            quantise(1, big[:, 0, :], 128)
            quantise(2, big[:, 0, :], 128)
            pool.wait_ge(s["root_in"], 1)
            pool.tensor_tensor(s1(M_QB + 1), s1(M_QB), s1(M_QB + 2), ALU.pow).then_inc(s["root"], 1)
            value_ones(0)
            rstd_of(1)
            last_keys_head(0)
            pool.wait_ge(s["pv_ps"], 2 * T)
            pool.wait_ge(s["k_evp"], 1)
            link(pool.memset(big[96:99, 0, :], MAX_FACTOR_PAIR))
            rstd_of(2)
            pool.wait_ge(s["ln_rstd"], 3)
            pool.memset(big[96:99, 1, :], MAX_FACTOR_PAIR).then_inc(s["key_ones"], 1)
            pool.wait_ge(s["key_ones"], 1)
            pool.wait_ge(s["u_ps"], FC)
            value_ones(1)
            rstd_of(3)
            for r in range(R):
                pool.wait_ge(s["lq_low"], r + 1)
                pool.tensor_scalar(head_queries(r, 3), split_queries(r), hm[0:96, 3:4], 1.0, ALU.mult, ALU.mult)\
                    .then_inc(s["lq_e3"], 1)
            rstd_of(4)
            last_keys_head(1)
            rstd_of(5)

        @block.scalar
        def _(act):
            links = [0]

            def link(ins):
                links[0] += 1
                ins.then_inc(s["act_link"], 1)
                act.wait_ge(s["act_link"], links[0])

            def affine(o, i, scale=1.0, bias=0.0, func=ACT.Identity, **kw):
                return nc.scalar.activation(o, i, func, bias=bias, scale=scale, **kw)

            act.wait_ge(s["ld_wx"], 16)
            act.wait_ge(s["consts"], 1)
            for n, (c, w) in enumerate(X_COLS.values()):
                last = nc.scalar.activation(big[:, 0, c:c + w], wx[:, c:c + w], ACT.Abs, accum_out=s1(M_ABS + n))
            last.then_inc(s["wabs"], 1)

            def quantise(layer, src, pn):
                act.wait_ge(s["scale_ready"], layer + 1)
                for c in range(3, NCH, 4):
                    affine(yq[0:pn, chunk(c)], src[0:pn, chunk(c)], scale=sm[0:pn, M_INV + layer:M_INV + layer + 1],
                           bias=sm[0:pn, M_MAG:M_MAG + 1]).then_inc(s["quant_act"], 1)

            def ctx_evacuate(layer, bias, with_sum=False):
                for c in range(NCH):
                    act.wait_ge(s["ctx_mm"], NCH * layer + c + 1)
                    kw = {"accum_out": avg[:, c:c + 1]} if with_sum else {}
                    affine(big[:, 0, chunk(c)], PS[:, c % 4, :], scale=s1(M_SC + layer), bias=bias, **kw)\
                        .then_inc(s["ctx_ev"], 1)

            for b in range(B):
                act.wait_ge(ld_ctx[b // 2], 16)
                last = affine(big[0:DC + 1, 1, chunk(b)], cx[0:DC + 1, chunk(b)], accum_out=csum[0:DC + 1, b:b + 1])
            last.then_inc(s["ctx_sums"], 1)
            quantise(0, cx, DC)
            act.wait_ge(s["ld_cols"], 16)
            ctx_evacuate(0, col(K_D2V))
            act.wait_ge(s["ld_wa"], 16)
            nc.scalar.activation(mix[:, 0:128], A("wk"), ACT.Abs)
            nc.scalar.activation(mix[:, 128:256].rearrange("p (r n) -> p r n", r=R),
                                 wa[:, A_WQR:A_WQR + 512].rearrange("p (r n) -> p r n", r=R)[:, :, 0:32],
                                 ACT.Square).then_inc(s["bound_in"], 1)
            act.wait_ge(s["ft_ps"], 1)
            nc.scalar.copy(ft[:, 0, :], PS[:, 4, 0:128])
            affine(ft[:, 1, :], PS[:, 4, 128:256], scale=-1.0).then_inc(s["ft_ok"], 1)
            act.wait_ge(s["txt_tp"], 1)
            nc.scalar.copy(qT[:, :], PS[:, 6, 0:256].bitcast(bf16)).then_inc(s["txt_qT"], 1)
            quantise(1, big[:, 0, :], 128)
            ctx_evacuate(1, col(K_IMG), True)
            act.wait_ge(s["lin_ps"], 1)
            nc.scalar.copy(lin[:, :], PS[:, 6, 384:512]).then_inc(s["lin_ok"], 1)
            quantise(2, big[:, 0, :], 128)
            ctx_evacuate(2, col(K_ATT))

            def key_high(c, bank):
                act.wait_ge(s["kp_ps"], c + 1)
                affine(khl[:, 0, chunk(c)], PS[:, bank, :], scale=s1(M_AL)).then_inc(s["kp_h"], 1)

            act.wait_ge(s["scales_ok"], 1)
            for j in range(2):
                act.wait_ge(s["fk_tp"], j + 1)
                affine(xT[:, :], PS[:, 7, :], scale=float(D) ** -0.5).then_inc(s["fkT"], 1)
                for t in range(T):
                    act.wait_ge(s["sc_max"], T * j + t + 1)
                    if j:
                        act.wait_ge(s["sc_tp"], t + 1)
                    nc.scalar.activation(work[:, t, :], PS[:, t, :], ACT.Exp, bias=s1(M_NMX + t),
                                         accum_out=s1(M_DEN + t)).then_inc(s["sc_exp"], 1)
                for t in range(1, T, 2):
                    act.wait_ge(s["sc_tp"], T * j + t + 1)
                    nc.scalar.copy(wt[:, t, :], PS[:, 4 + t % 2, :]).then_inc(s["sc_teva"], 1)
                    key_high(4 * j + t // 2, t // 2)
                for c, bank in KEYS_AFTER_ROUND[j]:
                    key_high(c, bank)

            act.wait_ge(s["f1_tp"], 1)
            nc.scalar.copy(qT[:, :], PS[:, 6, 0:256].bitcast(bf16)).then_inc(s["f1_qT"], 1)
            for fc in range(FC):
                act.wait_ge(s["f1_ps"], fc + 1)
                affine(work[:, fc, :], PS[:, fc, :], scale=s1(M_SC + 5), bias=col(K_F1 + fc), func=ACT.Relu)\
                    .then_inc(s["f1_ev"], 1)
            for c, bank in KEYS_IN_FF[:2]:
                key_high(c, bank)
            act.wait_ge(s["f2_scale"], 1)
            for fc in (1, 3):
                affine(wt[:, fc, :], work[:, fc, :], scale=s1(M_INV + 6), bias=s1(M_MAG)).then_inc(s["f2_qa"], 1)
            for c, bank in KEYS_IN_FF[2:]:
                key_high(c, bank)

            def context_values(part, step=None):
                for c, bank in VALUES[part] if step is None else VALUES[part][step:step + 1]:
                    act.wait_ge(s["vp_ps"], c + 1)
                    nc.scalar.copy(cx[:, chunk(c)], PS[:, bank, :]).then_inc(s["vp_ev"], 1)

            context_values(0)

            def rows_to_features(n):
                act.wait_ge(s["xt_ps"], n)
                nc.scalar.copy(xT[:, :], PS[:, 7, :]).then_inc(s["xt_ev"], 1)

            def self_attention(k):
                act.wait_ge(s["qk_ps"], 2 * k + 1)
                affine(qTs[:, :], PS[:, 4, :], bias=col(K_Q1) if k else 0.0).then_inc(s["q_ev"], 1)
                act.wait_ge(s["k_plain"], k + 1)
                affine(kexp[:, 2, :], mix[:, :], scale=hm[:, 2:3]).then_inc(s["k_eva"], 1)

                def values(half):
                    act.wait_ge(s["v_ps"], 2 * k + half + 1)
                    b0 = 8 * (1 - half)
                    src = PS[:, 4 + b0 // 4:6 + b0 // 4, :].rearrange("p a (b r c) -> p (a b) r c", b=4, r=R)
                    for h in range(4):
                        affine(vexp[:, b0:b0 + 8, :, 8 * h:8 * h + 8], src[:, :, :, 8 * h:8 * h + 8],
                               scale=rm[:, h:h + 1]).then_inc(s["v_ev"], 1)

                values(0)
                for r in range(R):
                    act.wait_ge(s["sa_sub"], R * k + r + 1)
                    nc.scalar.activation(work[:, r, :], work[:, r, :], ACT.Exp, scale=HEAD_SCALE)\
                        .then_inc(s["sa_exp"], 1)
                for r in (1, 3):
                    act.wait_ge(s["sa_tp"], R * k + r + 1)
                    nc.scalar.copy(wt[:, r, :], PS[:, r, :]).then_inc(s["sa_teva"], 1)
                    if r == 1:
                        values(1)
                act.wait_ge(s["ot_ps"], k + 1)
                affine(xT[:, :], PS[:, 6, :], bias=col(K_V1) if k else 0.0).then_inc(s["ot_ev"], 1)

            rows_to_features(1)
            self_attention(0)
            context_values(1)
            rows_to_features(2)
            act.wait_ge(s["g_ps"], 1)
            affine(fused[:, :, :].rearrange("p t d -> p (t d)"), PS[:, 0, :], bias=col(K_G1), func=ACT.Relu)\
                .then_inc(s["g_relu"], 1)
            for fc in range(FC):
                act.wait_ge(s["u_pre"], fc + 1)
                nc.scalar.activation(u[:, fc, :], u[:, fc, :], ACT.Gelu_apprx_tanh).then_inc(s["u_act"], 1)
            rows_to_features(3)
            for r in range(R):
                act.wait_ge(s["lq_ps"], r + 1)
                affine(kexp[:, r, :], PS[:, r, :], scale=s1(M_BE), bias=s1(M_BQS + r)).then_inc(s["lq_ev"], 1)
            for r in range(R):
                act.wait_ge(s["lq_low"], r + 1)
                affine(head_queries(r, 2), split_queries(r), scale=hm[0:96, 2:3]).then_inc(s["lq_e2"], 1)

            for n in range(R * B + LAG_T):
                b, r = n // R, n % R
                if (b, r) in VALUE_STEPS:
                    context_values(2, VALUE_STEPS.index((b, r)))
                i = n - LAG_T
                if i >= 0:
                    act.wait_ge(s["lt_ps"], i + 1)
                    if i >= 12:
                        act.wait_ge(s["lo_ps"], i // R - 2)
                    nc.scalar.activation(pt(i), PS[:, ST_BANK[i % 2], :], ACT.Exp, scale=s1(M_ES))\
                        .then_inc(s["lt_exp"], 1)
                if r == ROWS_AT and 1 <= b <= B:
                    act.wait_ge(s["ls_rows_ps"], b)
                    nc.scalar.copy(qe[96:99, :, b - 1, :], PS[96:99, M_BANK, :].rearrange("p (r n) -> p r n", r=R))\
                        .then_inc(s["ls_rows"], 1)
            rows_to_features(4)
            self_attention(1)
            rows_to_features(5)

        @block.vector
        def _(dve):
            V = nc.vector
            links = [0]

            def link(ins):
                links[0] += 1
                ins.then_inc(s["dve_link"], 1)
                dve.wait_ge(s["dve_link"], links[0])

            def layer_norm(n, out_tile, done=None, product=None, stats=True):
                for t in range(T if stats else 0):
                    if product is not None:
                        ps_sem, k = product
                        dve.wait_ge(ps_sem, T * k + t + 1)
                        V.tensor_tensor(x[:, t, :], x[:, t, :], PS[:, t, 0:128], ALU.add).then_inc(s["x_tile"], 1)
                        n_tiles[0] += 1
                        if t:
                            dve.wait_ge(s["x_tile"], n_tiles[0] - 1)
                            V.bn_stats(bn[:, t - 1, :], x[:, t - 1, :])
                        if t == T - 1:
                            dve.wait_ge(s["x_tile"], n_tiles[0])
                            last = V.bn_stats(bn[:, t, :], x[:, t, :])
                    else:
                        last = V.bn_stats(bn[:, t, :], x[:, t, :])
                if stats:
                    link(last)
                for t in range(T):
                    last = V.bn_aggr(mv[:, t, :], bn[:, t, :])
                link(last)
                V.tensor_scalar(veps[:, :], mv[:, :, 1], LN_EPS, None, ALU.add).then_inc(s["ln_veps"], 1)
                dve.wait_ge(s["ln_rstd"], n + 1)
                for t in range(T):
                    last = V.tensor_scalar(out_tile[:, t, :], x[:, t, :], mv[:, t, 0:1], rstd[:, t:t + 1],
                                           ALU.subtract, ALU.mult)
                    if done is not None:
                        last.then_inc(done, 1)
                if done is None:
                    link(last)

            n_gmax, n_tiles = [0], [0]

            def maximum_of(i):
                n_gmax[0] += 1
                dve.wait_ge(s["gm_ps"], n_gmax[0])
                link(V.tensor_reduce(s1(M_G + i), PS[:, 7, 0:128], AX, ALU.max))

            def scales_of(i, ws):
                link(V.tensor_scalar(s1(M_SI + i), s1(M_G + i), 1e-8, 1.0 / 127.0, ALU.max, ALU.mult))
                V.tensor_tensor(s1(M_SC + i), s1(ws), s1(M_SI + i), ALU.mult)
                return V.reciprocal(s1(M_INV + i), s1(M_SI + i))

            def global_scale(i, ncols, ws, meanwhile=None):
                if ncols > 1:
                    link(V.tensor_reduce(s1(M_V + 18), s1(M_V, ncols), AX, ALU.max))
                v = s1(M_V + 18) if ncols > 1 else s1(M_V)
                V.tensor_scalar(diag[:, :], ident, v, None, ALU.mult).then_inc(s["gm_diag"], 1)
                if meanwhile is not None:
                    meanwhile()
                maximum_of(i)
                return scales_of(i, ws)

            dve.wait_ge(s["ld_x"], 16)
            dve.wait_ge(s["consts"], 1)
            layer_norm(0, xn)
            link(V.tensor_reduce(s1(M_V), xn[:, :, :].rearrange("p t d -> p (t d)"), AX, ALU.max,
                                 apply_absolute_value=True))
            dve.wait_ge(s["ld_cst"], 16)
            V.tensor_scalar(diag[:, :], ident, s1(M_V), None, ALU.mult).then_inc(s["gm_diag"], 1)

            def ctx_maxima(i0, i1):
                for i in range(i0, i1):
                    w = CP // 8
                    dve.wait_ge(ld_ctx[i], 16)
                    last = V.tensor_reduce(sm[0:DC, M_V + i:M_V + i + 1], cx[0:DC, i * w:(i + 1) * w], AX, ALU.max,
                                           apply_absolute_value=True)
                return last

            def ternary_of(which):
                for n, (c, w) in enumerate(X_COLS.values()):
                    if n in which:
                        last = V.tensor_scalar(tern[:, c:c + w], wx[:, c:c + w], s1(M_NTH + n), None, ALU.is_lt)
                link(last)
                for n, (c, w) in enumerate(X_COLS.values()):
                    if n in which:
                        V.scalar_tensor_tensor(tern[:, c:c + w], wx[:, c:c + w], s1(M_TH + n), tern[:, c:c + w],
                                               ALU.is_gt, ALU.subtract).then_inc(s["ternary"], 1)

            dve.wait_ge(s["gm_diag"], 1)
            link(V.memset(s1(M_V, 16), 0.0))
            ctx_maxima(0, 2)
            maximum_of(3)
            link(ctx_maxima(2, 8))

            def weight_scales():
                dve.wait_ge(s["ws_ps"], 1)
                link(V.tensor_tensor(s1(M_WS, 7), PS[:, 6, 0:7], cst[:, C_CNT:C_CNT + 7], ALU.mult))
                link(V.tensor_scalar(s1(M_WS, 7), s1(M_WS, 7), 1e-5, None, ALU.max))
                V.tensor_scalar(s1(M_TH, 7), s1(M_WS, 7), 0.5, None, ALU.mult)
                V.tensor_copy(sm[0:64, M_WA:M_WA + 1], sm[0:64, M_WS + 3:M_WS + 4])
                V.tensor_copy(sm[64:128, M_WA:M_WA + 1], sm[64:128, M_WS + 4:M_WS + 5])
                link(V.tensor_scalar(s1(M_NTH, 7), s1(M_WS, 7), -0.5, None, ALU.mult))
                ternary_of((0,))

            for layer in range(3):
                src, pn = (cx, DC) if layer == 0 else (big[:, 0, :], 128)
                if layer:
                    for c in range(NCH):
                        dve.wait_ge(s["ctx_ev"], NCH * (layer - 1) + c + 1)
                        last = V.tensor_reduce(s1(M_V + c), big[:, 0, chunk(c)], AX, ALU.max, apply_absolute_value=True)
                    link(last)
                last = global_scale(layer, 8 if layer == 0 else NCH, (M_WS, M_WS + 1, M_WA)[layer],
                                    weight_scales if layer == 0 else None)
                last.then_inc(s["scale_ready"], 1)
                dve.wait_ge(s["scale_ready"], layer + 1)
                for c in range(0, NCH, 2):
                    V.tensor_scalar(yq[0:pn, chunk(c)], src[0:pn, chunk(c)], sm[0:pn, M_INV + layer:M_INV + layer + 1],
                                    MAGIC, ALU.mult, ALU.add).then_inc(s["quant_dve"], 1)
                if layer == 0:
                    link(scales_of(3, M_WS + 2))
                    link(V.tensor_scalar(tmp[:, :, :], xn[:, :, :], s1(M_INV + 3), ROUND, ALU.mult, ALU.add))
                    V.tensor_scalar(qb[:, :, :], tmp[:, :, :], ROUND, None, ALU.subtract).then_inc(s["txt_q"], 1)
                    ternary_of((1, 2, 3, 4))
                elif layer == 1:
                    dve.wait_ge(s["kv_off_ps"], 1)
                    dve.wait_ge(s["ft_ok"], 1)
                    V.tensor_copy(kv_off, PS[:, 4, 256:384])
                    dve.wait_ge(s["txt_ps"], 1)
                    dve.wait_ge(s["ld_rows"], 16)
                    V.scalar_tensor_tensor(fused[:, :, :], PS[:, 5, :].rearrange("p (t d) -> p t d", t=T), s1(M_SC + 3),
                                           row(R_TXT).unsqueeze(1).broadcast_to([128, T, D]), ALU.mult, ALU.add)
            def bound_step(n):
                if n == 0:
                    V.tensor_reduce(s1(M_BND), PS[:, 6, 0:128], AX, ALU.max)
                    V.tensor_reduce(s1(M_BND + 1), PS[:, 6, 128:256], AX, ALU.max)
                    V.tensor_scalar(s1(M_BND + 3), s1(M_G), 1.0, None, ALU.max)
                    link(V.tensor_reduce(s1(M_BND + 2), row(R_BQ), AX, ALU.max, apply_absolute_value=True))
                elif n == 1:
                    V.tensor_tensor(s1(M_BND + 4), s1(M_BND), s1(M_BND + 3), ALU.mult)
                    V.tensor_scalar(s1(M_QB), s1(M_BND + 1), float(D), None, ALU.mult).then_inc(s["root_in"], 1)
                    V.tensor_scalar(meanv[:, :], PS[:, 6, 256:256 + B], 1.0 / P, None, ALU.mult)
                elif n == 2:
                    dve.wait_ge(s["root"], 1)
                    link(V.tensor_tensor(s1(M_BND + 5), s1(M_QB + 1), s1(M_BND + 2), ALU.add))
                    link(V.tensor_scalar(s1(M_BND + 4, 2), s1(M_BND + 4, 2), 1e-30, 1.0 / F16_TOP, ALU.max, ALU.mult))
                elif n == 3:
                    V.reciprocal(s1(M_AL, 2), s1(M_BND + 4, 2))
                    link(V.scalar_tensor_tensor(s1(M_ES), s1(M_BND + 4), HEAD_SCALE, s1(M_BND + 5),
                                                ALU.mult, ALU.mult))
                elif n == 4:
                    V.tensor_scalar(flags[:, 0:1], s1(M_ES), HD * F16_TOP ** 2, 0.99 * CLIP, ALU.mult, ALU.is_le)\
                        .then_inc(s["flag_ok"], 1)
                    V.tensor_scalar(s1(M_BQS, 4), col(K_BQR, 4), s1(M_BE), None, ALU.mult)
                    link(V.reciprocal(s1(M_HI), s1(M_ES)))
                elif n == 5:
                    link(V.tensor_scalar(s1(M_LO), s1(M_HI), -CLIP, None, ALU.mult))
                    V.tensor_scalar(s1(M_HI), s1(M_HI), CLIP, None, ALU.mult).then_inc(s["scales_ok"], 1)

            dve.wait_ge(s["bound_ps"], 1)
            dve.wait_ge(s["lin_ok"], 1)
            dve.wait_ge(s["ld_cols"], 16)
            for c in range(NCH):
                dve.wait_ge(s["kv_mm"], c + 1)
                V.tensor_tensor(big[:, 1, chunk(c)].rearrange("p (k n) -> p k n", k=4),
                                PS[:, 4 + c % 2, :].rearrange("p (k n) -> p k n", k=4),
                                kv_off.unsqueeze(1).broadcast_to([128, 4, 128]), ALU.add).then_inc(s["kv_ev"], 1)
                if c % 2:
                    bound_step(c // 2)

            def key_low(c, bank):
                dve.wait_ge(s["kp_h"], c + 1)
                V.scalar_tensor_tensor(khl[:, 1, chunk(c)], PS[:, bank, :], s1(M_AL), khl[:, 0, chunk(c)],
                                       ALU.mult, ALU.subtract).then_inc(s["kp_l"], 1)

            for j in range(2):
                if j:
                    V.memset(tmp[:, :, 0:64], 0.0)
                else:
                    V.memset(tmp[:, :, 64:128], 0.0)
                V.tensor_tensor(tmp[:, :, 64 * j:64 * j + 64], fused[:, :, 0:64], fused[:, :, 64:128], ALU.add)\
                    .then_inc(s["fk_tok"], 1)
                if j:
                    for c, bank in ((1, 1),) + KEYS_AFTER_ROUND[0]:
                        key_low(c, bank)
                for t in range(T):
                    dve.wait_ge(s["sc_ps"], T * j + t + 1)
                    V.tensor_reduce(s1(M_NMX + t), PS[:, t, :], AX, ALU.max, negate=True).then_inc(s["sc_max"], 1)
                dve.wait_ge(s["fk_tok"], j + 1)
                V.scalar_tensor_tensor(fused[:, :, :], row(R_A0 + 128 * j).unsqueeze(1).broadcast_to([128, T, D]), 0.1,
                                       fused[:, :, :], ALU.mult, ALU.add)
                for t in range(0, T, 2):
                    dve.wait_ge(s["sc_tp"], T * j + t + 1)
                    V.tensor_copy(wt[:, t, :], PS[:, 4 + t % 2, :]).then_inc(s["sc_tev"], 1)
                key_low(4 * j, 0)
                dve.wait_ge(s["sc_exp"], T * j + T)
                V.reciprocal(s1(M_RD, T), s1(M_DEN, T))
                link(V.tensor_tensor(s1(M_RD + 5), s1(M_WS + 3 + j), s1(M_SI + 2), ALU.mult))
                link(V.tensor_scalar(s1(M_RD, T), s1(M_RD, T), s1(M_RD + 5), 0.1, ALU.mult, ALU.mult))
                ternary_of((5 + j,))
                for t in range(T):
                    dve.wait_ge(s["pv_ps"], T * j + t + 1)
                    V.scalar_tensor_tensor(fused[:, t, :], PS[:, MIX_BANK[t], 0:128], s1(M_RD + t), fused[:, t, :],
                                           ALU.mult, ALU.add).then_inc(s["pv_read"], 1)
                dve.wait_ge(s["pv_read"], T * j + T)

            V.tensor_reduce(s1(M_V), fused[:, :, :].rearrange("p t d -> p (t d)"), AX, ALU.max, apply_absolute_value=True)
            link(V.tensor_scalar(avgq[:, :], avg[:, :], 1.0 / P, None, ALU.mult))
            link(V.tensor_reduce(s1(M_V + 1), avgq[:, :], AX, ALU.max, apply_absolute_value=True))
            link(global_scale(5, 2, M_WS + 5))
            V.tensor_scalar(avgq[:, :], avgq[:, :], s1(M_INV + 5), ROUND, ALU.mult, ALU.add)
            link(V.tensor_scalar(tmp[:, :, :], fused[:, :, :], s1(M_INV + 5), ROUND, ALU.mult, ALU.add))
            V.tensor_scalar(avgb[:, :], avgq[:, :], ROUND, None, ALU.subtract)
            V.tensor_scalar(qb[:, :, :], tmp[:, :, :], ROUND, None, ALU.subtract).then_inc(s["f1_in"], 1)
            for c, bank in ((5, 1),) + KEYS_AFTER_ROUND[1]:
                key_low(c, bank)
            V.tensor_tensor(x[:, :, :], x[:, :, :], row(R_F2).unsqueeze(1).broadcast_to([128, T, D]), ALU.add)
            for fc in range(FC):
                dve.wait_ge(s["f1_ev"], fc + 1)
                last = V.tensor_reduce(s1(M_V + fc), work[:, fc, :], AX, ALU.max)
            link(last)
            global_scale(6, FC, M_WS + 6).then_inc(s["f2_scale"], 1)
            dve.wait_ge(s["f2_scale"], 1)
            for fc in (0, 2):
                V.tensor_scalar(wt[:, fc, :], work[:, fc, :], s1(M_INV + 6), MAGIC, ALU.mult, ALU.add)\
                    .then_inc(s["f2_qd"], 1)
            for c, bank in KEYS_IN_FF:
                key_low(c, bank)
            dve.wait_ge(s["f2_ps"], 1)
            flat = "p t d -> p (t d)"
            V.scalar_tensor_tensor(x[:, :, :].rearrange(flat), PS[:, 5, :], s1(M_SC + 6), x[:, :, :].rearrange(flat),
                                   ALU.mult, ALU.add).then_inc(s["x_up"], 1)

            dve.wait_ge(s["x_up"], 1)
            layer_norm(1, xn)
            pair = xn[:, :, :].rearrange("p t (n two) -> p t n two", two=2)
            cos = cst[:, C_COS:C_COS + 64].unsqueeze(1).broadcast_to([128, T, 64])
            sin = cst[:, C_SIN:C_SIN + 64].unsqueeze(1).broadcast_to([128, T, 64])
            V.tensor_tensor(fused[:, :, 0:64], pair[:, :, :, 0], cos, ALU.mult)
            V.tensor_tensor(tmp[:, :, 0:64], pair[:, :, :, 1], sin, ALU.mult)
            V.tensor_tensor(fused[:, :, 64:128], pair[:, :, :, 0], sin, ALU.mult)
            link(V.tensor_tensor(tmp[:, :, 64:128], pair[:, :, :, 1], cos, ALU.mult))
            V.tensor_tensor(fused[:, :, 0:64], fused[:, :, 0:64], tmp[:, :, 0:64], ALU.subtract)
            V.tensor_tensor(fused[:, :, 64:128], fused[:, :, 64:128], tmp[:, :, 64:128], ALU.add).then_inc(s["ln_out"], T)

            def self_attention(k):
                dve.wait_ge(s["xt_ev"], (1, 4)[k])
                V.tensor_copy(xrep.rearrange("p (b h q) -> p b h q", b=B, h=4),
                              xT[:, :].rearrange("p (b q) -> p b q", q=S).unsqueeze(2).broadcast_to([128, B, 4, S]))\
                    .then_inc(s["xrep_ok"], 1)
                dve.wait_ge(s["qk_ps"], 2 * k + 2)
                V.tensor_scalar(mix[:, :], PS[:, 5, :], col(K_K1) if k else s1(M_Z4), None, ALU.add)\
                    .then_inc(s["k_plain"], 1)
                dve.wait_ge(s["k_plain"], k + 1)
                for h in (0, 1):
                    V.tensor_scalar(kexp[:, h, :], mix[:, :], hm[:, h:h + 1], None, ALU.mult).then_inc(s["k_evd"], 1)
                for r in range(R):
                    dve.wait_ge(s["sa_ps"], R * k + r + 1)
                    mx = s1(M_SAM + 16 * r, 16)
                    sc = PS[:, r, :].rearrange("p (g n) -> p g n", n=S)
                    link(V.tensor_reduce(mx, sc, AX, ALU.max))
                    V.tensor_tensor(work[:, r, :].rearrange("p (g n) -> p g n", n=S), sc,
                                    mx.unsqueeze(2).broadcast_to([128, 16, S]), ALU.subtract).then_inc(s["sa_sub"], 1)
                for r in (0, 2):
                    dve.wait_ge(s["sa_tp"], R * k + r + 1)
                    V.tensor_copy(wt[:, r, :], PS[:, r, :]).then_inc(s["sa_tevd"], 1)
                dve.wait_ge(s["sa_pv"], k + 1)
                pv = [PS[:, P_BANK[a], 0:288].rearrange("p (g c) -> p g c", c=36) for a in range(2)]
                for a in range(2):
                    last = V.reciprocal(s1(M_RD64 + 32 * a, 32).rearrange("p (g h) -> p g h", h=4), pv[a][:, :, 32:36])
                link(last)
                for a in range(2):
                    rd = s1(M_RD64 + 32 * a, 32).rearrange("p (g h) -> p g h", h=4).unsqueeze(3)\
                        .broadcast_to([128, 8, 4, HD])
                    last = V.tensor_tensor(tmp[:, 2 * a:2 * a + 2, :].rearrange("p t (r h d) -> p (t r) h d", r=R, h=4),
                                           pv[a][:, :, 0:32].rearrange("p g (h d) -> p g h d", h=4), rd, ALU.mult)
                last.then_inc(s["sa_o"], 1)

            def add_bias(r):
                link(V.tensor_tensor(x[:, :, :], x[:, :, :], row(r).unsqueeze(1).broadcast_to([128, T, D]), ALU.add))

            self_attention(0)

            layer_norm(2, xn, s["ln_out"], (s["wo_ps"], 0))
            dve.wait_ge(s["g_relu"], 1)
            link(V.tensor_reduce(s1(M_HM, 16), fused[:, :, :].rearrange("p t (b q) -> p (t b) q", q=S), AX, ALU.add))
            V.tensor_tensor(mix[:, 0:128].rearrange("p (e b) -> p e b", e=E),
                            wa[:, A_G2:A_G2 + E].unsqueeze(2).broadcast_to([128, E, B]),
                            s1(M_HM, 16).unsqueeze(1).broadcast_to([128, E, B]), ALU.mult).then_inc(s["g_x"], 1)
            dve.wait_ge(s["g_bc_ps"], 1)
            link(V.scalar_tensor_tensor(gbc[:, :, :], PS[:, 1, 0:128].rearrange("p (e b) -> p e b", e=E), 1.0 / S,
                                        row(R_G2, E).unsqueeze(2).broadcast_to([128, E, B]), ALU.mult, ALU.add))
            for e in range(E):
                V.tensor_tensor(zz[:, e, :].rearrange("p (b q) -> p b q", q=S), xT[:, :].rearrange("p (b q) -> p b q", q=S),
                                gbc[:, e, :].unsqueeze(2).broadcast_to([128, B, S]), ALU.mult).then_inc(s["z_ready"], 1)
            be = "p (c b e) -> p c b e"
            link(V.tensor_tensor(mix[:, :].rearrange(be, c=FC, b=B),
                                 gbc[:, :, :].rearrange("p e b -> p b e").unsqueeze(1).broadcast_to([128, FC, B, E]),
                                 col(K_TB1, FC * E).rearrange("p (c e) -> p c e", c=FC).unsqueeze(2)
                                 .broadcast_to([128, FC, B, E]), ALU.mult))
            link(V.tensor_reduce(mb1[:, :, :], mix[:, :].rearrange(be, c=FC, b=B), AX, ALU.add))
            link(V.tensor_tensor(mb1[:, :, :], mb1[:, :, :], col(K_B1, FC).unsqueeze(2).broadcast_to([128, FC, B]), ALU.add))
            te = "p (t e b) -> p t e b"
            link(V.tensor_tensor(mix[:, 0:128].rearrange(te, t=T, e=E),
                                 gbc[:, :, :].rearrange("p e (t b) -> p t e b", t=T),
                                 rm.unsqueeze(1).unsqueeze(1).broadcast_to([128, T, E, 4]), ALU.mult))
            link(V.tensor_reduce(gtok[:, :, :], mix[:, 0:128].rearrange(te, t=T, e=E), AX, ALU.add))
            add_bias(R_B2)
            dve.wait_ge(s["ld_tb2"], 16)
            for e in range(E):
                for t in range(T):
                    last = V.scalar_tensor_tensor(x[:, t, :], tb2[:, tile(e)], gtok[:, t, e:e + 1], x[:, t, :],
                                                  ALU.mult, ALU.add)
                link(last)
                if e % 2:
                    fc = e // 2
                    dve.wait_ge(s["u_ps"], fc + 1)
                    V.tensor_tensor(u[:, fc, :].rearrange("p (b q) -> p b q", q=S),
                                    PS[:, 2 + fc, :].rearrange("p (b q) -> p b q", q=S),
                                    mb1[:, fc, :].unsqueeze(2).broadcast_to([128, B, S]), ALU.add).then_inc(s["u_pre"], 1)
            for t in range(T):
                for g in range(3):
                    dve.wait_ge(s["y_ps"], 3 * t + g + 1)
                    for n in range(3):
                        e = 3 * g + n
                        ps = PS[:, Y_BANK[t % 2][g], 128 * n:128 * n + 128]
                        if e == 0:
                            last = V.tensor_tensor(x[:, t, :], ps, x[:, t, :], ALU.add)
                        else:
                            last = V.scalar_tensor_tensor(x[:, t, :], ps, gtok[:, t, e - 1:e], x[:, t, :],
                                                          ALU.mult, ALU.add)
                        link(last)
                V.bn_stats(bn[:, t, :], x[:, t, :]).then_inc(s["y_used"], 1)
            dve.wait_ge(s["y_used"], T)

            layer_norm(3, xn, s["ln_out"], stats=False)
            dve.wait_ge(s["ln_out"], 3 * T)
            add_bias(R_BO)
            for r in range(R):
                dve.wait_ge(s["lq_ev"], r + 1)
                link(V.tensor_copy(qs16[0:96, r, :], kexp[0:96, r, :]))
                V.tensor_tensor(qs16[64:96, r, :], kexp[64:96, r, :], qs16[64:96, r, :], ALU.subtract).then_inc(s["lq_low"], 1)
                dve.wait_ge(s["lq_low"], r + 1)
                for h in (0, 1):
                    V.tensor_scalar(head_queries(r, h), split_queries(r), hm[0:96, h:h + 1], None, ALU.mult)\
                        .then_inc(s["lq_e"], 1)

            dve.wait_ge(s["flag_ok"], 1)
            in_bounds = dve.value_load(flags[0:1, 0:1], min_val=0, max_val=1)

            def clip(i):
                sc = PS[:, S_BANK[i % 3], :]
                V.tensor_copy(mix[:, :], sc).then_inc(s["clip_step"], 1)
                dve.wait_ge(s["clip_step"], 3 * i + 1)
                V.tensor_tensor(mix[:, :], mix[:, :], mix[:, :], ALU.not_equal).then_inc(s["clip_step"], 1)
                dve.wait_ge(s["clip_step"], 3 * i + 2)
                V.tensor_reduce(s1(M_NAN + 64 + i), mix[:, :], AX, ALU.max)
                V.tensor_scalar(sc, sc, s1(M_LO), s1(M_HI), ALU.max, ALU.min).then_inc(s["clip_step"], 1)
                dve.wait_ge(s["clip_step"], 3 * i + 3)

            def clip_transposed(i):
                dve.wait_ge(s["lt_raw"], i + 1)
                sc = PS[:, ST_BANK[i % 2], :]
                V.tensor_scalar(sc, sc, s1(M_LO), s1(M_HI), ALU.max, ALU.min).then_inc(s["lt_clipped"], 1)

            def split_maximum(b, n):
                k = b % 2
                mx, rest = s1(M_MX + R * k, R), mrest[:, k, :]
                high, mid, low = (mparts[:, k, :, m] for m in range(3))
                if n == 0:
                    if b >= 2:
                        dve.wait_ge(s["ls_rows_ps"], b - 1)
                    V.tensor_scalar(high, mx, 1.0 / MAX_FACTOR, None, ALU.mult).then_inc(s["split"], 1)
                elif n == 1:
                    V.scalar_tensor_tensor(rest, mx, 1.0 / MAX_FACTOR, high, ALU.mult, ALU.subtract)\
                        .then_inc(s["split"], 1)
                elif n == 2:
                    V.tensor_copy(mid, rest).then_inc(s["split"], 1)
                else:
                    V.tensor_tensor(low, rest, mid, ALU.subtract).then_inc(s["ls_parts"], 1)

            def sum_heads(g, n):
                o = nd[:, :, 64 * g:64 * g + 64].rearrange("p v (b q) -> p v b q", q=S)
                ps = PS[:, O_BANK[g % 2], :].rearrange("p (v b h q) -> p v b h q", v=2, b=2, h=4)
                num, den = nd[:, 0, 64 * g:64 * g + 64], nd[:, 1, 64 * g:64 * g + 64]
                if n == 0:
                    dve.wait_ge(s["lo_ps"], 2 * g + 2)
                    V.tensor_scalar(o, ps[:, :, :, 0, :], hm[:, 0:1], None, ALU.mult).then_inc(s["sum_step"], 1)
                    return
                dve.wait_ge(s["sum_step"], 6 * g + n)
                if n < 4:
                    V.scalar_tensor_tensor(o, ps[:, :, :, n, :], hm[:, n:n + 1], o, ALU.mult, ALU.add)\
                        .then_inc(s["sum_step"], 1)
                elif n == 4:
                    V.reciprocal(den, den).then_inc(s["sum_step"], 1)
                else:
                    V.tensor_tensor(qTs[:, 64 * g:64 * g + 64], num, den, ALU.mult).then_inc(s["sum_step"], 1)

            def sum_denominators(g):
                dve.wait_ge(s["lo_ps"], 2 * g + 2)
                V.tensor_reduce(s1(M_NAN + g), PS[:, O_BANK[g % 2], 256:512], AX, ALU.add).then_inc(s["den_sum"], 1)

            for b in range(B + 2):
                for r in range(R):
                    if b < B:
                        i = R * b + r
                        dve.wait_ge(s["ls_ps"], i + 1)
                        with dve.If(in_bounds == 0):
                            clip(i)
                        V.tensor_reduce(s1(M_MX + i % 8), PS[:, S_BANK[i % 3], :], AX, ALU.max, negate=True)\
                            .then_inc(s["ls_max"], 1)
                    if 0 <= R * b + r - LAG_T < R * B:
                        with dve.If(in_bounds == 0):
                            clip_transposed(R * b + r - LAG_T)
                    if 1 <= b <= B and r == 0:
                        dve.wait_ge(s["ls_max"], R * b)
                        split_maximum(b - 1, 0)
                    if b % 2 and b >= 5 and r >= 1:
                        sum_heads((b - 5) // 2, r - 1)
                        if r == 1:
                            sum_denominators((b - 5) // 2)
                    elif b % 2 == 0 and b >= 6 and r < 3:
                        sum_heads((b - 6) // 2, 3 + r)
                    if 1 <= b <= B and r == 0:
                        for n in range(1, 4):
                            dve.wait_ge(s["split"], 3 * b - 3 + n)
                            split_maximum(b - 1, n)
            for n in (3, 4, 5):
                sum_heads(B // 2 - 2, n)
            g = B // 2 - 1
            sum_denominators(g)
            sum_heads(g, 0)
            dve.wait_ge(s["den_sum"], B // 2)
            V.tensor_tensor(s1(M_NAN, B // 2), s1(M_NAN, B // 2), s1(M_NAN, B // 2), ALU.not_equal)                .then_inc(s["nan_marks"], 1)
            sum_heads(g, 1)
            dve.wait_ge(s["nan_marks"], 1)
            V.tensor_reduce(s1(M_V), s1(M_NAN, 128), AX, ALU.max).then_inc(s["nan_max"], 1)
            sum_heads(g, 2)
            dve.wait_ge(s["nan_max"], 1)
            V.tensor_scalar(diag[:, :], ident, s1(M_V), None, ALU.mult).then_inc(s["gm_diag"], 1)
            sum_heads(g, 3)
            sum_heads(g, 4)
            dve.wait_ge(s["gm_ps"], n_gmax[0] + 1)
            V.tensor_reduce(s1(M_V + 1), PS[:, 7, 0:128], AX, ALU.max).then_inc(s["nan_max"], 1)
            sum_heads(g, 5)
            dve.wait_ge(s["nan_max"], 2)
            link(V.tensor_scalar(flags[:, 1:2], s1(M_V + 1), 0.0, None, ALU.is_gt))
            dve.wait_ge(s["sum_step"], 6 * B // 2)
            for t in range(T):
                V.copy_predicated(qTs[:, tile(t)].rearrange("p (b q) -> p b q", q=S),
                                  flags[:, 1:2].unsqueeze(2).broadcast_to([128, 4, S]),
                                  meanv[:, 4 * t:4 * t + 4].unsqueeze(2).broadcast_to([128, 4, S]))\
                    .then_inc(s["nan_ok"], 1)

            layer_norm(4, xn, s["ln_out"], (s["wo_ps"], 1))
            dve.wait_ge(s["ln_out"], 4 * T)
            add_bias(R_BM)
            self_attention(1)

            layer_norm(5, xn, s["ln_out"], (s["wo_ps"], 2))
            dve.wait_ge(s["ln_out"], 5 * T)
            add_bias(R_FB)
            for t in range(T):
                dve.wait_ge(s["fin_ps"], t + 1)
                V.tensor_tensor(x[:, t, :], x[:, t, :], PS[:, t, 0:128], ALU.add).then_inc(s["x_done"], 1)

        @block.tensor
        def _(pe):
            def mm(o, lhsT, rhs, start=True, stop=True, **kw):
                return nc.tensor.matmul(o, lhsT, rhs, start=start, stop=stop, **kw)

            n_gmax = [0]

            def spread_max():
                n_gmax[0] += 1
                pe.wait_ge(s["gm_diag"], n_gmax[0])
                mm(PS[:, 7, 0:128], ones[:, :], diag[:, :]).then_inc(s["gm_ps"], 1)

            def transpose_rows(bank, src, idm, f=None):
                for t in range(T):
                    o = PS[:, bank, tile(t)] if f is None else PS[:, bank, 0:256].bitcast(bf16)[:, tile(t)]
                    last = nc.tensor.transpose(o, src[:, t, :], idm)
                return last

            pe.wait_ge(s["consts"], 1)
            spread_max()
            pe.wait_ge(s["wabs"], 1)
            mm(PS[:, 6, 0:7], ones[:, :], s1(M_ABS, 7)).then_inc(s["ws_ps"], 1)
            def quantised(layer, c):
                if c % 2 == 0:
                    pe.wait_ge(s["quant_dve"], 8 * layer + c // 2 + 1)
                elif c % 4 == 1:
                    pe.wait_ge(s["quant_pool"], 4 * layer + c // 4 + 1)
                else:
                    pe.wait_ge(s["quant_act"], 4 * layer + c // 4 + 1)

            cosm, sinm = cst[:, C_DC:C_DC + 128], cst[:, C_DS:C_DS + 128]
            cosn, nsinn = cst[:, C_DCN:C_DCN + 128], cst[:, C_DSN:C_DSN + 128]
            att = tern[:, 384:512]
            noff4 = noff[:, :].unsqueeze(1).broadcast_to([128, 4, 128])
            for layer in range(3):
                w = (TW("d2v")[0:DC, :], TW("img"), att)[layer]
                pn = DC if layer == 0 else 128
                if layer == 1:
                    pe.wait_ge(s["ld_wa"], 16)
                    mm(PS[:, 4, 0:128], A("wr"), cosm, stop=False)
                    mm(PS[:, 4, 0:128], A("wi"), sinm, start=False)
                    mm(PS[:, 4, 128:256], A("wi"), cosn, stop=False)
                    mm(PS[:, 4, 128:256], A("wr"), nsinn, start=False).then_inc(s["ft_ps"], 1)
                    pe.wait_ge(s["casts"], 1)
                    pe.wait_ge(s["txt_q"], 1)
                    transpose_rows(6, qb, identb[:, :], 1).then_inc(s["txt_tp"], 1)
                spread_max()
                if layer == 1:
                    pe.wait_ge(s["txt_qT"], 1)
                    for t in range(T):
                        last = mm(PS[:, 5, tile(t)], qT[:, tile(t)], TW("txt"))
                    last.then_inc(s["txt_ps"], 1)
                    mm(PS[:, 4, 256:384], noff[:, :], att).then_inc(s["kv_off_ps"], 1)
                    pe.wait_ge(s["bound_in"], 1)
                    pe.wait_ge(s["ctx_sums"], 1)
                    mm(PS[:, 6, 0:128], ones[:, :], mix[:, 0:128])
                    mm(PS[:, 6, 128:256], ones[:, :], mix[:, 128:256])
                    mm(PS[:, 6, 256:256 + B], A("wv", DC + 1), csum[0:DC + 1, :]).then_inc(s["bound_ps"], 1)
                if layer == 2:
                    pe.wait_ge(s["ft_ok"], 1)
                    mm(PS[:, 6, 384:512], ft[:, 0, :], cosn, stop=False)
                    mm(PS[:, 6, 384:512], ft[:, 1, :], sinm, start=False).then_inc(s["lin_ps"], 1)
                pe.wait_ge(s["ternary"], 5 if layer else 1)
                for c in range(NCH):
                    quantised(layer, c)
                    if NCH * layer + c >= 4:
                        pe.wait_ge(s["ctx_ev"], NCH * layer + c - 3)
                    mm(PS[:, c % 4, :], w, y16[0:pn, chunk(c)], stop=False)
                    mm(PS[:, c % 4, :], w, noff4[0:pn], start=False).then_inc(s["ctx_mm"], 1)
                    if layer == 2:
                        if c >= 2:
                            pe.wait_ge(s["kv_ev"], c - 1)
                        for k in range(4):
                            last = mm(PS[:, 4 + c % 2, tile(k)], y16[:, 512 * c + 128 * k:512 * c + 128 * k + 128], att)
                        last.then_inc(s["kv_mm"], 1)

            wk, wv = A("wk", DC + 1), A("wv", DC + 1)

            def keys(c, bank):
                mm(PS[:, bank, :], wk, cx[0:DC + 1, chunk(c)]).then_inc(s["kp_ps"], 1)

            for j in range(2):
                pe.wait_ge(s["fk_tok"], j + 1)
                transpose_rows(7, tmp, ident).then_inc(s["fk_tp"], 1)
                pe.wait_ge(s["fkT"], j + 1)
                pe.wait_ge(s["ctx_ev"], 3 * NCH)
                pe.wait_ge(s["kv_ev"], NCH)
                for t in range(T):
                    if j:
                        pe.wait_ge(s["kp_l"], t + 1)
                    for b in range(4):
                        c = 128 * t + 32 * b
                        last = mm(PS[32 * b:32 * b + 32, t, :], xT[:, c:c + 32], big[:, 0, chunk(4 * t + b)])
                    last.then_inc(s["sc_ps"], 1)

                def transposed(t):
                    pe.wait_ge(s["sc_exp"], T * j + t + 1)
                    if t >= 2:
                        if t % 2:
                            pe.wait_ge(s["sc_teva"], 2 * j + 1)
                        else:
                            pe.wait_ge(s["sc_tev"], 2 * j + 1)
                    for k in range(4):
                        last = nc.tensor.transpose(PS[:, 4 + t % 2, tile(k)], work[:, t, tile(k)], ident)
                    last.then_inc(s["sc_tp"], 1)

                def mixed(t):
                    if t % 2:
                        pe.wait_ge(s["sc_teva"], 2 * j + t // 2 + 1)
                    else:
                        pe.wait_ge(s["sc_tev"], 2 * j + t // 2 + 1)
                    for k in range(4):
                        for b in range(4):
                            c = 512 * (4 * t + b) + 128 * k + 64 * j
                            last = mm(PS[32 * b:32 * b + 32, MIX_BANK[t], 0:128],
                                      wt[:, t, 128 * k + 32 * b:128 * k + 32 * b + 32],
                                      big[:, 1, c:c + 64].unsqueeze(1).broadcast_to([128, 2, 64]),
                                      start=(k == 0), stop=(k == 3))
                    last.then_inc(s["pv_ps"], 1)

                transposed(0)
                transposed(1)
                keys(4 * j, 0)
                mixed(0)
                transposed(2)
                mixed(1)
                transposed(3)
                mixed(2)
                mixed(3)
                keys(4 * j + 1, 1)
                for n, (c, bank) in enumerate(KEYS_AFTER_ROUND[j]):
                    if j and n == 1:
                        spread_max()
                    if n >= 2:
                        pe.wait_ge(s["pv_read"], T * j + n + 1)
                    keys(c, bank)

            pe.wait_ge(s["f1_in"], 1)
            transpose_rows(6, qb, identb[:, :], 1).then_inc(s["f1_tp"], 1)
            pe.wait_ge(s["f1_qT"], 1)
            pe.wait_ge(s["ternary"], 7)
            avg_rows = avgb[:, :].unsqueeze(2).broadcast_to([128, B, S])
            for fc in range(FC):
                pe.wait_ge(s["kp_l"], 6 if fc < 2 else 5 + fc)
                mm(PS[:, fc, :], TW("f1")[:, 128 * fc:128 * fc + 128], qT[:, :], stop=False)
                mm(PS[:, fc, :], TW("f1")[:, FF + 128 * fc:FF + 128 * fc + 128], avg_rows, start=False)\
                    .then_inc(s["f1_ps"], 1)
            pe.wait_ge(s["kp_l"], 9)
            for c, bank in KEYS_IN_FF[:2]:
                keys(c, bank)
            spread_max()
            for n, (c, bank) in enumerate(KEYS_IN_FF[2:]):
                pe.wait_ge(s["f1_ev"], n + 1)
                keys(c, bank)
            pe.wait_ge(s["f2_qd"], 2)
            pe.wait_ge(s["f2_qa"], 2)
            wt16 = w1[:, FF + 2048:FF + 4096].bitcast(f16).rearrange("p (r n two) -> p r n two", r=4, two=2)[:, :, :, 0]
            for t in range(T):
                for fc in range(FC):
                    w = TW("f2")[:, tile(fc)]
                    mm(PS[:, 5, tile(t)], wt16[:, fc, tile(t)], w, start=(fc == 0), stop=False)
                    last = mm(PS[:, 5, tile(t)], noff[:, :], w, start=False, stop=(fc == FC - 1))
            last.then_inc(s["f2_ps"], 1)

            def context_values(part, step=None):
                for n, (c, bank) in enumerate(VALUES[part] if step is None else VALUES[part][step:step + 1]):
                    n += step or 0
                    if part == 0 and c < 4:
                        pe.wait_ge(s["kp_l"], 13 + c)
                    elif n >= (4, 3, 2)[part]:
                        pe.wait_ge(s["vp_ev"], c - (3, 2, 1)[part])
                    for k in range(4):
                        a = 512 * c + 128 * k
                        last = mm(PS[:, bank, tile(k)], cx[0:DC + 1, a:a + 128], wv)
                    last.then_inc(s["vp_ps"], 1)

            context_values(0)
            def rows_to_features(n, src):
                for t in range(T):
                    pe.wait_ge(s["ln_out"], T * (n - 1) + t + 1)
                    last = nc.tensor.transpose(PS[:, 7, tile(t)], src[:, t, :], ident)
                last.then_inc(s["xt_ps"], 1)

            def self_attention(k):
                q, kk, v, o = ("q1", "k1", "v1", "m1") if k else ("q0", "k0", "v0", "o0")
                pe.wait_ge(s["xt_ev"], (1, 4)[k])
                mm(PS[:, 4, :], A(q), xT[:, :]).then_inc(s["qk_ps"], 1)
                mm(PS[:, 5, :], A(kk), xT[:, :]).then_inc(s["qk_ps"], 1)

                def values(half):
                    for b in range(8 * (1 - half), 8 * (2 - half)):
                        last = mm(PS[:, 4 + b // 4, tile(b % 4)],
                                  xrep[:, tile(b)], A(v))
                    last.then_inc(s["v_ps"], 1)

                pe.wait_ge(s["xrep_ok"], k + 1)
                values(0)
                if k == 0:
                    pe.wait_ge(s["vp_ev"], len(VALUES[0]))
                for r in range(R):
                    mm(PS[:, r, :], identb[:, :], maskb[:, k, :].unsqueeze(1).broadcast_to([128, 4, 128]), stop=False,
                       skip_group_check=True)
                pe.wait_ge(s["q_ev"], k + 1)
                pe.wait_ge(s["k_evd"], 2 * k + 2)
                pe.wait_ge(s["k_eva"], k + 1)
                pe.wait_ge(s["k_evp"], k + 1)
                for r in range(R):
                    for b in range(B):
                        t, b4 = b // 4, b % 4
                        last = mm(PS[32 * b4:32 * b4 + 32, r, tile(t)], qTs[32 * r:32 * r + 32, 32 * b:32 * b + 32],
                                  kexp[32 * r:32 * r + 32, :, 32 * b:32 * b + 32], start=False, stop=(b >= 12),
                                  skip_group_check=True)
                    last.then_inc(s["sa_ps"], 1)
                values(1)
                for r in range(R):
                    pe.wait_ge(s["sa_exp"], R * k + r + 1)
                    for t in range(T):
                        last = nc.tensor.transpose(PS[:, r, tile(t)], work[:, r, tile(t)], ident)
                    last.then_inc(s["sa_tp"], 1)
                pe.wait_ge(s["vones"], k + 1)
                for half in range(2):
                    pe.wait_ge(s["v_ev"], 8 * k + 4 * half + 4)
                    for r in range(R):
                        if r % 2:
                            pe.wait_ge(s["sa_teva"], 2 * k + r // 2 + 1)
                        else:
                            pe.wait_ge(s["sa_tevd"], 2 * k + r // 2 + 1)
                        for b in range(8 * (1 - half), 8 * (2 - half)):
                            t, b4 = b // 4, b % 4
                            c = 144 * (t % 2) + 36 * r
                            last = mm(PS[32 * b4:32 * b4 + 32, P_BANK[t // 2], c:c + 36], wt[:, r, 32 * b:32 * b + 32],
                                      vexp[:, b, r, :])
                last.then_inc(s["sa_pv"], 1)
                pe.wait_ge(s["sa_o"], k + 1)
                transpose_rows(6, tmp, ident).then_inc(s["ot_ps"], 1)
                pe.wait_ge(s["ot_ev"], k + 1)
                for t in range(T):
                    mm(PS[:, t, 0:128], xT[:, tile(t)], A(o)).then_inc(s["wo_ps"], 1)

            rows_to_features(1, fused)
            self_attention(0)
            context_values(1)

            rows_to_features(2, xn)
            pe.wait_ge(s["xt_ev"], 2)
            mm(PS[:, 0, :], A("gate1"), xT[:, :]).then_inc(s["g_ps"], 1)

            def hidden(fc, e):
                return mm(PS[:, 2 + fc, :], w1[:, FF * e + 128 * fc:FF * e + 128 * fc + 128],
                          zz[:, e - 1, :] if e else xT[:, :], start=(e == 0), stop=(e == E))

            pe.wait_ge(s["ld_w1"], 16)
            pe.wait_ge(s["vp_ev"], len(VALUES[0]) + len(VALUES[1]))
            hidden(0, 0)
            hidden(1, 0)
            pe.wait_ge(s["g_x"], 1)
            mm(PS[:, 1, 0:128], ones[:, :], mix[:, 0:128]).then_inc(s["g_bc_ps"], 1)
            hidden(2, 0)
            hidden(3, 0)
            for fc in range(FC):
                for e in range(1, E1):
                    if fc == 0:
                        pe.wait_ge(s["z_ready"], e)
                        pe.wait_ge(ld_ws[e - 1], 16)
                    last = hidden(fc, e)
                last.then_inc(s["u_ps"], 1)
            pe.wait_ge(s["ld_w2"], 16)
            for t in range(T):
                if t >= 2:
                    pe.wait_ge(s["y_used"], t - 1)
                for g in range(3):
                    for fc in range(FC):
                        if t == 0 and g == 0:
                            pe.wait_ge(s["u_act"], fc + 1)
                        last = mm(PS[:, Y_BANK[t % 2][g], 0:384], u[:, fc, tile(t)], w2[:, fc, 3 * g:3 * g + 3, :],
                                  start=(fc == 0), stop=(fc == FC - 1))
                    last.then_inc(s["y_ps"], 1)

            rows_to_features(3, xn)
            pe.wait_ge(s["xt_ev"], 3)
            for r in range(R):
                mm(PS[:, r, :], wa[:, A_WQR + 128 * r:A_WQR + 128 * r + 128], xT[:, :]).then_inc(s["lq_ps"], 1)
            pe.wait_ge(s["flag_ok"], 1)
            in_bounds = pe.value_load(flags[0:1, 0:1], min_val=0, max_val=1)

            def scores(i):
                b, r = i // R, i % R
                if i >= 3:
                    pe.wait_ge(s["ls_max"], i - 2)
                if b == 0:
                    pe.wait_ge(s["lq_ev"], r + 1)
                    pe.wait_ge(s["lq_e"], 2 * r + 2)
                    pe.wait_ge(s["lq_e2"], r + 1)
                    pe.wait_ge(s["lq_e3"], r + 1)
                mm(PS[:, S_BANK[i % 3], :], qe[0:96, r, b, :], kst[0:96, r, chunk(b)]).then_inc(s["ls_ps"], 1)

            def maxima_rows(b):
                pe.wait_ge(s["ls_parts"], b + 1)
                if b >= 1:
                    pe.wait_ge(s["ls_rows"], b)
                for r in range(R):
                    last = mm(PS[96:99, M_BANK, tile(r)], mparts[:, b % 2, r, :], identh[:, :])
                last.then_inc(s["ls_rows_ps"], 1)

            def transposed_scores(i):
                b, r = i // R, i % R
                pe.wait_ge(s["ls_rows"], b + 1)
                if i >= 2:
                    pe.wait_ge(s["lt_exp"], i - 1)

                def products(p0, p1, start):
                    for k in range(4):
                        last = mm(PS[:, ST_BANK[i % 2], tile(k)], kst[p0:p1, r, 512 * b + 128 * k:512 * b + 128 * k + 128],
                                  qe[p0:p1, r, b, :], start=start and k == 0, skip_group_check=True)
                    return last

                with pe.If(in_bounds == 0):
                    products(0, 96, True).then_inc(s["lt_raw"], 1)
                    pe.wait_ge(s["lt_clipped"], i + 1)
                    products(96, 99, False).then_inc(s["lt_ps"], 1)
                with pe.If(in_bounds != 0):
                    products(0, 99, True).then_inc(s["lt_ps"], 1)

            def outputs(b, k):
                if b % 2 == 0 and b >= 4 and k == 0:
                    pe.wait_ge(s["sum_step"], 6 * (b // 2 - 2) + 4)
                    pe.wait_ge(s["den_sum"], b // 2 - 1)
                if b == 0 and k == 0:
                    pe.wait_ge(s["vp_ev"], NCH)
                if k == 0:
                    pe.wait_ge(s["lt_exp"], R * b + R)
                bank = O_BANK[(b // 2) % 2]
                first = b % 2 == 0 and k == 0
                for r in range(R):
                    v0 = 512 * b + 128 * k + 32 * r
                    mm(PS[32 * r:32 * r + 32, bank, tile(b % 2)], cx[:, v0:v0 + 32],
                       pt(R * b + r)[:, tile(k)], start=first, stop=False, skip_group_check=True)
                for r in range(R):
                    last = mm(PS[32 * r:32 * r + 32, bank, tile(2 + b % 2)], ones[:, 0:32],
                              pt(R * b + r)[:, tile(k)], start=False, stop=(b % 2 == 1 and k == 3),
                              skip_group_check=True)
                if k == 3:
                    last.then_inc(s["lo_ps"], 1)

            pe.wait_ge(s["kst_done"], 3 * R * 16)
            pe.wait_ge(s["key_ones"], 1)
            for n in range(R * B + LAG_O):
                b, r = n // R, n % R
                if n < R * B:
                    scores(n)
                if 0 <= n - LAG_T < R * B:
                    transposed_scores(n - LAG_T)
                if (b, r) in VALUE_STEPS:
                    context_values(2, VALUE_STEPS.index((b, r)))
                if n >= LAG_O:
                    outputs((n - LAG_O) // 4, (n - LAG_O) % 4)
                if r == ROWS_AT and 1 <= b <= B:
                    maxima_rows(b - 1)
            spread_max()
            for t in range(T):
                pe.wait_ge(s["nan_ok"], t + 1)
                mm(PS[:, t, 0:128], qTs[:, tile(t)], A("wo")).then_inc(s["wo_ps"], 1)

            rows_to_features(4, xn)
            self_attention(1)
            rows_to_features(5, xn)
            pe.wait_ge(s["xt_ev"], 5)
            for t in range(T):
                mm(PS[:, t, 0:128], xT[:, tile(t)], lin[:, :]).then_inc(s["fin_ps"], 1)


def _constants():
    c = np.zeros((128, C_END), np.float32)
    p = np.arange(128)
    c[:, C_ID:C_ID + 128] = np.eye(128)
    theta = (1.0 / 10000.0 ** (np.arange(64, dtype=np.float32) / 64)).astype(np.float32)
    ang = (p % S).astype(np.float32)[:, None] * theta[None, :]
    c[:, C_COS:C_COS + 64] = np.cos(ang)
    c[:, C_SIN:C_SIN + 64] = np.sin(ang)
    c[:, C_HM:C_HM + 4] = ((p // HD) % 4)[:, None] == np.arange(4)[None, :]
    c[:, C_RM:C_RM + 4] = (p // 32)[:, None] == np.arange(4)[None, :]
    later = (p % S)[None, :] > (p % S)[:, None]
    c[:, C_MK0:C_MK0 + 128] = later * -1e9
    c[:, C_MK1:C_MK1 + 128] = later * -1e12
    a = 2 * np.pi * ((p[:, None] * p[None, :]) % D) / D
    c[:, C_DC:C_DC + 128], c[:, C_DS:C_DS + 128] = np.cos(a), np.sin(a)
    c[:, C_DCN:C_DCN + 128], c[:, C_DSN:C_DSN + 128] = np.cos(a) / D, -np.sin(a) / D
    c[:, C_CNT:C_CNT + 7] = 1.0 / np.array(X_COUNT)
    return c


def _pad(a, rows=128):
    z = np.zeros((rows, a.shape[1]), np.float32)
    z[:a.shape[0]] = a
    return z


def kernel(**inputs):
    import concourse.bacc as _bacc
    from concourse import mybir as _mybir
    from concourse.bass_utils import run_bass_kernel_spmd as _run

    v = {k: np.asarray(a) for k, a in inputs.items()}
    X, SA0, F0 = "L0_xattn_", "L0_attn_", "L0_ffn_"
    X1, SA1, F1 = "L1_xattn_", "L1_attn_", "L1_ffn_"

    def rep_heads(w):
        return np.repeat(w.reshape(R, 1, HD, D), 4, axis=1).reshape(D, D).T

    wx = np.concatenate([_pad(v[X + "W_d2v"].T), v[X + "W_img"].T, v[X + "W_txt"].T, v[X + "W_att0"].T,
                         v[X + "W_att1"].T, v[X + "W_f1"].T[:128], v[X + "W_f1"].T[128:]]
                        + [v[X + "W_f2"].T[128 * c:128 * c + 128] for c in range(FC)], axis=1)
    wqr = np.tile(v[X1 + "Wq"].reshape(D, R, 1, 32), (1, 1, 4, 1)).reshape(D, 512)
    wa = np.concatenate(
        [v[SA0 + "W_q"].T, rep_heads(v[SA0 + "W_k"]), rep_heads(v[SA0 + "W_v"]), v[SA0 + "W_o"].T,
         v[F0 + "gate_w1"].T, v[X1 + "Wo"], v[SA1 + "Wq"], v[SA1 + "Wk"], v[SA1 + "Wv"], v[SA1 + "Wm"],
         v[F1 + "w_freq_real"], v[F1 + "w_freq_imag"],
         _pad(np.concatenate([v[X1 + "Wk"], v[X1 + "bk"][None]])), _pad(np.concatenate([v[X1 + "Wv"], v[X1 + "bv"][None]])),
         wqr, v[F0 + "gate_w2"].T], axis=1)
    w1 = np.concatenate([v[F0 + "W1"][None], v[F0 + "TW1"]]).transpose(2, 0, 1).reshape(D, E1 * FF)
    w2 = np.concatenate([v[F0 + "W2"][None], v[F0 + "TW2"]])
    w2 = w2.reshape(E1, D, FC, 128).transpose(3, 2, 0, 1).reshape(128, FC * E1 * D)
    tb1 = v[F0 + "Tb1"].reshape(E, FC, 128).transpose(2, 1, 0).reshape(128, FC * E)
    c1 = lambda a: a.reshape(-1, 128).T
    cols = np.concatenate([c1(v[X + "b_d2v"]), c1(v[X + "b_img"]),
                           c1(np.concatenate([v[X + "b_att0"], v[X + "b_att1"]])), c1(v[X + "b_f1"]),
                           c1(v[F0 + "gate_b1"]), np.zeros((128, 3), np.float32),
                           c1(np.tile(v[X1 + "bq"].reshape(R, 1, 32), (1, 4, 1)).reshape(512)),
                           c1(v[SA1 + "bq"]), c1(v[SA1 + "bk"]), c1(v[SA1 + "bv"]), c1(v[F0 + "b1"]), tb1], axis=1)
    assert cols.shape[1] == K_END
    a0, a1 = v[X + "b_att0"], v[X + "b_att1"]
    row = np.concatenate([v[X + "b_txt"], a0, a0, a1, a1, v[X + "b_f2"], v[X1 + "bo"], v[SA1 + "bm"], v[F1 + "bias"],
                          v[F0 + "b2"], v[F0 + "gate_b2"], v[X1 + "bq"], v[F0 + "Tb2"].reshape(-1)])
    assert row.shape[0] == R_END + E * D
    arrays = {
        "x_in": v["x"].reshape(N, D), "ctx_in": np.concatenate([v["ctx_768"].reshape(CP, DC).T, np.ones((1, CP), np.float32)]), "wx_in": wx, "wa_in": wa,
        "w1_in": w1, "w2_in": w2, "const_in": _constants(), "cols_in": cols, "rows_in": np.tile(row[None], (128, 1)),
    }
    arrays = {k: np.ascontiguousarray(a) for k, a in arrays.items()}
    nc = _bacc.Bacc("TRN2", target_bir_lowering=False, num_devices=1)
    args = [nc.dram_tensor(k, a.shape, _mybir.dt.float32, kind="ExternalInput").ap() for k, a in arrays.items()]
    args.append(nc.dram_tensor("out", (N, D), _mybir.dt.float32, kind="ExternalOutput").ap())
    perceiver(nc, *args)
    return _run(nc, [arrays], core_ids=[0]).results[0]["out"].reshape(B, S, D)
```
